# Optimizing a Trainium2 kernel written in Bass

```python
import numpy as np
import jax
import jax.numpy as jnp

def _softmax(x, axis=-1):
    return jax.nn.softmax(x, axis=axis)

def _gelu(x):
    return jax.nn.gelu(x, approximate=True)

def _silu(x):
    return jax.nn.silu(x)

def _sigmoid(x):
    return jax.nn.sigmoid(x)

def _layernorm(x, axis=-1, eps=1e-05):
    m = jnp.mean(x, axis=axis, keepdims=True)
    v = jnp.var(x, axis=axis, keepdims=True)
    return (x - m) / jnp.sqrt(v + eps)

def _scatter_add(tgt, idx, src, axis=0):
    return tgt.at[idx].add(src)

def _segment_sum(src, seg, n):
    return jax.ops.segment_sum(src, seg, n)
kernel_name = 'mk_gnn_ffn_d1_gnn_r32_3e41f7'

def setup_inputs(seed: int=0):
    np.random.seed(seed)
    _w = jnp.asarray

    def _rec_inputs():
        import jax
        import jax.numpy as jnp
        _gk = jax.random.key(seed)
        x = -0.0006008 + 1.001 * jax.random.normal(jax.random.fold_in(_gk, 1), (50000, 256), jnp.float32)
        src = jax.random.randint(jax.random.fold_in(_gk, 2), (50000,), 0, 50000, jnp.int32)
        dst = jax.random.randint(jax.random.fold_in(_gk, 3), (50000,), 0, 50000, jnp.int32)
        _o = jnp.argsort(dst, stable=True)
        src = src[_o]
        dst = dst[_o]
        return (x, src, dst)
    x, src, dst = _rec_inputs()

    def _L0_gnn_setup():
        import jax, jax.numpy as jnp
        import numpy as np
        N = 10000
        E = 9375
        D = 256
        key = jax.random.key(seed)
        k1, k2, k3, k4 = jax.random.split(key, 4)
        x = jax.random.normal(k1, (N, D), dtype=jnp.float32)
        edge_index = jax.random.randint(k2, (2, E), 0, N, dtype=jnp.int32)
        s = 1.0 / np.sqrt(D)
        W1 = jax.random.uniform(k3, (D, D), jnp.float32, -s, s)
        b1 = jnp.zeros((D,), jnp.float32)
        W2 = jax.random.uniform(k4, (D, D), jnp.float32, -s, s)
        b2 = jnp.zeros((D,), jnp.float32)
        return {'x': x, 'W1': W1, 'b1': b1, 'W2': W2, 'b2': b2, 'edge_index': edge_index}
    _L0_gnn_all = _L0_gnn_setup()
    _L0_gnn_in = {k: v for k, v in _L0_gnn_all.items() if k in ('W1', 'b1', 'W2', 'b2')}
    del _L0_gnn_all

    def _L0_ffn_setup():
        import jax, jax.numpy as jnp
        import numpy as np
        DIM = 256
        H = 8
        D = 64
        G = 64
        INNER = H * D
        SCALE = D ** (-0.5)
        key = jax.random.key(seed)
        ks = jax.random.split(key, 12)
        B, N = (4, 512)
        x = jax.random.normal(ks[0], (B, N, DIM), dtype=jnp.float32)
        s = lambda fan_in: 1.0 / np.sqrt(fan_in)
        W_fx = jax.random.normal(ks[1], (DIM, INNER), dtype=jnp.float32) * s(DIM)
        b_fx = jnp.zeros((INNER,), dtype=jnp.float32)
        W_x = jax.random.normal(ks[2], (DIM, INNER), dtype=jnp.float32) * s(DIM)
        b_x = jnp.zeros((INNER,), dtype=jnp.float32)
        A = jax.random.normal(ks[3], (G, D), dtype=jnp.float32)
        Q, _ = jnp.linalg.qr(A.T)
        W_slice = Q[:, :G].astype(jnp.float32)
        b_slice = jnp.zeros((G,), dtype=jnp.float32)
        W_q = jax.random.normal(ks[4], (D, D), dtype=jnp.float32) * s(D)
        W_k = jax.random.normal(ks[5], (D, D), dtype=jnp.float32) * s(D)
        W_v = jax.random.normal(ks[6], (D, D), dtype=jnp.float32) * s(D)
        W_out = jax.random.normal(ks[7], (INNER, DIM), dtype=jnp.float32) * s(INNER)
        b_out = jnp.zeros((DIM,), dtype=jnp.float32)
        temperature = jnp.ones((1, H, 1, 1), dtype=jnp.float32) * 0.5
        return {'x': x, 'W_fx': W_fx, 'b_fx': b_fx, 'W_x': W_x, 'b_x': b_x, 'W_slice': W_slice, 'b_slice': b_slice, 'W_q': W_q, 'W_k': W_k, 'W_v': W_v, 'W_out': W_out, 'b_out': b_out, 'temperature': temperature}
    _L0_ffn_all = _L0_ffn_setup()
    _L0_ffn_in = {k: v for k, v in _L0_ffn_all.items() if k in ('W_fx', 'b_fx', 'W_x', 'b_x', 'W_slice', 'b_slice', 'W_q', 'W_k', 'W_v', 'W_out', 'b_out', 'temperature')}
    del _L0_ffn_all
    return {'x': x, 'src': src, 'dst': dst, 'L0_gnn_W1': _L0_gnn_in['W1'], 'L0_gnn_b1': _L0_gnn_in['b1'], 'L0_gnn_W2': _L0_gnn_in['W2'], 'L0_gnn_b2': _L0_gnn_in['b2'], 'L0_ffn_W_fx': _L0_ffn_in['W_fx'], 'L0_ffn_b_fx': _L0_ffn_in['b_fx'], 'L0_ffn_W_x': _L0_ffn_in['W_x'], 'L0_ffn_b_x': _L0_ffn_in['b_x'], 'L0_ffn_W_slice': _L0_ffn_in['W_slice'], 'L0_ffn_b_slice': _L0_ffn_in['b_slice'], 'L0_ffn_W_q': _L0_ffn_in['W_q'], 'L0_ffn_W_k': _L0_ffn_in['W_k'], 'L0_ffn_W_v': _L0_ffn_in['W_v'], 'L0_ffn_W_out': _L0_ffn_in['W_out'], 'L0_ffn_b_out': _L0_ffn_in['b_out'], 'L0_ffn_temperature': _L0_ffn_in['temperature']}

def reference(x, src, dst, L0_gnn_W1, L0_gnn_b1, L0_gnn_W2, L0_gnn_b2, L0_ffn_W_fx, L0_ffn_b_fx, L0_ffn_W_x, L0_ffn_b_x, L0_ffn_W_slice, L0_ffn_b_slice, L0_ffn_W_q, L0_ffn_W_k, L0_ffn_W_v, L0_ffn_W_out, L0_ffn_b_out, L0_ffn_temperature):
    import jax
    import jax.numpy as jnp

    def _L0_gnn_ref(x, W1, b1, W2, b2, edge_index):
        import jax, jax.numpy as jnp
        import numpy as np
        N = 10000
        E = 9375
        D = 256
        n = x.shape[0]
        loops = jnp.arange(n, dtype=edge_index.dtype)
        src = jnp.concatenate([edge_index[0], loops])
        dst = jnp.concatenate([edge_index[1], loops])
        deg = jax.ops.segment_sum(jnp.ones(src.shape[0], x.dtype), dst, num_segments=n)
        dinv = jnp.where(deg > 0, jax.lax.rsqrt(jnp.maximum(deg, 1e-12)), 0.0)
        norm = dinv[src] * dinv[dst]

        def gcn_conv(h, W, b):
            m = (h @ W)[src] * norm[:, None]
            return jax.ops.segment_sum(m, dst, num_segments=n) + b
        x1 = gcn_conv(x, W1, b1)
        x1 = x1 / jnp.maximum(jnp.linalg.norm(x1, axis=-1, keepdims=True), 1e-12)
        x2 = gcn_conv(x1, W2, b2)
        return x2 + x

    def _L0_ffn_ref(x, W_fx, b_fx, W_x, b_x, W_slice, b_slice, W_q, W_k, W_v, W_out, b_out, temperature):
        import jax, jax.numpy as jnp
        import numpy as np
        DIM = 256
        H = 8
        D = 64
        G = 64
        INNER = H * D
        SCALE = D ** (-0.5)
        B, N, _ = x.shape
        fx_mid = (x @ W_fx + b_fx).reshape(B, N, H, D).transpose(0, 2, 1, 3)
        x_mid = (x @ W_x + b_x).reshape(B, N, H, D).transpose(0, 2, 1, 3)
        temp = jnp.clip(temperature, 0.1, 5.0)
        slice_weights = jax.nn.softmax((x_mid @ W_slice + b_slice) / temp, axis=-1)
        slice_norm = slice_weights.sum(axis=2)
        slice_token = jnp.einsum('bhnc,bhng->bhgc', fx_mid, slice_weights)
        slice_token = slice_token / (slice_norm[..., None] + 1e-05)
        q = slice_token @ W_q
        k = slice_token @ W_k
        v = slice_token @ W_v
        attn = jax.nn.softmax(jnp.einsum('bhgc,bhkc->bhgk', q, k) * SCALE, axis=-1)
        out_slice = jnp.einsum('bhgk,bhkc->bhgc', attn, v)
        out_x = jnp.einsum('bhgc,bhng->bhnc', out_slice, slice_weights)
        out_x = out_x.transpose(0, 2, 1, 3).reshape(B, N, INNER)
        return out_x @ W_out + b_out
    edge_index = jnp.stack([src, dst])
    x = x + _L0_gnn_ref(_layernorm(x, axis=-1), L0_gnn_W1, L0_gnn_b1, L0_gnn_W2, L0_gnn_b2, edge_index)
    x = x + _L0_ffn_ref(_layernorm(x, axis=-1)[None], L0_ffn_W_fx, L0_ffn_b_fx, L0_ffn_W_x, L0_ffn_b_x, L0_ffn_W_slice, L0_ffn_b_slice, L0_ffn_W_q, L0_ffn_W_k, L0_ffn_W_v, L0_ffn_W_out, L0_ffn_b_out, L0_ffn_temperature)[0]
    return x

_drawn_inputs = setup_inputs


def setup_inputs(seed=0):
    import zlib

    import numpy as np

    out = dict(_drawn_inputs(seed))
    spreads = {'L0_gnn_b1': (0.0, 0.8),
     'L0_gnn_b2': (0.0, 0.1),
     'L0_ffn_b_fx': (0.0, 0.1),
     'L0_ffn_b_x': (0.0, 0.8),
     'L0_ffn_b_slice': (0.0, 0.8),
     'L0_ffn_b_out': (0.0, 0.1),
     'L0_ffn_temperature': (0.5, 0.6)}
    factors = {'L0_gnn_W1': 3.352,
     'L0_gnn_W2': 3.231,
     'L0_ffn_W_x': 8.0,
     'L0_ffn_W_slice': 8.0,
     'L0_ffn_W_q': 8.0,
     'L0_ffn_W_k': 8.0}
    for name, (base, spread) in spreads.items():
        noise = np.random.default_rng([zlib.crc32(name.encode()), seed]).standard_normal(out[name].shape)
        drawn = base * np.exp(spread * noise) if base else spread * noise
        out[name] = jnp.asarray(drawn.astype(out[name].dtype))
    for name, factor in factors.items():
        out[name] = (out[name] * factor).astype(out[name].dtype)
    return out
```

```python
from contextlib import ExitStack

import concourse.bass as bass
from concourse import mybir

F32 = mybir.dt.float32
BF16 = mybir.dt.bfloat16
I32 = mybir.dt.int32
ACT = mybir.ActivationFunctionType
ALU = mybir.AluOpType
AX = mybir.AxisListType

P = 128
D = 256
KD = D // P
SLOTS = 4
GROUP = P * SLOTS
HEADS = 8
HD = 64
SL = 64
HS = HEADS * SL
CH = HS // P
LN_EPS = 1e-5
TOKEN_EPS = 1e-5
BODY_GROUPS = 2


class Model:
    pass


def padded(n):
    step = GROUP * BODY_GROUPS
    return (n + step - 1) // step * step


def wait(engine, semaphore, value):
    if isinstance(value, int) and value <= 0:
        return
    engine.wait_ge(semaphore, value)


def carry(engine, passed):
    engine.sem_inc(passed, 1)


def loop(engine, count, body):
    body(0)
    if count > 2:
        with engine.Fori(1, count - 1) as it:
            body(it)
    body(count - 1)


def grouped(dram, width):
    return dram[0:dram.shape[0] // GROUP * GROUP, :].rearrange(
        "(g p j) d -> g p (j d)", p=P, j=SLOTS)


def one_group(view, g, width):
    return view[bass.ds(g, 1), :, :].rearrange("g p (j d) -> p (g j) d", d=width)


def count_degrees(nc, m):
    nt, iters = m.nt, m.iters
    body_tiles = SLOTS * BODY_GROUPS
    with ExitStack() as ctx:
        sb = lambda n, s, d=F32: ctx.enter_context(nc.sbuf_tensor(n, s, d))
        sem = lambda n: ctx.enter_context(nc.semaphore(n))
        lo_i, hi_a, hi_b, hi_i = (sb(n, [P, nt], I32) for n in ("lo_i", "hi_a", "hi_b", "hi_i"))
        lo_f, hi_f = sb("lo_f", [P, nt]), sb("hi_f", [P, nt])
        lo_now = sb("lo_now", [P, body_tiles])
        iota_hi, iota_lo = sb("iota_hi", [P, nt], BF16), sb("iota_lo", [P, P], BF16)
        hot_hi, hot_lo = sb("hot_hi", [P, body_tiles, nt], BF16), sb("hot_lo", [P, body_tiles, P], BF16)
        degree, root = sb("degree", [P, nt]), sb("root", [P, nt])
        zeros = sb("zeros", [P, SLOTS * D])
        counts = ctx.enter_context(nc.psum_tensor("counts", [P, nt], F32))
        dst_in, rows_in, zeroed = sem("dst_in"), sem("rows_in"), sem("zeroed")
        consts, split, digits = sem("consts"), sem("split"), sem("digits")
        lo_copied, hi_hot, lo_hot, counted = sem("lo_copied"), sem("hi_hot"), sem("lo_hot"), sem("counted")
        degree_ok, rooted, inverted = sem("degree_ok"), sem("rooted"), sem("inverted")
        block = ctx.enter_context(nc.Block())

        @block.sync
        def _(sp):
            sp.dma_start(m.dst_i[:, :], m.dst_cols).then_inc(dst_in, 16)
            sp.dma_start(m.src_i[:, :], m.src_cols).then_inc(rows_in, 16)
            sp.dma_start(m.b1[:, :], m.b1_dram.partition_broadcast(P)).then_inc(rows_in, 16)
            sp.dma_start(m.b2[:, :], m.b2_dram.partition_broadcast(P)).then_inc(rows_in, 16)
            sp.dma_start(m.b_out[:, :], m.b_out_dram.partition_broadcast(P)).then_inc(rows_in, 16)
            sp.wait_ge(zeroed, 1)
            for sums in m.sums:
                sp.dma_start(sums[m.np:m.np + GROUP, :].rearrange("(p j) d -> p (j d)", j=SLOTS),
                             zeros[:, :]).then_inc(rows_in, 16)
            sp.wait_ge(rows_in, 96)

        @block.gpsimd
        def _(pool):
            pool.iota(iota_hi[:, :], [[1, nt]], base=-(nt // 2), channel_multiplier=0,
                      allow_small_or_imprecise_dtypes=True).then_inc(consts, 1)
            pool.iota(iota_lo[:, :], [[1, P]], base=0, channel_multiplier=0,
                      allow_small_or_imprecise_dtypes=True).then_inc(consts, 1)
            pool.memset(zeros[:, :], 0.0).then_inc(zeroed, 1)
            pool.memset(m.ident[:, :], 0.0).then_inc(consts, 1)
            pool.memset(m.earlier[:, :], 1.0).then_inc(consts, 1)
            pool.iota(m.spare[:, :], [[1, SLOTS]], base=m.np, channel_multiplier=SLOTS,
                      allow_small_or_imprecise_dtypes=True).then_inc(consts, 1)
            pool.wait_ge(consts, 5)
            pool.affine_select(out=m.ident[:, :], in_=m.ident[:, :], compare_op=ALU.not_equal,
                               fill=1.0, base=0, pattern=[[-1, P]], channel_multiplier=1).then_inc(consts, 1)
            last = m.earlier[:, (SLOTS - 1) * P:]
            pool.affine_select(out=last, in_=last, compare_op=ALU.is_gt, fill=0.0, base=0,
                               pattern=[[-1, P]], channel_multiplier=1).then_inc(consts, 1)
            pool.wait_ge(digits, 2)

            def body(it):
                wait(pool, lo_hot, body_tiles * it)
                pool.tensor_copy(lo_now[:, :], lo_f[:, bass.ds(it * body_tiles, body_tiles)]
                                 ).then_inc(lo_copied, 1)
                pool.wait_ge(lo_copied, it + 1)
                for k in range(body_tiles):
                    t = it * body_tiles + k
                    wait(pool, counted, t - body_tiles + 1)
                    carry(pool, m.pool_passed)
                    pool.tensor_scalar(hot_lo[:, k, :], iota_lo[:, :], lo_now[:, k:k + 1], None,
                                       ALU.is_equal).then_inc(lo_hot, 1)
            loop(pool, iters, body)

        @block.vector
        def _(dve):
            dve.wait_ge(dst_in, 16)
            dve.tensor_scalar(lo_i[:, :], m.dst_i[:, :], 2, P - 1, ALU.logical_shift_right,
                              ALU.bitwise_and).then_inc(split, 1)
            dve.tensor_scalar(hi_a[:, :], m.dst_i[:, :], 9, 2, ALU.logical_shift_right,
                              ALU.logical_shift_left).then_inc(split, 1)
            dve.tensor_scalar(hi_b[:, :], m.dst_i[:, :], SLOTS - 1, None, ALU.bitwise_and).then_inc(split, 1)
            dve.tensor_copy(m.dst_f[:, :], m.dst_i[:, :]).then_inc(split, 1)
            dve.wait_ge(split, 4)
            dve.tensor_copy(lo_f[:, :], lo_i[:, :]).then_inc(digits, 1)
            dve.tensor_tensor(hi_i[:, :], hi_a[:, :], hi_b[:, :], ALU.bitwise_or).then_inc(split, 1)
            dve.wait_ge(split, 5)
            dve.tensor_scalar(hi_f[:, :], hi_i[:, :], float(-(nt // 2)), None, ALU.add).then_inc(digits, 1)
            dve.wait_ge(digits, 2)
            dve.wait_ge(consts, 2)

            def body(it):
                for k in range(body_tiles):
                    t = it * body_tiles + k
                    wait(dve, counted, t - body_tiles + 1)
                    dve.tensor_scalar(hot_hi[:, k, :], iota_hi[:, :], hi_f[:, bass.ds(t, 1)], None,
                                      ALU.is_equal).then_inc(hi_hot, 1)
            loop(dve, iters, body)
            dve.wait_ge(counted, nt)
            dve.tensor_scalar(degree[:, :], counts[:, :], 1.0, 1e-12, ALU.add, ALU.max).then_inc(degree_ok, 1)
            dve.wait_ge(rooted, 1)
            dve.reciprocal(m.dinv[:, :], root[:, :]).then_inc(inverted, 1)
            dve.wait_ge(inverted, 1)

        @block.scalar
        def _(act):
            act.wait_ge(degree_ok, 1)
            act.activation(root[:, :], degree[:, :], ACT.Sqrt).then_inc(rooted, 1)

        @block.tensor
        def _(pe):
            def body(it):
                for k in range(body_tiles):
                    t = it * body_tiles + k
                    pe.wait_ge(hi_hot, t + 1)
                    pe.wait_ge(lo_hot, t + 1)
                    pe.matmul(counts[:, :], hot_lo[:, k, :], hot_hi[:, k, :],
                              start=isinstance(t, int) and t == 0,
                              stop=isinstance(t, int) and t == nt - 1).then_inc(counted, 1)
            loop(pe, iters, body)


def transform(nc, m, conv):
    iters = m.iters
    source = grouped(m.x if conv == 0 else m.sums[0], D)
    stores = [grouped(m.messages[conv], D), grouped(m.sums[conv], D)]
    weights = m.w1 if conv == 0 else m.w2
    with ExitStack() as ctx:
        sb = lambda n, s, d=F32: ctx.enter_context(nc.sbuf_tensor(f"{n}{conv}", s, d))
        sem = lambda n: ctx.enter_context(nc.semaphore(f"{n}{conv}"))
        ps = lambda n, s: ctx.enter_context(nc.psum_tensor(f"{n}{conv}", s, F32))
        w = sb("w", [P, KD, D])
        rows = sb("rows", [P, 2, SLOTS, D])
        cent = sb("cent", [P, 2, SLOTS, D])
        cent_t = sb("cent_t", [P, 2, 2, KD, P])
        out = sb("out", [P, 2, SLOTS, D])
        squares = sb("squares", [P, D])
        stats = sb("stats", [P, 2, SLOTS, 6])
        mean_var = sb("mean_var", [P, 2, SLOTS, 2])
        var = sb("var", [P, 2, SLOTS])
        root = sb("root_r", [P, 2, SLOTS])
        safe = sb("safe", [P, 2, SLOTS])
        inverse = sb("inverse", [P, 2, SLOTS])
        factor = sb("factor", [P, 2, SLOTS])
        turned = ps("turned", [P, 2, 2, KD, P])
        product = ps("product", [P, 2, 2, D])
        w_in = sem("w_in")
        rows_in = [sem(f"rows_in{b}_") for b in range(2)]
        stored = [sem(f"stored{b}_") for b in range(2)]
        stats_ok, mean_ok, var_ok, cent_ok = sem("stats_ok"), sem("mean_ok"), sem("var_ok"), sem("cent_ok")
        squared, rooted, made_safe, inverted = sem("squared"), sem("rooted"), sem("made_safe"), sem("inverted")
        saved, factor_ok = sem("saved"), sem("factor_ok")
        turned_ok, copied, product_ok, out_ok = sem("turned_ok"), sem("copied"), sem("product_ok"), sem("out_ok")
        block = ctx.enter_context(nc.Block())

        @block.sync
        def _(sp):
            sp.dma_start(w[:, :, :], weights.rearrange("(k p) n -> p k n", p=P)).then_inc(w_in, 16)

            def load(g, b):
                wait(sp, cent_ok, SLOTS * (g - 1))
                sp.dma_start(rows[:, b, :, :], one_group(source, g, D)).then_inc(rows_in[b], 16)

            def body(it):
                for b in range(2):
                    g = it * 2 + b
                    if not (isinstance(g, int) and g + 2 >= m.ng):
                        load(g + 2, b)
                    sp.wait_ge(out_ok, 2 * g + 2)
                    for dram in stores:
                        sp.dma_start(one_group(dram, g, D), out[:, b, :, :]).then_inc(stored[b], 16)
            load(0, 0)
            load(1, 1)
            loop(sp, iters, body)
            for b in range(2):
                sp.wait_ge(stored[b], 32 * iters)

        @block.vector
        def _(dve):
            def layernorm(it, b):
                g = it * 2 + b
                cols = bass.ds(g * SLOTS, SLOTS)
                dve.wait_ge(rows_in[b], 16 * (it + 1))
                for j in range(SLOTS):
                    dve.bn_stats(stats[:, b, j, :], rows[:, b, j, :]).then_inc(stats_ok, 1)
                dve.wait_ge(stats_ok, SLOTS * (g + 1))
                carry(dve, m.dve_passed)
                for j in range(SLOTS):
                    dve.bn_aggr(mean_var[:, b, j, :], stats[:, b, j, :]).then_inc(mean_ok, 1)
                dve.wait_ge(mean_ok, SLOTS * (g + 1))
                dve.tensor_scalar(var[:, b, :], mean_var[:, b, :, 1], LN_EPS, None, ALU.add).then_inc(var_ok, 1)
                wait(dve, turned_ok, 2 * (g - 1))
                for j in range(SLOTS):
                    dve.tensor_scalar(cent[:, b, j, :], rows[:, b, j, :], mean_var[:, b, j, 0:1], None,
                                      ALU.subtract).then_inc(cent_ok, 1)
                dve.tensor_copy(m.mean[:, cols], mean_var[:, b, :, 0]).then_inc(saved, 1)
                dve.wait_ge(rooted, g + 1)
                dve.reciprocal(inverse[:, b, :], root[:, b, :]).then_inc(inverted, 1)
                dve.wait_ge(inverted, g + 1)
                dve.tensor_copy(m.rstd[:, cols], inverse[:, b, :]).then_inc(saved, 1)
                dve.tensor_tensor(factor[:, b, :], inverse[:, b, :], m.dinv[:, cols], ALU.mult
                                  ).then_inc(factor_ok, 1)

            def normalise(it, b):
                g = it * 2 + b
                cols = bass.ds(g * SLOTS, SLOTS)
                dve.wait_ge(rows_in[b], 16 * (it + 1))
                wait(dve, turned_ok, 2 * (g - 1))
                wait(dve, rooted, g - 1)
                for j in range(SLOTS):
                    dve.scalar_tensor_tensor(cent[:, b, j, :], rows[:, b, j, :],
                                             m.dinv[:, bass.ds(g * SLOTS + j, 1)], m.b1[:, :],
                                             ALU.mult, ALU.add).then_inc(cent_ok, 1)
                dve.wait_ge(rooted, g + 1)
                dve.tensor_scalar(safe[:, b, :], root[:, b, :], 1e-12, None, ALU.max).then_inc(made_safe, 1)
                dve.wait_ge(made_safe, g + 1)
                dve.reciprocal(inverse[:, b, :], safe[:, b, :]).then_inc(inverted, 1)
                dve.wait_ge(inverted, g + 1)
                dve.tensor_tensor(factor[:, b, :], inverse[:, b, :], m.dinv[:, cols], ALU.mult
                                  ).then_inc(factor_ok, 1)

            def body(it):
                for b in range(2):
                    (layernorm if conv == 0 else normalise)(it, b)
            loop(dve, iters, body)
            if conv == 0:
                dve.wait_ge(saved, 2 * m.ng)
                dve.tensor_scalar(m.scale[:, :], m.rstd[:, :], 1.0, None, ALU.add).then_inc(saved, 1)
                dve.scalar_tensor_tensor(m.shift[:, :], m.mean[:, :], -1.0, m.rstd[:, :],
                                         ALU.mult, ALU.mult).then_inc(saved, 1)
                dve.wait_ge(saved, 2 * m.ng + 2)

        @block.scalar
        def _(act):
            def roots(it, b):
                g = it * 2 + b
                if conv == 0:
                    act.wait_ge(var_ok, g + 1)
                    act.activation(root[:, b, :], var[:, b, :], ACT.Sqrt).then_inc(rooted, 1)
                    return
                for j in range(SLOTS):
                    act.wait_ge(cent_ok, SLOTS * g + j + 1)
                    wait(act, squared, SLOTS * g + j)
                    act.activation(squares[:, :], cent[:, b, j, :], ACT.Square,
                                   accum_out=var[:, b, j:j + 1]).then_inc(squared, 1)
                act.wait_ge(squared, SLOTS * (g + 1))
                act.activation(root[:, b, :], var[:, b, :], ACT.Sqrt).then_inc(rooted, 1)

            def copy_turned(u, k):
                act.wait_ge(turned_ok, u + 1)
                wait(act, product_ok, u - 1)
                act.activation(cent_t[:, k % 2, :, :, :], turned[:, k % 2, :, :, :], ACT.Copy
                               ).then_inc(copied, 1)

            def scale_product(u, k, it):
                b = k // 2
                act.wait_ge(product_ok, u + 1)
                if k % 2 == 0:
                    act.wait_ge(factor_ok, it * 2 + b + 1)
                    wait(act, stored[b], 32 * it)
                for h in range(2):
                    j = k % 2 * 2 + h
                    done = act.activation(out[:, b, j, :], product[:, k % 2, h, :], ACT.Copy,
                                          scale=factor[:, b, j:j + 1])
                done.then_inc(out_ok, 1)

            def body(it):
                for k in range(4):
                    u = it * 4 + k
                    if k % 2 == 0:
                        roots(it, k // 2)
                    copy_turned(u, k)
                    if not (isinstance(u, int) and u == 0):
                        scale_product(u - 1, (k - 1) % 4, it if k else it - 1)
            loop(act, iters, body)
            scale_product(4 * iters - 1, 3, iters - 1)

        @block.tensor
        def _(pe):
            pe.wait_ge(w_in, 16)

            def turn(u, k):
                b = k // 2
                pe.wait_ge(cent_ok, 2 * u + 2)
                wait(pe, copied, u - 1)
                for h in range(2):
                    for c in range(KD):
                        done = pe.transpose(turned[:, k % 2, h, c, :],
                                            cent[:, b, k % 2 * 2 + h, c * P:(c + 1) * P], m.ident[:, :])
                done.then_inc(turned_ok, 1)

            def multiply(u, k):
                pe.wait_ge(copied, u + 1)
                wait(pe, out_ok, u - 1)
                for h in range(2):
                    for c in range(KD):
                        done = pe.matmul(product[:, k % 2, h, :], cent_t[:, k % 2, h, c, :], w[:, c, :],
                                         start=c == 0, stop=c == KD - 1)
                done.then_inc(product_ok, 1)

            def body(it):
                for k in range(4):
                    u = it * 4 + k
                    turn(u, k)
                    if not (isinstance(u, int) and u == 0):
                        multiply(u - 1, (k - 1) % 4)
            loop(pe, iters, body)
            multiply(4 * iters - 1, 3)


def add_edges(nc, m, conv):
    iters = m.iters
    first_block = [0, 1, 3, 6]
    messages, sums = m.messages[conv], m.sums[conv]
    with ExitStack() as ctx:
        sb = lambda n, s, d=F32: ctx.enter_context(nc.sbuf_tensor(f"{n}{conv}", s, d))
        sem = lambda n: ctx.enter_context(nc.semaphore(f"{n}{conv}"))
        dst_row = sb("dst_row", [P, 2, GROUP], I32)
        same = sb("same", [P, 2, 10, P])
        seen = sb("seen", [P, SLOTS, GROUP])
        n_before = sb("n_before", [P, 2, SLOTS])
        not_owner = sb("not_owner", [P, 2, SLOTS])
        to_spare = sb("to_spare", [P, 2, SLOTS])
        moved = sb("moved", [P, 2, SLOTS])
        target = sb("target", [P, 2, SLOTS], I32)
        src_now = sb("src_now", [P, 2, SLOTS], I32)
        got = sb("got", [P, 2, SLOTS, D])
        merged = sb("merged", [P, 2, SLOTS, D])
        total = ctx.enter_context(nc.psum_tensor(f"total{conv}", [P, 2, SLOTS, D], F32))
        row_in = [sem(f"row_in{b}_") for b in range(2)]
        gathered = [sem(f"gathered{b}_") for b in range(2)]
        added = [sem(f"added{b}_") for b in range(2)]
        src_ok, same_ok, before_ok, spare_ok, moved_ok, target_ok = (
            sem(n) for n in ("src_ok", "same_ok", "before_ok", "spare_ok", "moved_ok", "target_ok"))
        total_ok, merged_ok = sem("total_ok"), sem("merged_ok")
        block = ctx.enter_context(nc.Block())

        @block.sync
        def _(sp):
            def body(it):
                for b in range(2):
                    g = it * 2 + b
                    wait(sp, before_ok, SLOTS * (g - 1))
                    sp.dma_start(dst_row[:, b, :], m.dst_rows[bass.ds(g, 1), :].to_broadcast([P, GROUP])
                                 ).then_inc(row_in[b], 16)
            loop(sp, iters, body)

        @block.vector
        def _(dve):
            def body(it):
                for b in range(2):
                    g = it * 2 + b
                    cols = bass.ds(g * SLOTS, SLOTS)
                    wait(dve, gathered[b], 64 * it)
                    dve.tensor_copy(src_now[:, b, :], m.src_i[:, cols]).then_inc(src_ok, 1)
                    dve.wait_ge(row_in[b], 16 * (it + 1))
                    wait(dve, total_ok, 2 * (g - 1))
                    for q in range(SLOTS):
                        f = first_block[q]
                        dve.tensor_scalar(same[:, b, f:f + q + 1, :], dst_row[:, b, 0:(q + 1) * P],
                                          m.dst_f[:, bass.ds(g * SLOTS + q, 1)], None, ALU.is_equal
                                          ).then_inc(same_ok, 1)
                    wait(dve, moved_ok, g - 1)
                    for q in range(SLOTS):
                        dve.scalar_tensor_tensor(
                            seen[:, q, 0:(q + 1) * P], dst_row[:, b, 0:(q + 1) * P],
                            m.dst_f[:, bass.ds(g * SLOTS + q, 1)],
                            m.earlier[:, (SLOTS - 1 - q) * P:], ALU.is_equal, ALU.mult,
                            accum_out=n_before[:, b, q:q + 1]).then_inc(before_ok, 1)
                    dve.tensor_tensor(to_spare[:, b, :], m.spare[:, :], m.dst_f[:, cols], ALU.subtract
                                      ).then_inc(spare_ok, 1)
                    dve.wait_ge(before_ok, SLOTS * (g + 1))
                    dve.tensor_scalar(not_owner[:, b, :], n_before[:, b, :], 1.0, None, ALU.min
                                      ).then_inc(spare_ok, 1)
                    dve.wait_ge(spare_ok, 2 * (g + 1))
                    dve.tensor_tensor(moved[:, b, :], not_owner[:, b, :], to_spare[:, b, :], ALU.mult
                                      ).then_inc(moved_ok, 1)
                    dve.wait_ge(moved_ok, g + 1)
                    wait(dve, added[b], 64 * it)
                    dve.tensor_tensor(target[:, b, :], moved[:, b, :], m.dst_f[:, cols], ALU.add
                                      ).then_inc(target_ok, 1)
            loop(dve, iters, body)

        @block.gpsimd
        def _(pool):
            def gather(g, b):
                pool.wait_ge(src_ok, g + 1)
                wait(pool, total_ok, 2 * (g - 1))
                carry(pool, m.pool_passed)
                for q in range(SLOTS):
                    pool.indirect_dma_start(
                        out=got[:, b, q, :], out_offset=None, in_=messages,
                        in_offset=bass.IndirectOffsetOnAxis(ap=src_now[:, b, q:q + 1], axis=0)
                    ).then_inc(gathered[b], 16)

            def scatter(it, b):
                g = it * 2 + b
                pool.wait_ge(target_ok, g + 1)
                pool.wait_ge(merged_ok, 2 * g + 2)
                wait(pool, added[1 - b], 64 * (it + b))
                carry(pool, m.pool_passed)
                for q in range(SLOTS):
                    pool.indirect_dma_start(
                        out=sums, out_offset=bass.IndirectOffsetOnAxis(ap=target[:, b, q:q + 1], axis=0),
                        in_=merged[:, b, q, :], in_offset=None, compute_op=ALU.add
                    ).then_inc(added[b], 16)

            def body(it):
                for b in range(2):
                    g = it * 2 + b
                    if not (isinstance(g, int) and g + 1 >= m.ng):
                        gather(g + 1, 1 - b)
                    scatter(it, b)
            gather(0, 0)
            loop(pool, iters, body)
            for b in range(2):
                pool.wait_ge(added[b], 64 * iters)

        @block.tensor
        def _(pe):
            def body(it):
                for b in range(2):
                    g = it * 2 + b
                    pe.wait_ge(gathered[b], 64 * (it + 1))
                    pe.wait_ge(same_ok, SLOTS * (g + 1))
                    for h in range(2):
                        wait(pe, merged_ok, 2 * (g - 2) + h + 1)
                        for owner in (2 * h, 2 * h + 1):
                            for q in range(owner, SLOTS):
                                done = pe.matmul(total[:, b, owner, :],
                                                 same[:, b, first_block[q] + owner, :], got[:, b, q, :],
                                                 start=q == owner, stop=q == SLOTS - 1)
                        done.then_inc(total_ok, 1)
            loop(pe, iters, body)

        @block.scalar
        def _(act):
            def body(it):
                for b in range(2):
                    g = it * 2 + b
                    wait(act, added[b], 64 * it)
                    for h in range(2):
                        act.wait_ge(total_ok, 2 * g + h + 1)
                        act.activation(merged[:, b, 2 * h:2 * h + 2, :], total[:, b, 2 * h:2 * h + 2, :],
                                       ACT.Copy).then_inc(merged_ok, 1)
            loop(act, iters, body)


def prepare_attention(nc, m):
    with ExitStack() as ctx:
        sb = lambda n, s, d=F32: ctx.enter_context(nc.sbuf_tensor(n, s, d))
        sem = lambda n: ctx.enter_context(nc.semaphore(n))
        wx_t = sb("wx_t", [HD, HEADS, D])
        w_slice = sb("w_slice", [HD, SL])
        bx_t = sb("bx_t", [HD, HEADS])
        b_slice = sb("b_slice", [1, SL])
        temp, clipped, inv_temp = sb("temp", [P, HEADS]), sb("clipped", [P, HEADS]), sb("inv_temp", [P, HEADS])
        bias0, bias = sb("bias0", [1, HS]), sb("bias", [1, HS])
        rest1, rest2 = sb("rest1", [1, HS]), sb("rest2", [1, HS])
        parts = sb("parts", [1, 3, HS], BF16)
        folded = ctx.enter_context(nc.psum_tensor("folded", [P, KD, HS], F32))
        bias_ps = ctx.enter_context(nc.psum_tensor("bias_ps", [1, HS], F32))
        inputs_in, parts_in, step, projected = sem("inputs_in"), sem("parts_in"), sem("step"), sem("projected")
        block = ctx.enter_context(nc.Block())

        @block.sync
        def _(sp):
            sp.dma_start(wx_t[:, :, :], m.wx_t_dram.rearrange("(h c) f -> c h f", c=HD)).then_inc(inputs_in, 16)
            sp.dma_start(w_slice[:, :], m.w_slice_dram).then_inc(inputs_in, 16)
            sp.dma_start(bx_t[:, :], m.bx_t_dram).then_inc(inputs_in, 16)
            sp.dma_start(b_slice[:, :], m.b_slice_dram).then_inc(inputs_in, 16)
            sp.dma_start(temp[:, :], m.temp_dram.partition_broadcast(P)).then_inc(inputs_in, 16)
            sp.wait_ge(step, 9)
            for r in range(3):
                sp.dma_start(m.bias_rows[r:r + 1, :], parts[0:1, r, :]).then_inc(parts_in, 16)
            sp.wait_ge(parts_in, 48)

        @block.gpsimd
        def _(pool):
            pool.memset(m.ones3[:, :], 1.0).then_inc(m.const_ok, 1)
            pool.memset(m.y[:, :, :, D:D + 2], 1.0).then_inc(m.const_ok, 1)
            pool.memset(m.half[:, :], -0.5).then_inc(m.const_ok, 1)
            pool.wait_ge(m.const_ok, 3)

        @block.tensor
        def _(pe):
            pe.wait_ge(inputs_in, 80)
            for c in range(KD):
                for h in range(HEADS):
                    pe.matmul(folded[:, c, h * SL:(h + 1) * SL], wx_t[:, h, c * P:(c + 1) * P],
                              w_slice[:, :], start=True, stop=True)
            for h in range(HEADS):
                done = pe.matmul(bias_ps[:, h * SL:(h + 1) * SL], bx_t[:, h:h + 1], w_slice[:, :],
                                 start=True, stop=True)
            done.then_inc(projected, 1)

        @block.vector
        def _(dve):
            dve.wait_ge(inputs_in, 80)
            dve.tensor_scalar(clipped[:, :], temp[:, :], 0.1, 5.0, ALU.max, ALU.min).then_inc(step, 1)
            dve.wait_ge(step, 1)
            dve.reciprocal(inv_temp[:, :], clipped[:, :]).then_inc(step, 1)
            dve.wait_ge(step, 2)
            dve.wait_ge(projected, 1)
            for c in range(KD):
                dve.tensor_tensor(m.w_logit[:, c, :].rearrange("p (h s) -> p h s", h=HEADS),
                                  folded[:, c, :].rearrange("p (h s) -> p h s", h=HEADS),
                                  inv_temp[:, :, None].to_broadcast([P, HEADS, SL]), ALU.mult
                                  ).then_inc(projected, 1)
            heads = lambda a: a[:, :].rearrange("p (h s) -> p h s", h=HEADS)
            dve.tensor_tensor(heads(bias0), heads(bias_ps),
                              b_slice[:, None, :].to_broadcast([1, HEADS, SL]), ALU.add).then_inc(step, 1)
            dve.wait_ge(step, 3)
            dve.tensor_tensor(heads(bias), heads(bias0),
                              inv_temp[0:1, :, None].to_broadcast([1, HEADS, SL]), ALU.mult).then_inc(step, 1)
            dve.wait_ge(step, 4)
            dve.tensor_copy(parts[:, 0, :], bias[:, :]).then_inc(step, 1)
            dve.wait_ge(step, 5)
            dve.tensor_tensor(rest1[:, :], bias[:, :], parts[:, 0, :], ALU.subtract).then_inc(step, 1)
            dve.wait_ge(step, 6)
            dve.tensor_copy(parts[:, 1, :], rest1[:, :]).then_inc(step, 1)
            dve.wait_ge(step, 7)
            dve.tensor_tensor(rest2[:, :], rest1[:, :], parts[:, 1, :], ALU.subtract).then_inc(step, 1)
            dve.wait_ge(step, 8)
            dve.tensor_copy(parts[:, 2, :], rest2[:, :]).then_inc(step, 1)
            dve.wait_ge(projected, 3)


def attend_tokens(nc, m):
    iters = m.iters
    last_rows = (m.n - (m.ng - 1) * GROUP) // SLOTS
    x_dram, sums_dram = grouped(m.x, D), grouped(m.sums[1], D)
    x1_dram, weights_dram = grouped(m.x1, D), grouped(m.slice_weights, HS)
    with ExitStack() as ctx:
        sb = lambda n, s, d=F32: ctx.enter_context(nc.sbuf_tensor(n, s, d))
        sem = lambda n: ctx.enter_context(nc.semaphore(n))
        ps = lambda n, s: ctx.enter_context(nc.psum_tensor(n, s, F32))
        x_in, sum_in = sb("x_in", [P, 2, SLOTS, D]), sb("sum_in", [P, 2, SLOTS, D])
        base = sb("base", [P, 2, SLOTS, D])
        x1 = sb("x1_now", [P, 2, SLOTS, D])
        stats = sb("a_stats", [P, 2, SLOTS, 6])
        mean_var = sb("a_mean_var", [P, 2, SLOTS, 2])
        var, rstd = sb("a_var", [P, 2, SLOTS]), sb("a_rstd", [P, 2, SLOTS])
        y_t = sb("y_t", [P, 2, KD, P])
        shifted = sb("shifted", [P, 2, HS])
        expd = sb("expd", [P, 2, HS])
        top, total, inv_total = sb("top", [P, 2, HEADS]), sb("total", [P, 2, HEADS]), sb("inv_total", [P, 2, HEADS])
        weights = sb("weights", [P, 2, SLOTS, HS])
        turned = [ps(f"y_turned{i}", [P, KD, P]) for i in range(2)]
        logits = [ps(f"logits{i}", [P, HS]) for i in range(2)]
        rows_in = [sem(f"a_rows_in{b}") for b in range(2)]
        x1_stored = [sem(f"x1_stored{b}") for b in range(2)]
        w_stored = [sem(f"w_stored{b}") for b in range(2)]
        scaled, biased, x1_ok, stats_ok, mean_ok, var_ok, rstd_ok, y_ok = (
            sem("a_" + n) for n in ("scaled", "biased", "x1_ok", "stats_ok", "mean_ok", "var_ok", "rstd_ok", "y_ok"))
        turned_ok, y_t_ok, logits_ok, top_ok, shifted_ok, exp_ok, total_ok, inv_ok, weights_ok, tokens_ok = (
            sem("a_" + n) for n in ("turned_ok", "y_t_ok", "logits_ok", "top_ok", "shifted_ok", "exp_ok",
                                    "total_ok", "inv_ok", "weights_ok", "tokens_ok"))
        block = ctx.enter_context(nc.Block())
        heads = lambda a: a.rearrange("p (h s) -> p h s", h=HEADS)
        per_head = lambda a: a[:, :, None].to_broadcast([P, HEADS, SL])

        def steps(engine, step):
            def body(it):
                for k in range(2 * SLOTS):
                    step(it, k)
            loop(engine, iters, body)

        def ahead(it, k):
            if k < SLOTS:
                return it, 1
            if isinstance(it, int) and it == iters - 1:
                return None
            return it + 1, 0

        @block.sync
        def _(sp):
            def load(g, b):
                wait(sp, x1_ok, SLOTS * (g - 1))
                sp.dma_start(x_in[:, b, :, :], one_group(x_dram, g, D)).then_inc(rows_in[b], 16)
                sp.dma_start(sum_in[:, b, :, :], one_group(sums_dram, g, D)).then_inc(rows_in[b], 16)

            def body(it):
                for b in range(2):
                    g = it * 2 + b
                    sp.wait_ge(x1_ok, SLOTS * (g + 1))
                    sp.dma_start(one_group(x1_dram, g, D), x1[:, b, :, :]).then_inc(x1_stored[b], 16)
                    if not (isinstance(g, int) and g + 2 >= m.ng):
                        load(g + 2, b)
                    sp.wait_ge(weights_ok, SLOTS * (g + 1))
                    sp.dma_start(one_group(weights_dram, g, HS), weights[:, b, :, :]).then_inc(w_stored[b], 16)
            load(0, 0)
            load(1, 1)
            loop(sp, iters, body)
            for b in range(2):
                sp.wait_ge(x1_stored[b], 16 * iters)
                sp.wait_ge(w_stored[b], 16 * iters)

        @block.scalar
        def _(act):
            def scale_half(it, b, half):
                g = it * 2 + b
                act.wait_ge(rows_in[b], 32 * (it + 1))
                wait(act, x1_ok, SLOTS * (g - 1))
                for j in (2 * half, 2 * half + 1):
                    col = bass.ds(g * SLOTS + j, 1)
                    act.activation(base[:, b, j, :], x_in[:, b, j, :], ACT.Identity, bias=m.shift[:, col],
                                   scale=m.scale[:, col]).then_inc(scaled, 1)

            def copy_turned(t, par):
                act.wait_ge(turned_ok, t + 1)
                wait(act, logits_ok, t - 1)
                act.activation(y_t[:, par, :, :], turned[par][:, :, :], ACT.Copy).then_inc(y_t_ok, 1)

            def step(it, k):
                t = it * 2 * SLOTS + k
                nxt = ahead(it, k)
                if k % SLOTS < 2 and nxt is not None:
                    scale_half(*nxt, k % SLOTS)
                if not (isinstance(t, int) and t == m.nt - 1):
                    copy_turned(t + 1, (k + 1) % 2)
                act.wait_ge(shifted_ok, t + 1)
                wait(act, total_ok, t - 1)
                wait(act, weights_ok, t - 1)
                act.activation(expd[:, k % 2, :], shifted[:, k % 2, :], ACT.Exp).then_inc(exp_ok, 1)

            scale_half(0, 0, 0)
            scale_half(0, 0, 1)
            copy_turned(0, 0)
            steps(act, step)

        @block.gpsimd
        def _(pool):
            def bias_half(it, b, half):
                for j in (2 * half, 2 * half + 1):
                    pool.wait_ge(scaled, (it * 2 + b) * SLOTS + j + 1)
                    pool.tensor_tensor(base[:, b, j, :], base[:, b, j, :], m.b2[:, :], ALU.add).then_inc(biased, 1)

            def rstd_half(it, b, half):
                pool.wait_ge(var_ok, (it * 2 + b) * 2 + half + 1)
                two = slice(2 * half, 2 * half + 2)
                pool.tensor_tensor(rstd[:, b, two], var[:, b, two], m.half[:, :], ALU.pow).then_inc(rstd_ok, 1)

            def normalise(t, k, it):
                b, j = k // SLOTS, k % SLOTS
                pool.wait_ge(inv_ok, t + 1)
                wait(pool, tokens_ok, t - 7)
                if j == 0:
                    wait(pool, w_stored[b], 16 * it)
                pool.tensor_tensor(heads(weights[:, b, j, :]), heads(expd[:, k % 2, :]),
                                   per_head(inv_total[:, k % 2, :]), ALU.mult).then_inc(weights_ok, 1)

            def step(it, k):
                t = it * 2 * SLOTS + k
                j, nxt = k % SLOTS, ahead(it, k)
                if j < 2 and nxt is not None:
                    bias_half(*nxt, j)
                if 1 <= j < 3 and nxt is not None:
                    rstd_half(*nxt, j - 1)
                if not (isinstance(t, int) and t == 0):
                    normalise(t - 1, (k - 1) % (2 * SLOTS), it if k else it - 1)

            for half in range(2):
                bias_half(0, 0, half)
            for half in range(2):
                rstd_half(0, 0, half)
            steps(pool, step)
            normalise(m.nt - 1, 2 * SLOTS - 1, iters - 1)

        @block.vector
        def _(dve):
            def residual_half(it, b, half):
                g = it * 2 + b
                if half == 0:
                    wait(dve, x1_stored[b], 16 * it)
                tiles = (2 * half, 2 * half + 1)
                for j in tiles:
                    dve.wait_ge(biased, g * SLOTS + j + 1)
                    dve.scalar_tensor_tensor(x1[:, b, j, :], sum_in[:, b, j, :],
                                             m.dinv[:, bass.ds(g * SLOTS + j, 1)], base[:, b, j, :],
                                             ALU.mult, ALU.add).then_inc(x1_ok, 1)
                for j in tiles:
                    dve.wait_ge(x1_ok, g * SLOTS + j + 1)
                    dve.bn_stats(stats[:, b, j, :], x1[:, b, j, :]).then_inc(stats_ok, 1)
                for j in tiles:
                    dve.wait_ge(stats_ok, g * SLOTS + j + 1)
                    carry(dve, m.dve_passed)
                    dve.bn_aggr(mean_var[:, b, j, :], stats[:, b, j, :]).then_inc(mean_ok, 1)
                dve.wait_ge(mean_ok, g * SLOTS + 2 * half + 2)
                two = slice(2 * half, 2 * half + 2)
                dve.tensor_scalar(var[:, b, two], mean_var[:, b, two, 1], LN_EPS, None, ALU.add
                                  ).then_inc(var_ok, 1)

            def y_half(it, b, half):
                g = it * 2 + b
                dve.wait_ge(rstd_ok, 2 * g + half + 1)
                if half == 0:
                    wait(dve, tokens_ok, SLOTS * (g - 1))
                for j in (2 * half, 2 * half + 1):
                    dve.tensor_scalar(m.y[:, b, j, 0:D], x1[:, b, j, :], mean_var[:, b, j, 0:1],
                                      rstd[:, b, j:j + 1], ALU.subtract, ALU.mult).then_inc(y_ok, 1)

            def sums(t, par):
                dve.wait_ge(exp_ok, t + 1)
                dve.tensor_reduce(total[:, par, :], heads(expd[:, par, :]), AX.X, ALU.add).then_inc(total_ok, 1)
                dve.wait_ge(total_ok, t + 1)
                wait(dve, weights_ok, t - 1)
                dve.reciprocal(inv_total[:, par, :], total[:, par, :]).then_inc(inv_ok, 1)

            def step(it, k):
                t = it * 2 * SLOTS + k
                j, nxt = k % SLOTS, ahead(it, k)
                if j >= 2 and nxt is not None:
                    y_half(*nxt, j - 2)
                if 1 <= j < 3 and nxt is not None:
                    residual_half(*nxt, j - 1)
                par = k % 2
                dve.wait_ge(logits_ok, t + 1)
                dve.tensor_reduce(top[:, par, :], heads(logits[par][:, :]), AX.X, ALU.max).then_inc(top_ok, 1)
                dve.wait_ge(top_ok, t + 1)
                wait(dve, exp_ok, t - 1)
                dve.tensor_tensor(heads(shifted[:, par, :]), heads(logits[par][:, :]),
                                  per_head(top[:, par, :]), ALU.subtract).then_inc(shifted_ok, 1)
                if not (isinstance(t, int) and t == 0):
                    sums(t - 1, 1 - par)

            for half in range(2):
                residual_half(0, 0, half)
            for half in range(2):
                y_half(0, 0, half)
            steps(dve, step)
            sums(m.nt - 1, 1)

        @block.tensor
        def _(pe):
            def turn(t, k):
                b, j = k // SLOTS, k % SLOTS
                pe.wait_ge(y_ok, t + 1)
                wait(pe, y_t_ok, t - 1)
                for c in range(KD):
                    done = pe.transpose(turned[k % 2][:, c, :], m.y[:, b, j, c * P:(c + 1) * P], m.ident[:, :])
                done.then_inc(turned_ok, 1)

            def project(t, par):
                wait(pe, shifted_ok, t - 1)
                pe.matmul(logits[par][:, :], m.ones3[:, :], m.bias_rows[:, :], start=True, stop=False)
                pe.wait_ge(y_t_ok, t + 1)
                for c in range(KD):
                    done = pe.matmul(logits[par][:, :], y_t[:, par, c, :], m.w_logit[:, c, :],
                                     start=False, stop=c == KD - 1)
                done.then_inc(logits_ok, 1)

            def add_tokens(t, k):
                b, j = k // SLOTS, k % SLOTS
                pe.wait_ge(weights_ok, t + 1)
                at = t if isinstance(t, int) else None
                rows = last_rows if at is not None and at >= m.nt - SLOTS else P
                for c in range(CH):
                    done = pe.matmul(m.tokens[c][:, :], weights[0:rows, b, j, c * P:(c + 1) * P],
                                     m.y[0:rows, b, j, 0:D + 1], start=at == 0, stop=at == m.nt - 1)
                done.then_inc(tokens_ok, 1)

            def step(it, k):
                t = it * 2 * SLOTS + k
                at = t if isinstance(t, int) else None
                if at != m.nt - 1:
                    turn(t + 1, (k + 1) % (2 * SLOTS))
                project(t, k % 2)
                if at is None or at >= 2:
                    add_tokens(t - 2, (k - 2) % (2 * SLOTS))

            turn(0, 0)
            steps(pe, step)
            for t in (m.nt - 2, m.nt - 1):
                add_tokens(t, t % (2 * SLOTS))


def mix_tokens(nc, m):
    with ExitStack() as ctx:
        sb = lambda n, s, d=F32: ctx.enter_context(nc.sbuf_tensor(n, s, d))
        sem = lambda n: ctx.enter_context(nc.semaphore(n))
        ps = lambda n, s: ctx.enter_context(nc.psum_tensor(n, s, F32))
        w_fx, b_fx = sb("w_fx", [P, KD, HEADS * HD]), sb("b_fx", [1, HEADS * HD])
        w_q, w_k, w_v = sb("w_q", [HD, HD]), sb("w_k", [HD, HD]), sb("w_v", [HD, HD])
        w_out = sb("w_out", [HD, HEADS, D])
        safe, inv = sb("m_safe", [P, CH]), sb("m_inv", [P, CH])
        mean_y = sb("mean_y", [P, CH, D + 1])
        mean_t, share = sb("mean_t", [P, KD, HS]), sb("share", [1, HS])
        token_t = sb("token_t", [HD, HS])
        q_t, k_t, v = sb("q_t", [HD, HS]), sb("k_t", [HD, HS]), sb("v", [SL, HS])
        top, total, inv_total = sb("m_top", [SL, HEADS]), sb("m_total", [SL, HEADS]), sb("m_inv_total", [SL, HEADS])
        shifted, expd, probs, probs_t = (sb(n, [SL, HS]) for n in ("m_shifted", "m_expd", "probs", "probs_t"))
        out_t = sb("out_t", [HD, HEADS, P])
        bank = [ps(f"mix{i}", [P, HS]) for i in range(4)]
        inputs_in, zero_ok, step, made = sem("m_inputs_in"), sem("m_zero_ok"), sem("m_step"), sem("m_made")
        exp_ok = sem("m_exp_ok")
        block = ctx.enter_context(nc.Block())
        heads = lambda a: a.rearrange("p (h s) -> p h s", h=HEADS)
        per_head = lambda a: a[:, :, None].to_broadcast([SL, HEADS, SL])
        head = lambda h: slice(h * SL, (h + 1) * SL)

        @block.sync
        def _(sp):
            sp.dma_start(w_fx[:, :, :], m.w_fx_dram.rearrange("(k p) n -> p k n", p=P)).then_inc(inputs_in, 16)
            sp.dma_start(b_fx[:, :], m.b_fx_dram).then_inc(inputs_in, 16)
            for to, of in ((w_q, m.w_q_dram), (w_k, m.w_k_dram), (w_v, m.w_v_dram)):
                sp.dma_start(to[:, :], of).then_inc(inputs_in, 16)
            sp.dma_start(w_out[:, :, :], m.w_out_dram.rearrange("(h c) n -> c h n", c=HD)).then_inc(inputs_in, 16)

        @block.gpsimd
        def _(pool):
            pool.memset(out_t[:, :, :], 0.0).then_inc(zero_ok, 1)

        @block.tensor
        def _(pe):
            pe.wait_ge(inputs_in, 96)
            pe.wait_ge(step, 6)
            for c in range(CH):
                for k in range(KD):
                    pe.transpose(bank[k][:, c * P:(c + 1) * P], mean_y[:, c, k * P:(k + 1) * P], m.ident[:, :])
                done = pe.transpose(bank[2][0:1, c * P:(c + 1) * P], mean_y[:, c, D:D + 1], m.ident[:, :])
            done.then_inc(made, 1)
            pe.wait_ge(step, 9)
            for h in range(HEADS):
                for k in range(KD):
                    pe.matmul(bank[3][0:HD, head(h)], w_fx[:, k, head(h)], mean_t[:, k, head(h)],
                              start=k == 0, stop=False)
                done = pe.matmul(bank[3][0:HD, head(h)], b_fx[:, head(h)], share[:, head(h)],
                                 start=False, stop=True)
            done.then_inc(made, 1)
            pe.wait_ge(step, 10)
            pe.matmul(bank[0][0:HD, :], w_q[:, :], token_t[:, :], start=True, stop=True)
            pe.matmul(bank[1][0:HD, :], w_k[:, :], token_t[:, :], start=True, stop=True)
            for h in range(HEADS):
                done = pe.matmul(bank[2][0:SL, head(h)], token_t[:, head(h)], w_v[:, :], start=True, stop=True)
            done.then_inc(made, 1)
            pe.wait_ge(step, 13)
            for h in range(HEADS):
                done = pe.matmul(bank[3][0:SL, head(h)], q_t[:, head(h)], k_t[:, head(h)], start=True, stop=True)
            done.then_inc(made, 1)
            pe.wait_ge(step, 18)
            for h in range(HEADS):
                done = pe.transpose(bank[0][0:SL, head(h)], probs[:, head(h)], m.ident[0:SL, 0:SL])
            done.then_inc(made, 1)
            pe.wait_ge(step, 19)
            for h in range(HEADS):
                done = pe.matmul(bank[1][0:HD, head(h)], v[:, head(h)], probs_t[:, head(h)], start=True, stop=True)
            done.then_inc(made, 1)
            pe.wait_ge(step, 21)
            for c in range(CH):
                half = slice(c % 2 * D, (c % 2 + 1) * D)
                pe.matmul(bank[2 + c // 2][:, half], out_t[:, 2 * c, :], w_out[:, 2 * c, :], start=True, stop=False)
                done = pe.matmul(bank[2 + c // 2][:, half], out_t[:, 2 * c + 1, :], w_out[:, 2 * c + 1, :],
                                 start=False, stop=True)
            done.then_inc(made, 1)

        @block.scalar
        def _(act):
            act.wait_ge(step, 15)
            act.activation(expd[:, :], shifted[:, :], ACT.Exp, scale=float(HD) ** -0.5).then_inc(exp_ok, 1)

        @block.vector
        def _(dve):
            for c in range(CH):
                last = dve.tensor_scalar(safe[:, c:c + 1], m.tokens[c][:, D:D + 1], TOKEN_EPS, None, ALU.add)
            last.then_inc(step, 1)
            dve.wait_ge(step, 1)
            dve.reciprocal(inv[:, :], safe[:, :]).then_inc(step, 1)
            dve.wait_ge(step, 2)
            for c in range(CH):
                dve.tensor_scalar(mean_y[:, c, :], m.tokens[c][:, :], inv[:, c:c + 1], None, ALU.mult
                                  ).then_inc(step, 1)
            dve.wait_ge(made, 1)
            for k in range(KD):
                dve.tensor_copy(mean_t[:, k, :], bank[k][:, :]).then_inc(step, 1)
            dve.tensor_copy(share[:, :], bank[2][0:1, :]).then_inc(step, 1)
            dve.wait_ge(made, 2)
            dve.tensor_copy(token_t[:, :], bank[3][0:HD, :]).then_inc(step, 1)
            dve.wait_ge(made, 3)
            for n, to in enumerate((q_t, k_t, v)):
                dve.tensor_copy(to[:, :], bank[n][0:HD, :]).then_inc(step, 1)
            dve.wait_ge(made, 4)
            dve.tensor_reduce(top[:, :], heads(bank[3][0:SL, :]), AX.X, ALU.max).then_inc(step, 1)
            dve.wait_ge(step, 14)
            dve.tensor_tensor(heads(shifted[:, :]), heads(bank[3][0:SL, :]), per_head(top[:, :]),
                              ALU.subtract).then_inc(step, 1)
            dve.wait_ge(exp_ok, 1)
            dve.tensor_reduce(total[:, :], heads(expd[:, :]), AX.X, ALU.add).then_inc(step, 1)
            dve.wait_ge(step, 16)
            dve.reciprocal(inv_total[:, :], total[:, :]).then_inc(step, 1)
            dve.wait_ge(step, 17)
            dve.tensor_tensor(heads(probs[:, :]), heads(expd[:, :]), per_head(inv_total[:, :]),
                              ALU.mult).then_inc(step, 1)
            dve.wait_ge(made, 5)
            dve.tensor_copy(probs_t[:, :], bank[0][0:SL, :]).then_inc(step, 1)
            dve.wait_ge(made, 6)
            dve.wait_ge(zero_ok, 1)
            outs = bank[1][0:HD, :].rearrange("p (c a s) -> p c a s", a=2, s=SL)
            slots = out_t[:, :, :].rearrange("p (c a) s -> p c a s", a=2)
            for a in range(2):
                dve.tensor_copy(slots[:, :, a, a * SL:(a + 1) * SL], outs[:, :, a, :]).then_inc(step, 1)
            dve.wait_ge(made, 7)
            for n in range(2):
                dve.tensor_copy(m.mixed[:, 2 * n:2 * n + 2, :],
                                bank[2 + n][:, :].rearrange("p (c n) -> p c n", c=2)).then_inc(step, 1)
            dve.wait_ge(step, 23)


def write_output(nc, m):
    iters = m.iters
    weights_dram, x1_dram, out_dram = grouped(m.slice_weights, HS), grouped(m.x1, D), grouped(m.out, D)
    with ExitStack() as ctx:
        sb = lambda n, s, d=F32: ctx.enter_context(nc.sbuf_tensor(n, s, d))
        sem = lambda n: ctx.enter_context(nc.semaphore(n))
        weights = sb("o_weights", [P, 2, SLOTS, HS])
        x1, base, out = (sb(n, [P, 2, SLOTS, D]) for n in ("o_x1", "o_base", "o_out"))
        weights_t = sb("o_weights_t", [P, 2, CH, P])
        turned = [ctx.enter_context(nc.psum_tensor(f"o_turned{i}", [P, CH, P], F32)) for i in range(2)]
        product = [ctx.enter_context(nc.psum_tensor(f"o_product{i}", [P, D], F32)) for i in range(2)]
        rows_in = [sem(f"o_rows_in{b}") for b in range(2)]
        stored = [sem(f"o_stored{b}") for b in range(2)]
        turned_ok, copied, product_ok, base_ok, out_ok = (
            sem("o_" + n) for n in ("turned_ok", "copied", "product_ok", "base_ok", "out_ok"))
        block = ctx.enter_context(nc.Block())

        @block.sync
        def _(sp):
            def load(g, b):
                wait(sp, turned_ok, SLOTS * (g - 1))
                wait(sp, base_ok, SLOTS * (g - 1))
                sp.dma_start(weights[:, b, :, :], one_group(weights_dram, g, HS)).then_inc(rows_in[b], 16)
                sp.dma_start(x1[:, b, :, :], one_group(x1_dram, g, D)).then_inc(rows_in[b], 16)

            def body(it):
                for b in range(2):
                    g = it * 2 + b
                    if not (isinstance(g, int) and g + 2 >= m.ng):
                        load(g + 2, b)
                    sp.wait_ge(out_ok, SLOTS * (g + 1))
                    sp.dma_start(one_group(out_dram, g, D), out[:, b, :, :]).then_inc(stored[b], 16)
            load(0, 0)
            load(1, 1)
            loop(sp, iters, body)
            for b in range(2):
                sp.wait_ge(stored[b], 16 * iters)

        def steps(engine, step):
            def body(it):
                for k in range(2 * SLOTS):
                    step(it, k)
            loop(engine, iters, body)

        @block.tensor
        def _(pe):
            def multiply(t, par):
                pe.wait_ge(copied, t + 1)
                wait(pe, out_ok, t - 1)
                for c in range(CH):
                    done = pe.matmul(product[par][:, :], weights_t[:, par, c, :], m.mixed[:, c, :],
                                     start=c == 0, stop=c == CH - 1)
                done.then_inc(product_ok, 1)

            def step(it, k):
                t = it * 2 * SLOTS + k
                b, j = k // SLOTS, k % SLOTS
                pe.wait_ge(rows_in[b], 32 * (it + 1))
                wait(pe, copied, t - 1)
                for c in range(CH):
                    done = pe.transpose(turned[k % 2][:, c, :], weights[:, b, j, c * P:(c + 1) * P], m.ident[:, :])
                done.then_inc(turned_ok, 1)
                if not (isinstance(t, int) and t == 0):
                    multiply(t - 1, (k - 1) % 2)
            steps(pe, step)
            multiply(m.nt - 1, 1)

        @block.scalar
        def _(act):
            def step(it, k):
                t = it * 2 * SLOTS + k
                act.wait_ge(turned_ok, t + 1)
                wait(act, product_ok, t - 1)
                act.activation(weights_t[:, k % 2, :, :], turned[k % 2][:, :, :], ACT.Copy).then_inc(copied, 1)
            steps(act, step)

        @block.gpsimd
        def _(pool):
            def step(it, k):
                b, j = k // SLOTS, k % SLOTS
                g = it * 2 + b
                if j == 0:
                    pool.wait_ge(rows_in[b], 32 * (it + 1))
                    wait(pool, out_ok, SLOTS * (g - 1))
                pool.tensor_tensor(base[:, b, j, :], x1[:, b, j, :], m.b_out[:, :], ALU.add).then_inc(base_ok, 1)
            steps(pool, step)

        @block.vector
        def _(dve):
            def step(it, k):
                t = it * 2 * SLOTS + k
                b, j = k // SLOTS, k % SLOTS
                dve.wait_ge(product_ok, t + 1)
                dve.wait_ge(base_ok, t + 1)
                if j == 0:
                    wait(dve, stored[b], 16 * it)
                dve.tensor_tensor(out[:, b, j, :], product[k % 2][:, :], base[:, b, j, :], ALU.add
                                  ).then_inc(out_ok, 1)
            steps(dve, step)


def gnn_and_slice_attention(nc, ins, out, n):
    m = Model()
    m.x, m.src_cols, m.dst_cols, m.dst_rows = (ins[k] for k in ("x", "src_cols", "dst_cols", "dst_rows"))
    m.w1, m.b1_dram, m.w2, m.b2_dram = (ins[k] for k in ("w1", "b1_dram", "w2", "b2_dram"))
    m.w_fx_dram, m.b_fx_dram, m.wx_t_dram, m.bx_t_dram = (
        ins[k] for k in ("w_fx_dram", "b_fx_dram", "wx_t_dram", "bx_t_dram"))
    m.w_slice_dram, m.b_slice_dram, m.temp_dram = (ins[k] for k in ("w_slice_dram", "b_slice_dram", "temp_dram"))
    m.w_q_dram, m.w_k_dram, m.w_v_dram = (ins[k] for k in ("w_q_dram", "w_k_dram", "w_v_dram"))
    m.w_out_dram, m.b_out_dram = ins["w_out_dram"], ins["b_out_dram"]
    m.out, m.n, m.np = out, n, padded(n)
    m.nt, m.ng = m.np // P, m.np // GROUP
    m.iters = m.ng // BODY_GROUPS
    assert (n - (m.ng - 1) * GROUP) % SLOTS == 0 and 0 < n - (m.ng - 1) * GROUP
    dram = lambda name, rows, width: nc.dram_tensor(name, [rows, width], F32).ap()
    m.messages = [dram(f"messages{c}", m.np, D) for c in range(2)]
    m.sums = [dram(f"sums{c}", m.np + GROUP, D) for c in range(2)]
    m.x1 = dram("x1", m.np, D)
    m.slice_weights = dram("slice_weights", m.np, HS)
    with ExitStack() as ctx:
        sb = lambda name, s, d=F32: ctx.enter_context(nc.sbuf_tensor(name, s, d))
        m.ident = sb("ident", [P, P])
        m.earlier = sb("earlier", [P, GROUP])
        m.spare = sb("spare", [P, SLOTS])
        m.dst_i, m.src_i, m.dst_f = sb("dst_i", [P, m.nt], I32), sb("src_i", [P, m.nt], I32), sb("dst_f", [P, m.nt])
        m.dinv, m.mean, m.rstd, m.scale, m.shift = (
            sb(name, [P, m.nt]) for name in ("dinv", "mean", "rstd", "scale", "shift"))
        m.b1, m.b2, m.b_out = sb("b1", [P, D]), sb("b2", [P, D]), sb("b_out", [P, D])
        m.w_logit = sb("w_logit", [P, KD, HS])
        m.bias_rows, m.ones3 = sb("bias_rows", [3, HS], BF16), sb("ones3", [3, P], BF16)
        m.y = sb("y", [P, 2, SLOTS, D + 2])
        m.half = sb("half", [P, 2])
        m.mixed = sb("mixed", [P, CH, D])
        m.const_ok, m.pool_passed, m.dve_passed = (
            ctx.enter_context(nc.semaphore(name)) for name in ("const_ok", "pool_passed", "dve_passed"))
        count_degrees(nc, m)
        transform(nc, m, 0)
        add_edges(nc, m, 0)
        transform(nc, m, 1)
        add_edges(nc, m, 1)
        prepare_attention(nc, m)
        m.tokens = [ctx.enter_context(nc.psum_tensor(f"tokens{c}", [P, D + 1], F32)) for c in range(CH)]
        attend_tokens(nc, m)
        mix_tokens(nc, m)
        write_output(nc, m)


def kernel(**inputs):
    import numpy as _np
    import concourse.bacc as _bacc
    from concourse import mybir as _mybir
    from concourse.bass_utils import run_bass_kernel_spmd as _run

    a = {k: _np.asarray(v) for k, v in inputs.items()}
    n = a["x"].shape[0]
    rows = padded(n)
    x = _np.zeros((rows, D), _np.float32)
    x[:n] = a["x"]
    pad = _np.arange(n, rows, dtype=_np.int32)
    src, dst = (_np.concatenate([a[k], pad]) for k in ("src", "dst"))
    columns = lambda e: _np.ascontiguousarray(
        e.reshape(-1, P, SLOTS).transpose(1, 0, 2).reshape(P, -1))
    row = lambda v: _np.ascontiguousarray(v.reshape(1, -1))
    arrays = {
        "x": x,
        "src_cols": columns(src),
        "dst_cols": columns(dst),
        "dst_rows": _np.ascontiguousarray(dst.reshape(-1, P, SLOTS).transpose(0, 2, 1).reshape(-1, GROUP)),
        "w1": a["L0_gnn_W1"], "b1_dram": a["L0_gnn_b1"],
        "w2": a["L0_gnn_W2"], "b2_dram": a["L0_gnn_b2"],
        "w_fx_dram": a["L0_ffn_W_fx"], "b_fx_dram": row(a["L0_ffn_b_fx"]),
        "wx_t_dram": _np.ascontiguousarray(a["L0_ffn_W_x"].T),
        "bx_t_dram": _np.ascontiguousarray(a["L0_ffn_b_x"].reshape(HEADS, HD).T),
        "w_slice_dram": a["L0_ffn_W_slice"], "b_slice_dram": row(a["L0_ffn_b_slice"]),
        "w_q_dram": a["L0_ffn_W_q"], "w_k_dram": a["L0_ffn_W_k"], "w_v_dram": a["L0_ffn_W_v"],
        "w_out_dram": a["L0_ffn_W_out"], "b_out_dram": a["L0_ffn_b_out"],
        "temp_dram": a["L0_ffn_temperature"].reshape(-1),
    }
    nc = _bacc.Bacc("TRN2", target_bir_lowering=False, num_devices=1)
    ins = {k: nc.dram_tensor(f"in_{k}", v.shape, _mybir.dt.from_np(v.dtype), kind="ExternalInput").ap()
           for k, v in arrays.items()}
    out = nc.dram_tensor("out_0", (rows, D), F32, kind="ExternalOutput").ap()
    gnn_and_slice_attention(nc, ins, out, n)
    r = _run(nc, [{f"in_{k}": v for k, v in arrays.items()}], core_ids=[0])
    return r.results[0]["out_0"][:n]
```

```python
from contextlib import ExitStack

import concourse.bass as bass
from concourse import mybir

F32 = mybir.dt.float32
F32R = mybir.dt.float32r
BF16 = mybir.dt.bfloat16
I32 = mybir.dt.int32
ACT = mybir.ActivationFunctionType
ALU = mybir.AluOpType
AX = mybir.AxisListType

P = 128
D = 256
KD = D // P
SLOTS = 4
GROUP = P * SLOTS
HEADS = 8
HD = 64
SL = 64
HS = HEADS * SL
CH = HS // P
LN_EPS = 1e-5
TOKEN_EPS = 1e-5
RING = 4


class Model:
    pass


def padded(n):
    step = GROUP * 2
    return (n + step - 1) // step * step


def wait(engine, semaphore, value):
    if isinstance(value, int) and value <= 0:
        return
    engine.wait_ge(semaphore, value)


def carry(engine, passed):
    engine.sem_inc(passed, 1)


def loop(engine, m, group):
    for b in range(RING):
        group(0, b)
    if m.iters > 3:
        with engine.Fori(1, m.iters - 2) as it:
            for b in range(RING):
                group(it, b)
    for it in range(max(1, m.iters - 2), m.iters):
        for b in range(RING if it < m.iters - 1 else m.last):
            group(it, b)


def slot_uses(m, b):
    return m.iters - (b >= m.last)


def ring_wait(engine, semaphores, it, b, increment, uses_back=0):
    wait(engine, semaphores[b], increment * (it + 1 - uses_back))


def shifted_group(m, it, b, by):
    if isinstance(it, int) and RING * it + b + by >= m.ng:
        return None
    return it + (b + by) // RING, (b + by) % RING


def edge_group(dram, g):
    view = dram[0:dram.shape[0] // GROUP * GROUP, :].rearrange("(g j p) d -> g p j d", p=P, j=SLOTS)
    return view[bass.ds(g, 1), :, :, :].rearrange("g p j d -> p (g j) d")


def grouped(dram, width):
    return dram[0:dram.shape[0] // GROUP * GROUP, :].rearrange(
        "(g p j) d -> g p (j d)", p=P, j=SLOTS)


def one_group(view, g, width):
    return view[bass.ds(g, 1), :, :].rearrange("g p (j d) -> p (g j) d", d=width)


def cleared_semaphores(nc, ctx):
    made = []

    def give_back():
        nc.clear_and_free_semaphores(made)
        nc.all_engine_barrier()
    ctx.callback(give_back)

    def semaphore(name):
        made.append(nc.alloc_semaphore(name))
        return made[-1]
    return semaphore


def count_degrees(nc, m):
    nt, ng = m.nt, m.ng
    no_row = float(m.np)
    ring_tiles = SLOTS * RING
    on_pool = (0, 3, 6, 8, 11, 14)
    with ExitStack() as ctx:
        sb = lambda n, s, d=F32: ctx.enter_context(nc.sbuf_tensor(n, s, d))
        sem = lambda n: ctx.enter_context(nc.semaphore(n))
        ps = lambda n, s: ctx.enter_context(nc.psum_tensor(n, s, F32))
        lo_i, hi_a, hi_b, hi_i, prev_i = (
            sb(n, [P, nt], I32) for n in ("lo_i", "hi_a", "hi_b", "hi_i", "prev_i"))
        lo_f, hi_f = sb("lo_f", [P, nt]), sb("hi_f", [P, nt])
        lo_now = sb("lo_now", [P, 2, SLOTS])
        iota_hi, iota_lo = sb("iota_hi", [P, nt], BF16), sb("iota_lo", [P, P], BF16)
        hot_hi, hot_lo = sb("hot_hi", [P, ring_tiles, nt], BF16), sb("hot_lo", [P, ring_tiles, P], BF16)
        degree, root = sb("degree", [P, nt]), sb("root", [P, nt])
        falls, any_fall = sb("falls", [P, nt]), sb("any_fall", [P, 1])
        order = sb("order", [P, 1])
        cumulated, has_edges = sb("cumulated", [P, nt]), sb("has_edges", [P, nt])
        node_id, row_a, row_b = sb("node_id", [P, nt]), sb("row_a", [P, nt]), sb("row_b", [P, nt])
        scan = [sb(f"scan{i}", [P, ng]) for i in range(2)]
        group_base, first_row = sb("group_base", [P, ng]), sb("first_row", [P, ng])
        before, ones = sb("before", [P, P]), sb("ones", [P, P])
        zeros = sb("zeros", [P, SLOTS * D])
        counts = ps("counts", [P, nt])
        in_group, of_group, n_falls = ps("in_group", [P, ng]), ps("of_group", [P, ng]), ps("n_falls", [P, 1])
        dst_in, prev_in, rows_in, zeroed = sem("dst_in"), sem("prev_in"), sem("rows_in"), sem("zeroed")
        consts, split, digits, picked = sem("consts"), sem("split"), sem("digits"), sem("picked")
        lo_copied, hi_hot, lo_hot, lo_hot_pool, counted = (
            sem(n) for n in ("lo_copied", "hi_hot", "lo_hot", "lo_hot_pool", "counted"))
        degree_ok, rooted, linked, summed = sem("degree_ok"), sem("rooted"), sem("linked"), sem("summed")
        block = ctx.enter_context(nc.Block())
        by_slot = lambda a: a[:, :].rearrange("p (g j) -> p g j", j=SLOTS)

        @block.sync
        def _(sp):
            sp.dma_start(m.dst_i[:, :], m.dst_cols).then_inc(dst_in, 16)
            sp.dma_start(prev_i[:, :], m.prev_cols).then_inc(prev_in, 16)
            sp.dma_start(m.src_i[:, :], m.src_cols).then_inc(rows_in, 16)
            sp.dma_start(m.b1[:, :], m.b1_dram.partition_broadcast(P)).then_inc(rows_in, 16)
            sp.dma_start(m.b2[:, :], m.b2_dram.partition_broadcast(P)).then_inc(rows_in, 16)
            sp.dma_start(m.b_out[:, :], m.b_out_dram.partition_broadcast(P)).then_inc(rows_in, 16)
            sp.wait_ge(zeroed, 1)
            for table in m.table:
                sp.dma_start(table[m.np:m.np + GROUP, :].rearrange("(p j) d -> p (j d)", j=SLOTS),
                             zeros[:, :]).then_inc(rows_in, 16)
            sp.wait_ge(rows_in, 96)

        @block.gpsimd
        def _(pool):
            pool.iota(iota_hi[:, :], [[1, nt]], base=-(nt // 2), channel_multiplier=0,
                      allow_small_or_imprecise_dtypes=True).then_inc(consts, 1)
            pool.iota(iota_lo[:, :], [[1, P]], base=0, channel_multiplier=0,
                      allow_small_or_imprecise_dtypes=True).then_inc(consts, 1)
            pool.memset(zeros[:, :], 0.0).then_inc(zeroed, 1)
            pool.memset(m.ident[:, :], 0.0).then_inc(consts, 1)
            pool.memset(m.earlier[:, :], 1.0).then_inc(consts, 1)
            pool.memset(before[:, :], 1.0).then_inc(consts, 1)
            pool.memset(ones[:, :], 1.0).then_inc(consts, 1)
            pool.iota(m.spare[:, :], [[1, SLOTS]], base=m.np, channel_multiplier=SLOTS,
                      allow_small_or_imprecise_dtypes=True).then_inc(consts, 1)
            pool.iota(node_id[:, :], [[GROUP, ng], [1, SLOTS]], base=0, channel_multiplier=SLOTS,
                      allow_small_or_imprecise_dtypes=True).then_inc(consts, 1)
            pool.wait_ge(consts, 8)
            pool.affine_select(out=m.ident[:, :], in_=m.ident[:, :], compare_op=ALU.not_equal,
                               fill=1.0, base=0, pattern=[[-1, P]], channel_multiplier=1).then_inc(consts, 1)
            last = m.earlier[:, (SLOTS - 1) * P:]
            pool.affine_select(out=last, in_=last, compare_op=ALU.is_gt, fill=0.0, base=0,
                               pattern=[[-1, P]], channel_multiplier=1).then_inc(consts, 1)
            pool.affine_select(out=before[:, :], in_=before[:, :], compare_op=ALU.is_gt, fill=0.0, base=0,
                               pattern=[[1, P]], channel_multiplier=-1).then_inc(consts, 1)
            pool.wait_ge(picked, 2)
            pool.affine_select(out=m.prev_last[:, :], in_=m.prev_last[:, :], compare_op=ALU.is_ge, fill=-1.0,
                               base=-(P - 1), pattern=[[0, nt]], channel_multiplier=1).then_inc(consts, 1)
            pool.wait_ge(digits, 2)

            def group(it, b):
                g = RING * it + b
                mine = [j for j in range(SLOTS) if b * SLOTS + j in on_pool]
                per_ring = len(on_pool)
                done_before = len([k for k in on_pool if k < b * SLOTS])
                back = len([k for k in on_pool if (b - 1) * SLOTS <= k < b * SLOTS]) if b else len(
                    [k for k in on_pool if k >= (RING - 1) * SLOTS])
                wait(pool, lo_hot_pool, it * per_ring + done_before - back)
                pool.tensor_copy(lo_now[:, b % 2, :], lo_f[:, bass.ds(g * SLOTS, SLOTS)]).then_inc(lo_copied, 1)
                pool.wait_ge(lo_copied, g + 1)
                for j in mine:
                    wait(pool, counted, g * SLOTS + j - ring_tiles + 1)
                    carry(pool, m.pool_passed)
                    pool.tensor_scalar(hot_lo[:, b * SLOTS + j, :], iota_lo[:, :], lo_now[:, b % 2, j:j + 1],
                                       None, ALU.is_equal).then_inc(lo_hot_pool, 1)
            loop(pool, m, group)

        @block.vector
        def _(dve):
            dve.wait_ge(dst_in, 16)
            dve.tensor_scalar(lo_i[:, :], m.dst_i[:, :], 2, P - 1, ALU.logical_shift_right,
                              ALU.bitwise_and).then_inc(split, 1)
            dve.tensor_scalar(hi_a[:, :], m.dst_i[:, :], 9, 2, ALU.logical_shift_right,
                              ALU.logical_shift_left).then_inc(split, 1)
            dve.tensor_scalar(hi_b[:, :], m.dst_i[:, :], SLOTS - 1, None, ALU.bitwise_and).then_inc(split, 1)
            dve.tensor_copy(m.dst_f[:, :], m.dst_i[:, :]).then_inc(split, 1)
            dve.wait_ge(split, 4)
            dve.tensor_copy(lo_f[:, :], lo_i[:, :]).then_inc(digits, 1)
            dve.tensor_tensor(hi_i[:, :], hi_a[:, :], hi_b[:, :], ALU.bitwise_or).then_inc(split, 1)
            dve.tensor_copy(m.prev_last[:, 1:nt], m.dst_f[:, 0:nt - 1]).then_inc(picked, 1)
            dve.memset(m.prev_last[:, 0:1], -1.0).then_inc(picked, 1)
            dve.wait_ge(split, 5)
            dve.tensor_scalar(hi_f[:, :], hi_i[:, :], float(-(nt // 2)), None, ALU.add).then_inc(digits, 1)
            dve.wait_ge(digits, 2)
            dve.wait_ge(consts, 2)

            def group(it, b):
                g = RING * it + b
                for j in range(SLOTS):
                    t = g * SLOTS + j
                    wait(dve, counted, t - ring_tiles + 1)
                    dve.tensor_scalar(hot_hi[:, b * SLOTS + j, :], iota_hi[:, :], hi_f[:, bass.ds(t, 1)], None,
                                      ALU.is_equal).then_inc(hi_hot, 1)
                    if b * SLOTS + j not in on_pool:
                        dve.tensor_scalar(hot_lo[:, b * SLOTS + j, :], iota_lo[:, :], lo_f[:, bass.ds(t, 1)],
                                          None, ALU.is_equal).then_inc(lo_hot, 1)
            loop(dve, m, group)

            links = [0]

            def link(done):
                links[0] += 1
                done.then_inc(linked, 1)
                dve.wait_ge(linked, links[0])

            dve.wait_ge(prev_in, 16)
            link(dve.tensor_tensor(falls[:, :], prev_i[:, :], m.dst_i[:, :], ALU.is_gt))
            link(dve.tensor_reduce(any_fall[:, :], falls[:, :], AX.X, ALU.max))
            dve.sem_inc(summed, 1)
            dve.wait_ge(counted, nt)
            dve.tensor_scalar(degree[:, :], counts[:, :], 1.0, 1e-12, ALU.add, ALU.max).then_inc(degree_ok, 1)
            link(dve.tensor_copy(cumulated[:, :], counts[:, :]))
            link(dve.tensor_scalar(has_edges[:, :], cumulated[:, :], 1.0, None, ALU.min))
            for j in range(1, SLOTS):
                link(dve.tensor_tensor(by_slot(cumulated)[:, :, j], by_slot(cumulated)[:, :, j],
                                       by_slot(cumulated)[:, :, j - 1], ALU.add))
            dve.sem_inc(summed, 1)
            dve.wait_ge(summed, 3)
            link(dve.tensor_copy(scan[0][:, :], of_group[:, :]))
            at, reach = 0, 1
            while reach < ng:
                link(dve.tensor_copy(scan[1 - at][:, 0:reach], scan[at][:, 0:reach]))
                link(dve.tensor_tensor(scan[1 - at][:, reach:ng], scan[at][:, reach:ng],
                                       scan[at][:, 0:ng - reach], ALU.add))
                at, reach = 1 - at, 2 * reach
            link(dve.tensor_tensor(group_base[:, :], scan[at][:, :], of_group[:, :], ALU.subtract))
            link(dve.tensor_tensor(first_row[:, :], group_base[:, :], in_group[:, :], ALU.add))
            link(dve.tensor_tensor(by_slot(row_a), by_slot(cumulated),
                                   first_row[:, :, None].to_broadcast([P, ng, SLOTS]), ALU.add))
            link(dve.scalar_tensor_tensor(row_b[:, :], row_a[:, :], -1.0 - no_row, has_edges[:, :],
                                          ALU.add, ALU.mult))
            link(dve.tensor_scalar(order[:, :], n_falls[:, :], 0.0, None, ALU.is_equal))
            link(dve.tensor_copy(m.in_order[:, :], order[0:1, :]))
            link(dve.scalar_tensor_tensor(row_a[:, :], row_b[:, :], no_row, node_id[:, :], ALU.add, ALU.subtract))
            link(dve.scalar_tensor_tensor(m.node_row[:, :], row_a[:, :], order[:, :], node_id[:, :],
                                          ALU.mult, ALU.add))
            dve.wait_ge(rooted, 1)
            link(dve.reciprocal(m.dinv[:, :], root[:, :]))

        @block.scalar
        def _(act):
            act.wait_ge(degree_ok, 1)
            act.activation(root[:, :], degree[:, :], ACT.Sqrt).then_inc(rooted, 1)

        @block.tensor
        def _(pe):
            def group(it, b):
                g = RING * it + b
                dve_slots = [k for k in range(ring_tiles) if k not in on_pool]
                for j in range(SLOTS):
                    t, k = g * SLOTS + j, b * SLOTS + j
                    pe.wait_ge(hi_hot, t + 1)
                    slots, ready = (on_pool, lo_hot_pool) if k in on_pool else (dve_slots, lo_hot)
                    pe.wait_ge(ready, it * len(slots) + len([n for n in slots if n <= k]))
                    pe.matmul(counts[:, :], hot_lo[:, k, :], hot_hi[:, k, :],
                              start=isinstance(t, int) and t == 0,
                              stop=isinstance(t, int) and t == nt - 1).then_inc(counted, 1)
            loop(pe, m, group)
            pe.wait_ge(consts, 11)
            pe.wait_ge(summed, 2)
            edges = by_slot(cumulated)[:, :, SLOTS - 1]
            pe.matmul(n_falls[:, :], ones[:, :], any_fall[:, :], start=True, stop=True)
            pe.matmul(in_group[:, :], before[:, :], edges, start=True, stop=True)
            pe.matmul(of_group[:, :], ones[:, :], edges, start=True, stop=True).then_inc(summed, 1)


def transform(nc, m, conv):
    source = grouped(m.x if conv == 0 else m.messages[0], D)
    message_rows, base_rows = grouped(m.messages[conv], D), grouped(m.base, D)
    weights = m.w1 if conv == 0 else m.w2
    with ExitStack() as ctx:
        sb = lambda n, s, d=F32: ctx.enter_context(nc.sbuf_tensor(f"{n}{conv}", s, d))
        new_semaphore = cleared_semaphores(nc, ctx)
        sem = lambda n: new_semaphore(f"{n}{conv}")
        ps = lambda n, s: ctx.enter_context(nc.psum_tensor(f"{n}{conv}", s, F32))
        w = sb("w", [P, KD, D])
        w_hi, w_lo = sb("w_hi", [P, KD, D], F32R), sb("w_lo", [P, KD, D], F32R)
        rows = sb("rows", [P, RING, SLOTS, D])
        cent = sb("cent", [P, 2, SLOTS, D])
        hi, lo = sb("hi", [P, 2, 2, KD, P], F32R), sb("lo", [P, 2, 2, KD, P], F32R)
        out = sb("out", [P, RING, SLOTS, D])
        stats = sb("stats", [P, 2, SLOTS, 6])
        mean_var = sb("mean_var", [P, 2, SLOTS, 2])
        var = sb("var", [P, 2, SLOTS])
        root = sb("root_r", [P, 2, SLOTS])
        safe = sb("safe", [P, 2, SLOTS])
        inverse = sb("inverse", [P, 2, SLOTS])
        factor = sb("factor", [P, 2, SLOTS])
        turned = ps("turned", [P, 2, 2, KD, P])
        product = ps("product", [P, 2, 2, D])
        if conv == 0:
            base = sb("base_now", [P, RING, SLOTS, D])
            scale, shift = sb("scale", [P, 2, SLOTS]), sb("shift", [P, 2, SLOTS])
            scale_ok, scaled, base_ok = sem("scale_ok"), sem("scaled"), sem("base_ok")
            base_stored = [sem(f"base_stored{b}_") for b in range(RING)]
        else:
            found = sb("found", [P, RING, SLOTS, D])
            both = sb("both", [P, 2, SLOTS, D])
            row_now = sb("row_now", [P, RING, SLOTS], I32)
            squares = sb("squares", [P, D])
            found_in = [sem(f"found_in{b}_") for b in range(RING)]
            row_ok, both_ok, made_safe, squared = sem("row_ok"), sem("both_ok"), sem("made_safe"), sem("squared")
        w_in, w_split = sem("w_in"), sem("w_split")
        rows_in = [sem(f"rows_in{b}_") for b in range(RING)]
        stored = [sem(f"stored{b}_") for b in range(RING)]
        stats_ok, mean_ok, var_ok, cent_ok = sem("stats_ok"), sem("mean_ok"), sem("var_ok"), sem("cent_ok")
        rooted, inverted, factor_ok = sem("rooted"), sem("inverted"), sem("factor_ok")
        turned_ok, hi_ok, lo_ok, product_ok, out_ok = (
            sem(n) for n in ("turned_ok", "hi_ok", "lo_ok", "product_ok", "out_ok"))
        block = ctx.enter_context(nc.Block())

        @block.sync
        def _(sp):
            sp.dma_start(w[:, :, :], weights.rearrange("(k p) n -> p k n", p=P)).then_inc(w_in, 16)

            def load(g, b):
                if conv == 0:
                    wait(sp, scaled, SLOTS * (g - RING + 1))
                else:
                    wait(sp, both_ok, SLOTS * (g - RING + 1))
                sp.dma_start(rows[:, b, :, :], one_group(source, g, D)).then_inc(rows_in[b], 16)

            def group(it, b):
                g = RING * it + b
                later = shifted_group(m, it, b, RING - 1)
                if later is not None:
                    load(g + RING - 1, later[1])
                if conv == 0:
                    sp.wait_ge(base_ok, SLOTS * (g + 1))
                    sp.dma_start(one_group(base_rows, g, D), base[:, b, :, :]).then_inc(base_stored[b], 16)
                sp.wait_ge(out_ok, 2 * g + 2)
                sp.dma_start(one_group(message_rows, g, D), out[:, b, :, :]).then_inc(stored[b], 16)
            for g in range(RING - 1):
                load(g, g)
            loop(sp, m, group)
            for b in range(RING):
                sp.wait_ge(stored[b], 16 * slot_uses(m, b))
                if conv == 0:
                    sp.wait_ge(base_stored[b], 16 * slot_uses(m, b))

        @block.vector
        def _(dve):
            dve.wait_ge(w_in, 16)
            dve.tensor_copy(w_hi[:, :, :], w[:, :, :]).then_inc(w_split, 1)
            dve.wait_ge(w_split, 1)
            dve.tensor_tensor(w_lo[:, :, :], w[:, :, :], w_hi[:, :, :].bitcast(F32), ALU.subtract
                              ).then_inc(w_split, 1)

            def rest_of(u, k):
                dve.wait_ge(hi_ok, u + 1)
                wait(dve, product_ok, u - 1)
                dve.tensor_tensor(lo[:, k % 2, :, :, :], turned[:, k % 2, :, :, :],
                                  hi[:, k % 2, :, :, :].bitcast(F32), ALU.subtract).then_inc(lo_ok, 1)

            def layernorm(it, b):
                g, c = RING * it + b, b % 2
                cols = bass.ds(g * SLOTS, SLOTS)
                ring_wait(dve, rows_in, it, b, 16)
                for j in range(SLOTS):
                    dve.bn_stats(stats[:, c, j, :], rows[:, b, j, :]).then_inc(stats_ok, 1)
                dve.wait_ge(stats_ok, SLOTS * (g + 1))
                carry(dve, m.dve_passed)
                for j in range(SLOTS):
                    dve.bn_aggr(mean_var[:, c, j, :], stats[:, c, j, :]).then_inc(mean_ok, 1)
                dve.wait_ge(mean_ok, SLOTS * (g + 1))
                dve.tensor_scalar(var[:, c, :], mean_var[:, c, :, 1], LN_EPS, None, ALU.add).then_inc(var_ok, 1)
                wait(dve, turned_ok, 2 * (g - 1))
                for j in range(SLOTS):
                    dve.tensor_scalar(cent[:, c, j, :], rows[:, b, j, :], mean_var[:, c, j, 0:1], None,
                                      ALU.subtract).then_inc(cent_ok, 1)
                dve.wait_ge(rooted, g + 1)
                dve.reciprocal(inverse[:, c, :], root[:, c, :]).then_inc(inverted, 1)
                dve.wait_ge(inverted, g + 1)
                dve.tensor_tensor(factor[:, c, :], inverse[:, c, :], m.dinv[:, cols], ALU.mult
                                  ).then_inc(factor_ok, 1)
                wait(dve, scaled, SLOTS * (g - 1))
                dve.tensor_scalar(scale[:, c, :], inverse[:, c, :], 1.0, None, ALU.add).then_inc(scale_ok, 1)
                dve.scalar_tensor_tensor(shift[:, c, :], mean_var[:, c, :, 0], -1.0, inverse[:, c, :],
                                         ALU.mult, ALU.mult).then_inc(scale_ok, 1)

            def normalise(it, b):
                g, c = RING * it + b, b % 2
                cols = bass.ds(g * SLOTS, SLOTS)
                wait(dve, turned_ok, 2 * (g - 1))
                wait(dve, rooted, g - 1)
                for j in range(SLOTS):
                    dve.wait_ge(both_ok, g * SLOTS + j + 1)
                    dve.scalar_tensor_tensor(cent[:, c, j, :], both[:, c, j, :],
                                             m.dinv[:, bass.ds(g * SLOTS + j, 1)], m.b1[:, :],
                                             ALU.mult, ALU.add).then_inc(cent_ok, 1)
                dve.wait_ge(rooted, g + 1)
                dve.tensor_scalar(safe[:, c, :], root[:, c, :], 1e-12, None, ALU.max).then_inc(made_safe, 1)
                dve.wait_ge(made_safe, g + 1)
                dve.reciprocal(inverse[:, c, :], safe[:, c, :]).then_inc(inverted, 1)
                dve.wait_ge(inverted, g + 1)
                dve.tensor_tensor(factor[:, c, :], inverse[:, c, :], m.dinv[:, cols], ALU.mult
                                  ).then_inc(factor_ok, 1)

            def add_found(it, b):
                g, c = RING * it + b, b % 2
                ring_wait(dve, rows_in, it, b, 16)
                ring_wait(dve, found_in, it, b, 64)
                wait(dve, cent_ok, SLOTS * (g - 1))
                for j in range(SLOTS):
                    dve.tensor_tensor(both[:, c, j, :], rows[:, b, j, :], found[:, b, j, :], ALU.add
                                      ).then_inc(both_ok, 1)

            def rows_of(it, b):
                ring_wait(dve, found_in, it, b, 64, uses_back=1)
                dve.tensor_copy(row_now[:, b, :], m.node_row[:, bass.ds((RING * it + b) * SLOTS, SLOTS)]
                                ).then_inc(row_ok, 1)

            def group(it, b):
                g = RING * it + b
                later = shifted_group(m, it, b, 1)
                if conv == 1:
                    ahead = shifted_group(m, it, b, 3)
                    if ahead is not None:
                        rows_of(*ahead)
                rest_of(2 * g, 0)
                if later is not None:
                    if conv == 0:
                        layernorm(*later)
                    else:
                        add_found(*later)
                        normalise(*later)
                rest_of(2 * g + 1, 1)

            if conv == 0:
                layernorm(0, 0)
            else:
                for i in range(3):
                    rows_of(0, i)
                add_found(0, 0)
                normalise(0, 0)
            loop(dve, m, group)

        @block.gpsimd
        def _(pool):
            if conv == 0:
                def group(it, b):
                    g = RING * it + b
                    for j in range(SLOTS):
                        pool.wait_ge(scaled, g * SLOTS + j + 1)
                        pool.tensor_tensor(base[:, b, j, :], base[:, b, j, :], m.b2[:, :], ALU.add
                                           ).then_inc(base_ok, 1)
                loop(pool, m, group)
                return

            def group(it, b):
                g = RING * it + b
                pool.wait_ge(row_ok, g + 1)
                wait(pool, both_ok, SLOTS * (g - RING + 1))
                carry(pool, m.pool_passed)
                for j in range(SLOTS):
                    pool.indirect_dma_start(
                        out=found[:, b, j, :], out_offset=None, in_=m.table[0],
                        in_offset=bass.IndirectOffsetOnAxis(ap=row_now[:, b, j:j + 1], axis=0)
                    ).then_inc(found_in[b], 16)
            loop(pool, m, group)

        @block.scalar
        def _(act):
            def roots(it, b):
                g, c = RING * it + b, b % 2
                if conv == 0:
                    act.wait_ge(var_ok, g + 1)
                    act.activation(root[:, c, :], var[:, c, :], ACT.Sqrt).then_inc(rooted, 1)
                    return
                for j in range(SLOTS):
                    act.wait_ge(cent_ok, SLOTS * g + j + 1)
                    wait(act, squared, SLOTS * g + j)
                    act.activation(squares[:, :], cent[:, c, j, :], ACT.Square,
                                   accum_out=var[:, c, j:j + 1]).then_inc(squared, 1)
                act.wait_ge(squared, SLOTS * (g + 1))
                act.activation(root[:, c, :], var[:, c, :], ACT.Sqrt).then_inc(rooted, 1)

            def make_base(it, b):
                g, c = RING * it + b, b % 2
                act.wait_ge(scale_ok, 2 * (g + 1))
                ring_wait(act, base_stored, it, b, 16, uses_back=1)
                for j in range(SLOTS):
                    act.activation(base[:, b, j, :], rows[:, b, j, :], ACT.Identity,
                                   bias=shift[:, c, j:j + 1], scale=scale[:, c, j:j + 1]).then_inc(scaled, 1)

            def copy_turned(u, k):
                act.wait_ge(turned_ok, u + 1)
                wait(act, product_ok, u - 1)
                act.activation(hi[:, k % 2, :, :, :], turned[:, k % 2, :, :, :], ACT.Copy).then_inc(hi_ok, 1)

            def scale_product(it, b, h):
                g, c = RING * it + b, b % 2
                act.wait_ge(product_ok, 2 * g + h + 1)
                if h == 0:
                    act.wait_ge(factor_ok, g + 1)
                    ring_wait(act, stored, it, b, 16, uses_back=1)
                for j in (2 * h, 2 * h + 1):
                    done = act.activation(out[:, b, j, :], product[:, h, j % 2, :], ACT.Copy,
                                          scale=factor[:, c, j:j + 1])
                done.then_inc(out_ok, 1)

            def group(it, b):
                g = RING * it + b
                copy_turned(2 * g, 0)
                back = (it, b - 1) if b else (it - 1, RING - 1)
                if not (isinstance(g, int) and g == 0):
                    scale_product(*back, 1)
                later = shifted_group(m, it, b, 1)
                if later is not None:
                    roots(*later)
                copy_turned(2 * g + 1, 1)
                if conv == 0:
                    make_base(it, b)
                scale_product(it, b, 0)
            roots(0, 0)
            loop(act, m, group)
            scale_product(m.iters - 1, m.last - 1, 1)

        @block.tensor
        def _(pe):
            pe.wait_ge(w_split, 2)

            def turn(u, b, h):
                pe.wait_ge(cent_ok, 2 * u + 2)
                wait(pe, lo_ok, u - 1)
                for i in range(2):
                    for c in range(KD):
                        done = pe.transpose(turned[:, h, i, c, :],
                                            cent[:, b % 2, 2 * h + i, c * P:(c + 1) * P], m.ident[:, :])
                done.then_inc(turned_ok, 1)

            def multiply(u, h):
                pe.wait_ge(hi_ok, u + 1)
                wait(pe, out_ok, u - 1)
                for i in range(2):
                    for c in range(KD):
                        pe.matmul(product[:, h, i, :], hi[:, h, i, c, :], w_hi[:, c, :], start=c == 0, stop=False)
                        pe.matmul(product[:, h, i, :], hi[:, h, i, c, :], w_lo[:, c, :], start=False, stop=False)
                    if i == 0:
                        pe.wait_ge(lo_ok, u + 1)
                    for c in range(KD):
                        done = pe.matmul(product[:, h, i, :], lo[:, h, i, c, :], w_hi[:, c, :],
                                         start=False, stop=c == KD - 1)
                done.then_inc(product_ok, 1)

            def group(it, b):
                g = RING * it + b
                turn(2 * g, b, 0)
                if not (isinstance(g, int) and g == 0):
                    multiply(2 * g - 1, 1)
                turn(2 * g + 1, b, 1)
                multiply(2 * g, 0)
            loop(pe, m, group)
            multiply(2 * m.ng - 1, 1)


def sum_edges(nc, m, conv):
    in_order = nc.values_load(m.in_order[0:1, 0:1], min_val=0, max_val=1)
    with nc.If(in_order == 1):
        sum_sorted_edges(nc, m, conv)
    with nc.Else():
        sum_any_edges(nc, m, conv)


def sum_sorted_edges(nc, m, conv):
    messages, table = m.messages[conv], m.table[conv]
    with ExitStack() as ctx:
        sb = lambda n, s, d=F32: ctx.enter_context(nc.sbuf_tensor(f"s_{n}{conv}", s, d))
        new_semaphore = cleared_semaphores(nc, ctx)
        sem = lambda n: new_semaphore(f"s_{n}{conv}")
        dst_row = sb("dst_row", [P, RING, GROUP], I32)
        same = sb("same", [P, 2, SLOTS, P])
        same_as_last = sb("same_as_last", [P, 2, SLOTS, P])
        src_now = sb("src_now", [P, RING, SLOTS], I32)
        got = sb("got", [P, RING, SLOTS, D])
        merged = sb("merged", [P, RING, SLOTS, D])
        total = [ctx.enter_context(nc.psum_tensor(f"s_total{i}_{conv}", [P, D], F32)) for i in range(SLOTS)]
        row_in = [sem(f"row_in{b}_") for b in range(RING)]
        gathered = [sem(f"gathered{b}_") for b in range(RING)]
        stored = [sem(f"stored{b}_") for b in range(RING)]
        src_ok, same_ok, total_ok, merged_ok = (sem(n) for n in ("src_ok", "same_ok", "total_ok", "merged_ok"))
        block = ctx.enter_context(nc.Block())

        @block.sync
        def _(sp):
            def load(g, b):
                wait(sp, same_ok, 2 * SLOTS * (g - RING + 1))
                sp.dma_start(dst_row[:, b, :], m.dst_rows[bass.ds(g, 1), :].to_broadcast([P, GROUP])
                             ).then_inc(row_in[b], 16)

            def group(it, b):
                g = RING * it + b
                later = shifted_group(m, it, b, RING - 1)
                if later is not None:
                    load(g + RING - 1, later[1])
                sp.wait_ge(merged_ok, SLOTS * (g + 1))
                sp.dma_start(edge_group(table, g), merged[:, b, :, :]).then_inc(stored[b], 16)
            for g in range(RING - 1):
                load(g, g)
            loop(sp, m, group)
            for b in range(RING):
                sp.wait_ge(stored[b], 16 * slot_uses(m, b))

        @block.vector
        def _(dve):
            def sources(it, b):
                ring_wait(dve, gathered, it, b, 64, uses_back=1)
                dve.tensor_copy(src_now[:, b, :], m.src_i[:, bass.ds((RING * it + b) * SLOTS, SLOTS)]
                                ).then_inc(src_ok, 1)

            def group(it, b):
                g, c = RING * it + b, b % 2
                ahead = shifted_group(m, it, b, 3)
                if ahead is not None:
                    sources(*ahead)
                ring_wait(dve, row_in, it, b, 16)
                wait(dve, total_ok, SLOTS * (g - 1))
                for j in range(SLOTS):
                    col = bass.ds(g * SLOTS + j, 1)
                    for to, of in ((same, m.dst_f), (same_as_last, m.prev_last)):
                        dve.tensor_scalar(to[:, c, j, :], dst_row[:, b, j * P:(j + 1) * P], of[:, col], None,
                                          ALU.is_equal).then_inc(same_ok, 1)
            for i in range(3):
                sources(0, i)
            loop(dve, m, group)

        @block.gpsimd
        def _(pool):
            def group(it, b):
                g = RING * it + b
                pool.wait_ge(src_ok, g + 1)
                wait(pool, total_ok, SLOTS * (g - RING + 1))
                carry(pool, m.pool_passed)
                for j in range(SLOTS):
                    pool.indirect_dma_start(
                        out=got[:, b, j, :], out_offset=None, in_=messages,
                        in_offset=bass.IndirectOffsetOnAxis(ap=src_now[:, b, j:j + 1], axis=0)
                    ).then_inc(gathered[b], 16)
            loop(pool, m, group)

        @block.tensor
        def _(pe):
            def own(it, b, j):
                g = RING * it + b
                t = g * SLOTS + j
                if j == 0:
                    ring_wait(pe, gathered, it, b, 64)
                pe.wait_ge(same_ok, 2 * t + 2)
                wait(pe, merged_ok, t - SLOTS + 1)
                first = isinstance(t, int) and t == 0
                done = pe.matmul(total[j][:, :], same[:, b % 2, j, :], got[:, b, j, :], start=True, stop=first)
                if first:
                    done.then_inc(total_ok, 1)

            def carried(it, b, j):
                t = (RING * it + b) * SLOTS + j
                if isinstance(t, int) and t == 0:
                    return
                pe.wait_ge(merged_ok, t)
                before = merged[:, b, j - 1, :] if j else merged[:, (b - 1) % RING, SLOTS - 1, :]
                pe.matmul(total[j][:, :], same_as_last[:, b % 2, j, :], before, start=False, stop=True
                          ).then_inc(total_ok, 1)

            def group(it, b):
                for j in range(SLOTS):
                    if j + 1 < SLOTS:
                        own(it, b, j + 1)
                    else:
                        later = shifted_group(m, it, b, 1)
                        if later is not None:
                            own(*later, 0)
                    carried(it, b, j)
            own(0, 0, 0)
            loop(pe, m, group)

        @block.scalar
        def _(act):
            def group(it, b):
                ring_wait(act, stored, it, b, 16, uses_back=1)
                for j in range(SLOTS):
                    t = (RING * it + b) * SLOTS + j
                    act.wait_ge(total_ok, t + 1)
                    act.activation(merged[:, b, j, :], total[j][:, :], ACT.Copy).then_inc(merged_ok, 1)
            loop(act, m, group)


def sum_any_edges(nc, m, conv):
    first_block = [0, 1, 3, 6]
    messages, table = m.messages[conv], m.table[conv]
    table_rows = grouped(table, D)
    with ExitStack() as ctx:
        sb = lambda n, s, d=F32: ctx.enter_context(nc.sbuf_tensor(f"{n}{conv}", s, d))
        new_semaphore = cleared_semaphores(nc, ctx)
        sem = lambda n: new_semaphore(f"{n}{conv}")
        zeros = sb("any_zeros", [P, SLOTS, D])
        dst_row = sb("dst_row", [P, 2, GROUP], I32)
        same = sb("same", [P, 2, 10, P])
        seen = sb("seen", [P, SLOTS, GROUP])
        n_before = sb("n_before", [P, 2, SLOTS])
        not_owner = sb("not_owner", [P, 2, SLOTS])
        to_spare = sb("to_spare", [P, 2, SLOTS])
        moved = sb("moved", [P, 2, SLOTS])
        target = sb("target", [P, 2, SLOTS], I32)
        src_now = sb("src_now", [P, 2, SLOTS], I32)
        got = sb("got", [P, 2, SLOTS, D])
        merged = sb("merged", [P, 2, SLOTS, D])
        total = ctx.enter_context(nc.psum_tensor(f"total{conv}", [P, 2, SLOTS, D], F32))
        row_in = [sem(f"row_in{b}_") for b in range(2)]
        gathered = [sem(f"gathered{b}_") for b in range(2)]
        added = [sem(f"added{b}_") for b in range(2)]
        src_ok, same_ok, before_ok, spare_ok, moved_ok, target_ok = (
            sem(n) for n in ("src_ok", "same_ok", "before_ok", "spare_ok", "moved_ok", "target_ok"))
        total_ok, merged_ok, zeroed, cleared = sem("total_ok"), sem("merged_ok"), sem("any_zeroed"), sem("cleared")
        block = ctx.enter_context(nc.Block())

        def pairs(engine, pair):
            for b in range(2):
                pair(0, b)
            if m.ng > 4:
                with engine.Fori(1, m.ng // 2 - 1) as i:
                    for b in range(2):
                        pair(i, b)
            for b in range(2):
                pair(m.ng // 2 - 1, b)

        @block.sync
        def _(sp):
            sp.wait_ge(zeroed, 1)
            with sp.Fori(0, m.ng) as g:
                sp.dma_start(one_group(table_rows, g, D), zeros[:, :, :]).then_inc(cleared, 16)

            def pair(i, b):
                g = i * 2 + b
                wait(sp, before_ok, SLOTS * (g - 1))
                sp.dma_start(dst_row[:, b, :], m.dst_rows[bass.ds(g, 1), :].to_broadcast([P, GROUP])
                             ).then_inc(row_in[b], 16)
            pairs(sp, pair)

        @block.vector
        def _(dve):
            def pair(i, b):
                g = i * 2 + b
                cols = bass.ds(g * SLOTS, SLOTS)
                wait(dve, gathered[b], 64 * i)
                dve.tensor_copy(src_now[:, b, :], m.src_i[:, cols]).then_inc(src_ok, 1)
                dve.wait_ge(row_in[b], 16 * (i + 1))
                wait(dve, total_ok, 2 * (g - 1))
                for q in range(SLOTS):
                    f = first_block[q]
                    dve.tensor_scalar(same[:, b, f:f + q + 1, :], dst_row[:, b, 0:(q + 1) * P],
                                      m.dst_f[:, bass.ds(g * SLOTS + q, 1)], None, ALU.is_equal
                                      ).then_inc(same_ok, 1)
                wait(dve, moved_ok, g - 1)
                for q in range(SLOTS):
                    dve.scalar_tensor_tensor(
                        seen[:, q, 0:(q + 1) * P], dst_row[:, b, 0:(q + 1) * P],
                        m.dst_f[:, bass.ds(g * SLOTS + q, 1)],
                        m.earlier[:, (SLOTS - 1 - q) * P:], ALU.is_equal, ALU.mult,
                        accum_out=n_before[:, b, q:q + 1]).then_inc(before_ok, 1)
                dve.tensor_tensor(to_spare[:, b, :], m.spare[:, :], m.dst_f[:, cols], ALU.subtract
                                  ).then_inc(spare_ok, 1)
                dve.wait_ge(before_ok, SLOTS * (g + 1))
                dve.tensor_scalar(not_owner[:, b, :], n_before[:, b, :], 1.0, None, ALU.min
                                  ).then_inc(spare_ok, 1)
                dve.wait_ge(spare_ok, 2 * (g + 1))
                dve.tensor_tensor(moved[:, b, :], not_owner[:, b, :], to_spare[:, b, :], ALU.mult
                                  ).then_inc(moved_ok, 1)
                dve.wait_ge(moved_ok, g + 1)
                wait(dve, added[b], 64 * i)
                dve.tensor_tensor(target[:, b, :], moved[:, b, :], m.dst_f[:, cols], ALU.add
                                  ).then_inc(target_ok, 1)
            pairs(dve, pair)

        @block.gpsimd
        def _(pool):
            pool.memset(zeros[:, :, :], 0.0).then_inc(zeroed, 1)

            def gather(g, b):
                pool.wait_ge(src_ok, g + 1)
                wait(pool, total_ok, 2 * (g - 1))
                carry(pool, m.pool_passed)
                for q in range(SLOTS):
                    pool.indirect_dma_start(
                        out=got[:, b, q, :], out_offset=None, in_=messages,
                        in_offset=bass.IndirectOffsetOnAxis(ap=src_now[:, b, q:q + 1], axis=0)
                    ).then_inc(gathered[b], 16)

            def scatter(i, b):
                g = i * 2 + b
                pool.wait_ge(target_ok, g + 1)
                pool.wait_ge(merged_ok, 2 * g + 2)
                wait(pool, added[1 - b], 64 * (i + b))
                carry(pool, m.pool_passed)
                for q in range(SLOTS):
                    pool.indirect_dma_start(
                        out=table, out_offset=bass.IndirectOffsetOnAxis(ap=target[:, b, q:q + 1], axis=0),
                        in_=merged[:, b, q, :], in_offset=None, compute_op=ALU.add
                    ).then_inc(added[b], 16)

            def pair(i, b):
                g = i * 2 + b
                if not (isinstance(g, int) and g + 1 >= m.ng):
                    gather(g + 1, 1 - b)
                scatter(i, b)
            gather(0, 0)
            pool.wait_ge(cleared, 16 * m.ng)
            pairs(pool, pair)
            for b in range(2):
                pool.wait_ge(added[b], 32 * m.ng)

        @block.tensor
        def _(pe):
            def pair(i, b):
                g = i * 2 + b
                pe.wait_ge(gathered[b], 64 * (i + 1))
                pe.wait_ge(same_ok, SLOTS * (g + 1))
                for h in range(2):
                    wait(pe, merged_ok, 2 * (g - 2) + h + 1)
                    for owner in (2 * h, 2 * h + 1):
                        for q in range(owner, SLOTS):
                            done = pe.matmul(total[:, b, owner, :],
                                             same[:, b, first_block[q] + owner, :], got[:, b, q, :],
                                             start=q == owner, stop=q == SLOTS - 1)
                    done.then_inc(total_ok, 1)
            pairs(pe, pair)

        @block.scalar
        def _(act):
            def pair(i, b):
                g = i * 2 + b
                wait(act, added[b], 64 * i)
                for h in range(2):
                    act.wait_ge(total_ok, 2 * g + h + 1)
                    act.activation(merged[:, b, 2 * h:2 * h + 2, :], total[:, b, 2 * h:2 * h + 2, :],
                                   ACT.Copy).then_inc(merged_ok, 1)
            pairs(act, pair)


def prepare_attention(nc, m):
    with ExitStack() as ctx:
        sb = lambda n, s, d=F32: ctx.enter_context(nc.sbuf_tensor(n, s, d))
        sem = lambda n: ctx.enter_context(nc.semaphore(n))
        wx_t = sb("wx_t", [HD, HEADS, D])
        w_slice = sb("w_slice", [HD, SL])
        bx_t = sb("bx_t", [HD, HEADS])
        b_slice = sb("b_slice", [1, SL])
        temp, clipped, inv_temp = sb("temp", [P, HEADS]), sb("clipped", [P, HEADS]), sb("inv_temp", [P, HEADS])
        bias0, bias = sb("bias0", [1, HS]), sb("bias", [1, HS])
        rest1, rest2 = sb("rest1", [1, HS]), sb("rest2", [1, HS])
        parts = sb("parts", [1, 3, HS], BF16)
        folded = ctx.enter_context(nc.psum_tensor("folded", [P, KD, HS], F32))
        bias_ps = ctx.enter_context(nc.psum_tensor("bias_ps", [1, HS], F32))
        inputs_in, parts_in, step, projected = sem("inputs_in"), sem("parts_in"), sem("step"), sem("projected")
        block = ctx.enter_context(nc.Block())

        @block.sync
        def _(sp):
            sp.dma_start(wx_t[:, :, :], m.wx_t_dram.rearrange("(h c) f -> c h f", c=HD)).then_inc(inputs_in, 16)
            sp.dma_start(w_slice[:, :], m.w_slice_dram).then_inc(inputs_in, 16)
            sp.dma_start(bx_t[:, :], m.bx_t_dram).then_inc(inputs_in, 16)
            sp.dma_start(b_slice[:, :], m.b_slice_dram).then_inc(inputs_in, 16)
            sp.dma_start(temp[:, :], m.temp_dram.partition_broadcast(P)).then_inc(inputs_in, 16)
            sp.wait_ge(step, 9)
            for r in range(3):
                sp.dma_start(m.bias_rows[r:r + 1, :], parts[0:1, r, :]).then_inc(parts_in, 16)
            sp.wait_ge(parts_in, 48)

        @block.gpsimd
        def _(pool):
            pool.memset(m.ones3[:, :], 1.0).then_inc(m.const_ok, 1)
            pool.memset(m.y[:, :, :, D:D + 2], 1.0).then_inc(m.const_ok, 1)
            pool.memset(m.half[:, :], -0.5).then_inc(m.const_ok, 1)
            pool.wait_ge(m.const_ok, 3)

        @block.tensor
        def _(pe):
            pe.wait_ge(inputs_in, 80)
            for c in range(KD):
                for h in range(HEADS):
                    pe.matmul(folded[:, c, h * SL:(h + 1) * SL], wx_t[:, h, c * P:(c + 1) * P],
                              w_slice[:, :], start=True, stop=True)
            for h in range(HEADS):
                done = pe.matmul(bias_ps[:, h * SL:(h + 1) * SL], bx_t[:, h:h + 1], w_slice[:, :],
                                 start=True, stop=True)
            done.then_inc(projected, 1)

        @block.vector
        def _(dve):
            dve.wait_ge(inputs_in, 80)
            dve.tensor_scalar(clipped[:, :], temp[:, :], 0.1, 5.0, ALU.max, ALU.min).then_inc(step, 1)
            dve.wait_ge(step, 1)
            dve.reciprocal(inv_temp[:, :], clipped[:, :]).then_inc(step, 1)
            dve.wait_ge(step, 2)
            dve.wait_ge(projected, 1)
            for c in range(KD):
                dve.tensor_tensor(m.w_logit[:, c, :].rearrange("p (h s) -> p h s", h=HEADS),
                                  folded[:, c, :].rearrange("p (h s) -> p h s", h=HEADS),
                                  inv_temp[:, :, None].to_broadcast([P, HEADS, SL]), ALU.mult
                                  ).then_inc(projected, 1)
            heads = lambda a: a[:, :].rearrange("p (h s) -> p h s", h=HEADS)
            dve.tensor_tensor(heads(bias0), heads(bias_ps),
                              b_slice[:, None, :].to_broadcast([1, HEADS, SL]), ALU.add).then_inc(step, 1)
            dve.wait_ge(step, 3)
            dve.tensor_tensor(heads(bias), heads(bias0),
                              inv_temp[0:1, :, None].to_broadcast([1, HEADS, SL]), ALU.mult).then_inc(step, 1)
            dve.wait_ge(step, 4)
            dve.tensor_copy(parts[:, 0, :], bias[:, :]).then_inc(step, 1)
            dve.wait_ge(step, 5)
            dve.tensor_tensor(rest1[:, :], bias[:, :], parts[:, 0, :], ALU.subtract).then_inc(step, 1)
            dve.wait_ge(step, 6)
            dve.tensor_copy(parts[:, 1, :], rest1[:, :]).then_inc(step, 1)
            dve.wait_ge(step, 7)
            dve.tensor_tensor(rest2[:, :], rest1[:, :], parts[:, 1, :], ALU.subtract).then_inc(step, 1)
            dve.wait_ge(step, 8)
            dve.tensor_copy(parts[:, 2, :], rest2[:, :]).then_inc(step, 1)
            dve.wait_ge(projected, 3)
            dve.tensor_copy(m.w_hi[:, :, :], m.w_logit[:, :, :]).then_inc(projected, 1)
            dve.wait_ge(projected, 4)
            dve.tensor_tensor(m.w_lo[:, :, :], m.w_logit[:, :, :], m.w_hi[:, :, :].bitcast(F32), ALU.subtract
                              ).then_inc(projected, 1)
            dve.wait_ge(projected, 5)


def attend_tokens(nc, m):
    last_rows = (m.n - (m.ng - 1) * GROUP) // SLOTS
    message_rows, base_rows = grouped(m.messages[1], D), grouped(m.base, D)
    x1_dram, weights_dram = grouped(m.x1, D), grouped(m.slice_weights, HS)
    with ExitStack() as ctx:
        sb = lambda n, s, d=F32: ctx.enter_context(nc.sbuf_tensor(n, s, d))
        sem = lambda n: ctx.enter_context(nc.semaphore(n))
        ps = lambda n, s: ctx.enter_context(nc.psum_tensor(n, s, F32))
        message = sb("message", [P, RING, SLOTS, D])
        base = sb("a_base", [P, RING, SLOTS, D])
        found = sb("a_found", [P, RING, SLOTS, D])
        row_now = sb("a_row_now", [P, RING, SLOTS], I32)
        x1 = sb("x1_now", [P, 2, SLOTS, D])
        stats = sb("a_stats", [P, 2, SLOTS, 6])
        mean_var = sb("a_mean_var", [P, 2, SLOTS, 2])
        var, rstd = sb("a_var", [P, 2, SLOTS]), sb("a_rstd", [P, 2, SLOTS])
        y_hi, y_lo = sb("y_hi", [P, 2, KD, P], F32R), sb("y_lo", [P, 2, KD, P], F32R)
        shifted = sb("shifted", [P, 2, HS])
        expd = sb("expd", [P, 2, HS])
        top, total, inv_total = sb("top", [P, 2, HEADS]), sb("total", [P, 2, HEADS]), sb("inv_total", [P, 2, HEADS])
        weights = sb("weights", [P, RING, SLOTS, HS])
        turned = [ps(f"y_turned{i}", [P, KD, P]) for i in range(2)]
        logits = [ps(f"logits{i}", [P, HS]) for i in range(2)]
        rows_in = [sem(f"a_rows_in{b}") for b in range(RING)]
        found_in = [sem(f"a_found_in{b}") for b in range(RING)]
        x1_stored = [sem(f"x1_stored{b}") for b in range(2)]
        w_stored = [sem(f"w_stored{b}") for b in range(RING)]
        row_ok, both_ok, x1_ok, stats_ok, mean_ok, var_ok, rstd_ok, y_ok = (
            sem("a_" + n) for n in ("row_ok", "both_ok", "x1_ok", "stats_ok", "mean_ok", "var_ok", "rstd_ok", "y_ok"))
        turned_ok, hi_ok, lo_ok, logits_ok, top_ok, shifted_ok, exp_ok, total_ok, inv_ok, weights_ok, tokens_ok = (
            sem("a_" + n) for n in ("turned_ok", "hi_ok", "lo_ok", "logits_ok", "top_ok", "shifted_ok", "exp_ok",
                                    "total_ok", "inv_ok", "weights_ok", "tokens_ok"))
        block = ctx.enter_context(nc.Block())
        heads = lambda a: a.rearrange("p (h s) -> p h s", h=HEADS)
        per_head = lambda a: a[:, :, None].to_broadcast([P, HEADS, SL])

        def steps(engine, step):
            def group(it, b):
                for j in range(SLOTS):
                    step(it, b, j)
            loop(engine, m, group)

        def tile_before(it, b, j, by):
            k = b * SLOTS + j - by
            return (it, k // SLOTS, k % SLOTS) if k >= 0 else (it - 1, RING - 1, SLOTS + k)

        number = lambda it, b, j: (RING * it + b) * SLOTS + j

        @block.sync
        def _(sp):
            def load(g, b):
                wait(sp, both_ok, SLOTS * (g - RING + 1))
                wait(sp, x1_ok, SLOTS * (g - RING + 1))
                sp.dma_start(message[:, b, :, :], one_group(message_rows, g, D)).then_inc(rows_in[b], 16)
                sp.dma_start(base[:, b, :, :], one_group(base_rows, g, D)).then_inc(rows_in[b], 16)

            def group(it, b):
                g = RING * it + b
                sp.wait_ge(x1_ok, SLOTS * (g + 1))
                sp.dma_start(one_group(x1_dram, g, D), x1[:, b % 2, :, :]).then_inc(x1_stored[b % 2], 16)
                later = shifted_group(m, it, b, RING - 1)
                if later is not None:
                    load(g + RING - 1, later[1])
                sp.wait_ge(weights_ok, SLOTS * (g + 1))
                sp.dma_start(one_group(weights_dram, g, HS), weights[:, b, :, :]).then_inc(w_stored[b], 16)
            for g in range(RING - 1):
                load(g, g)
            loop(sp, m, group)
            for b in range(2):
                sp.wait_ge(x1_stored[b], 8 * m.ng)
            for b in range(RING):
                sp.wait_ge(w_stored[b], 16 * slot_uses(m, b))

        @block.scalar
        def _(act):
            def copy_turned(t, par):
                act.wait_ge(turned_ok, t + 1)
                wait(act, logits_ok, t - 1)
                act.activation(y_hi[:, par, :, :], turned[par][:, :, :], ACT.Copy).then_inc(hi_ok, 1)

            def step(it, b, j):
                t = number(it, b, j)
                if not (isinstance(t, int) and t >= m.nt - 2):
                    copy_turned(t + 2, j % 2)
                act.wait_ge(shifted_ok, t + 1)
                wait(act, total_ok, t - 1)
                wait(act, weights_ok, t - 1)
                act.activation(expd[:, j % 2, :], shifted[:, j % 2, :], ACT.Exp).then_inc(exp_ok, 1)

            copy_turned(0, 0)
            copy_turned(1, 1)
            steps(act, step)

        @block.gpsimd
        def _(pool):
            def find(it, b, j):
                g = RING * it + b
                if j == 0:
                    pool.wait_ge(row_ok, g + 1)
                    wait(pool, both_ok, SLOTS * (g - RING + 1))
                    carry(pool, m.pool_passed)
                pool.indirect_dma_start(
                    out=found[:, b, j, :], out_offset=None, in_=m.table[1],
                    in_offset=bass.IndirectOffsetOnAxis(ap=row_now[:, b, j:j + 1], axis=0)
                ).then_inc(found_in[b], 16)

            def add_half(it, b, half):
                if half == 0:
                    ring_wait(pool, rows_in, it, b, 32)
                    ring_wait(pool, found_in, it, b, 64)
                for j in (2 * half, 2 * half + 1):
                    pool.tensor_tensor(message[:, b, j, :], message[:, b, j, :], found[:, b, j, :], ALU.add
                                       ).then_inc(both_ok, 1)

            def rstd_half(it, b, half):
                pool.wait_ge(var_ok, (RING * it + b) * 2 + half + 1)
                two = slice(2 * half, 2 * half + 2)
                pool.tensor_tensor(rstd[:, b % 2, two], var[:, b % 2, two], m.half[:, :], ALU.pow
                                   ).then_inc(rstd_ok, 1)

            def normalise(it, b, j):
                t = number(it, b, j)
                pool.wait_ge(inv_ok, t + 1)
                wait(pool, tokens_ok, t - SLOTS * RING + 1)
                if j == 0:
                    ring_wait(pool, w_stored, it, b, 16, uses_back=1)
                pool.tensor_tensor(heads(weights[:, b, j, :]), heads(expd[:, j % 2, :]),
                                   per_head(inv_total[:, j % 2, :]), ALU.mult).then_inc(weights_ok, 1)

            def step(it, b, j):
                t = number(it, b, j)
                nxt, far = shifted_group(m, it, b, 1), shifted_group(m, it, b, 2)
                if 1 <= j < 3 and nxt is not None:
                    rstd_half(*nxt, j - 1)
                if far is not None:
                    find(*far, j)
                if j < 2 and nxt is not None:
                    add_half(*nxt, j)
                if not (isinstance(t, int) and t == 0):
                    normalise(*tile_before(it, b, j, 1))

            for b in range(2):
                for j in range(SLOTS):
                    find(0, b, j)
            for half in range(2):
                add_half(0, 0, half)
            for half in range(2):
                rstd_half(0, 0, half)
            steps(pool, step)
            normalise(m.iters - 1, m.last - 1, SLOTS - 1)

        @block.vector
        def _(dve):
            def rows_of(it, b):
                ring_wait(dve, found_in, it, b, 64, uses_back=1)
                dve.tensor_copy(row_now[:, b, :], m.node_row[:, bass.ds((RING * it + b) * SLOTS, SLOTS)]
                                ).then_inc(row_ok, 1)

            def residual_half(it, b, half):
                g, c = RING * it + b, b % 2
                if half == 0:
                    wait(dve, x1_stored[c], 16 * (RING // 2 * it + b // 2))
                tiles = (2 * half, 2 * half + 1)
                for j in tiles:
                    dve.wait_ge(both_ok, g * SLOTS + j + 1)
                    dve.scalar_tensor_tensor(x1[:, c, j, :], message[:, b, j, :],
                                             m.dinv[:, bass.ds(g * SLOTS + j, 1)], base[:, b, j, :],
                                             ALU.mult, ALU.add).then_inc(x1_ok, 1)
                for j in tiles:
                    dve.wait_ge(x1_ok, g * SLOTS + j + 1)
                    dve.bn_stats(stats[:, c, j, :], x1[:, c, j, :]).then_inc(stats_ok, 1)
                for j in tiles:
                    dve.wait_ge(stats_ok, g * SLOTS + j + 1)
                    carry(dve, m.dve_passed)
                    dve.bn_aggr(mean_var[:, c, j, :], stats[:, c, j, :]).then_inc(mean_ok, 1)
                dve.wait_ge(mean_ok, g * SLOTS + 2 * half + 2)
                two = slice(2 * half, 2 * half + 2)
                dve.tensor_scalar(var[:, c, two], mean_var[:, c, two, 1], LN_EPS, None, ALU.add
                                  ).then_inc(var_ok, 1)

            def y_half(it, b, half):
                g, c = RING * it + b, b % 2
                dve.wait_ge(rstd_ok, 2 * g + half + 1)
                if half == 0:
                    wait(dve, tokens_ok, SLOTS * (g - 1))
                for j in (2 * half, 2 * half + 1):
                    dve.tensor_scalar(m.y[:, c, j, 0:D], x1[:, c, j, :], mean_var[:, c, j, 0:1],
                                      rstd[:, c, j:j + 1], ALU.subtract, ALU.mult).then_inc(y_ok, 1)

            def rest_of(t, par):
                dve.wait_ge(hi_ok, t + 1)
                wait(dve, logits_ok, t - 1)
                dve.tensor_tensor(y_lo[:, par, :, :], turned[par][:, :, :], y_hi[:, par, :, :].bitcast(F32),
                                  ALU.subtract).then_inc(lo_ok, 1)

            def sums(t, par):
                dve.wait_ge(exp_ok, t + 1)
                dve.tensor_reduce(total[:, par, :], heads(expd[:, par, :]), AX.X, ALU.add).then_inc(total_ok, 1)
                dve.wait_ge(total_ok, t + 1)
                wait(dve, weights_ok, t - 1)
                dve.reciprocal(inv_total[:, par, :], total[:, par, :]).then_inc(inv_ok, 1)

            def step(it, b, j):
                t = number(it, b, j)
                nxt, far = shifted_group(m, it, b, 1), shifted_group(m, it, b, 3)
                if j == 0 and far is not None:
                    rows_of(*far)
                if j >= 2 and nxt is not None:
                    y_half(*nxt, j - 2)
                par = j % 2
                if not (isinstance(t, int) and t == m.nt - 1):
                    rest_of(t + 1, 1 - par)
                if 1 <= j < 3 and nxt is not None:
                    residual_half(*nxt, j - 1)
                if not (isinstance(t, int) and t == 0):
                    sums(t - 1, 1 - par)
                dve.wait_ge(logits_ok, t + 1)
                dve.tensor_reduce(top[:, par, :], heads(logits[par][:, :]), AX.X, ALU.max).then_inc(top_ok, 1)
                dve.wait_ge(top_ok, t + 1)
                wait(dve, exp_ok, t - 1)
                dve.tensor_tensor(heads(shifted[:, par, :]), heads(logits[par][:, :]),
                                  per_head(top[:, par, :]), ALU.subtract).then_inc(shifted_ok, 1)

            for b in range(3):
                rows_of(0, b)
            for half in range(2):
                residual_half(0, 0, half)
            for half in range(2):
                y_half(0, 0, half)
            rest_of(0, 0)
            steps(dve, step)
            sums(m.nt - 1, 1)

        @block.tensor
        def _(pe):
            def turn(it, b, j):
                t = number(it, b, j)
                pe.wait_ge(y_ok, t + 1)
                wait(pe, lo_ok, t - 1)
                for c in range(KD):
                    done = pe.transpose(turned[j % 2][:, c, :], m.y[:, b % 2, j, c * P:(c + 1) * P], m.ident[:, :])
                done.then_inc(turned_ok, 1)

            def project(t, par):
                wait(pe, shifted_ok, t - 1)
                pe.matmul(logits[par][:, :], m.ones3[:, :], m.bias_rows[:, :], start=True, stop=False)
                pe.wait_ge(hi_ok, t + 1)
                for c in range(KD):
                    pe.matmul(logits[par][:, :], y_hi[:, par, c, :], m.w_hi[:, c, :], start=False, stop=False)
                    pe.matmul(logits[par][:, :], y_hi[:, par, c, :], m.w_lo[:, c, :], start=False, stop=False)
                pe.wait_ge(lo_ok, t + 1)
                for c in range(KD):
                    done = pe.matmul(logits[par][:, :], y_lo[:, par, c, :], m.w_hi[:, c, :],
                                     start=False, stop=c == KD - 1)
                done.then_inc(logits_ok, 1)

            def add_tokens(it, b, j):
                t = number(it, b, j)
                pe.wait_ge(weights_ok, t + 1)
                at = t if isinstance(t, int) else None
                rows = last_rows if at is not None and at >= m.nt - SLOTS else P
                for c in range(CH):
                    done = pe.matmul(m.tokens[c][:, :], weights[0:rows, b, j, c * P:(c + 1) * P],
                                     m.y[0:rows, b % 2, j, 0:D + 1], start=at == 0, stop=at == m.nt - 1)
                done.then_inc(tokens_ok, 1)

            def step(it, b, j):
                t = number(it, b, j)
                at = t if isinstance(t, int) else None
                project(t, j % 2)
                if at is None or at < m.nt - 2:
                    turn(*((it, b, j + 2) if j + 2 < SLOTS else (*shifted_group(m, it, b, 1), j + 2 - SLOTS)))
                if at is None or at >= 2:
                    add_tokens(*tile_before(it, b, j, 2))

            turn(0, 0, 0)
            turn(0, 0, 1)
            steps(pe, step)
            for j in (SLOTS - 2, SLOTS - 1):
                add_tokens(m.iters - 1, m.last - 1, j)


def mix_tokens(nc, m):
    with ExitStack() as ctx:
        sb = lambda n, s, d=F32: ctx.enter_context(nc.sbuf_tensor(n, s, d))
        sem = lambda n: ctx.enter_context(nc.semaphore(n))
        ps = lambda n, s: ctx.enter_context(nc.psum_tensor(n, s, F32))
        w_fx, b_fx = sb("w_fx", [P, KD, HEADS * HD]), sb("b_fx", [1, HEADS * HD])
        w_q, w_k, w_v = sb("w_q", [HD, HD]), sb("w_k", [HD, HD]), sb("w_v", [HD, HD])
        w_out = sb("w_out", [HD, HEADS, D])
        safe, inv = sb("m_safe", [P, CH]), sb("m_inv", [P, CH])
        mean_y = sb("mean_y", [P, CH, D + 1])
        mean_t, share = sb("mean_t", [P, KD, HS]), sb("share", [1, HS])
        token_t = sb("token_t", [HD, HS])
        q_t, k_t, v = sb("q_t", [HD, HS]), sb("k_t", [HD, HS]), sb("v", [SL, HS])
        top, total, inv_total = sb("m_top", [SL, HEADS]), sb("m_total", [SL, HEADS]), sb("m_inv_total", [SL, HEADS])
        shifted, expd, probs, probs_t = (sb(n, [SL, HS]) for n in ("m_shifted", "m_expd", "probs", "probs_t"))
        out_t = sb("out_t", [HD, HEADS, P])
        bank = [ps(f"mix{i}", [P, HS]) for i in range(4)]
        inputs_in, zero_ok, step, made = sem("m_inputs_in"), sem("m_zero_ok"), sem("m_step"), sem("m_made")
        exp_ok = sem("m_exp_ok")
        block = ctx.enter_context(nc.Block())
        heads = lambda a: a.rearrange("p (h s) -> p h s", h=HEADS)
        per_head = lambda a: a[:, :, None].to_broadcast([SL, HEADS, SL])
        head = lambda h: slice(h * SL, (h + 1) * SL)

        @block.sync
        def _(sp):
            sp.dma_start(w_fx[:, :, :], m.w_fx_dram.rearrange("(k p) n -> p k n", p=P)).then_inc(inputs_in, 16)
            sp.dma_start(b_fx[:, :], m.b_fx_dram).then_inc(inputs_in, 16)
            for to, of in ((w_q, m.w_q_dram), (w_k, m.w_k_dram), (w_v, m.w_v_dram)):
                sp.dma_start(to[:, :], of).then_inc(inputs_in, 16)
            sp.dma_start(w_out[:, :, :], m.w_out_dram.rearrange("(h c) n -> c h n", c=HD)).then_inc(inputs_in, 16)

        @block.gpsimd
        def _(pool):
            pool.memset(out_t[:, :, :], 0.0).then_inc(zero_ok, 1)

        @block.tensor
        def _(pe):
            pe.wait_ge(inputs_in, 96)
            pe.wait_ge(step, 6)
            for c in range(CH):
                for k in range(KD):
                    pe.transpose(bank[k][:, c * P:(c + 1) * P], mean_y[:, c, k * P:(k + 1) * P], m.ident[:, :])
                done = pe.transpose(bank[2][0:1, c * P:(c + 1) * P], mean_y[:, c, D:D + 1], m.ident[:, :])
            done.then_inc(made, 1)
            pe.wait_ge(step, 9)
            for h in range(HEADS):
                for k in range(KD):
                    pe.matmul(bank[3][0:HD, head(h)], w_fx[:, k, head(h)], mean_t[:, k, head(h)],
                              start=k == 0, stop=False)
                done = pe.matmul(bank[3][0:HD, head(h)], b_fx[:, head(h)], share[:, head(h)],
                                 start=False, stop=True)
            done.then_inc(made, 1)
            pe.wait_ge(step, 10)
            pe.matmul(bank[0][0:HD, :], w_q[:, :], token_t[:, :], start=True, stop=True)
            pe.matmul(bank[1][0:HD, :], w_k[:, :], token_t[:, :], start=True, stop=True)
            for h in range(HEADS):
                done = pe.matmul(bank[2][0:SL, head(h)], token_t[:, head(h)], w_v[:, :], start=True, stop=True)
            done.then_inc(made, 1)
            pe.wait_ge(step, 13)
            for h in range(HEADS):
                done = pe.matmul(bank[3][0:SL, head(h)], q_t[:, head(h)], k_t[:, head(h)], start=True, stop=True)
            done.then_inc(made, 1)
            pe.wait_ge(step, 18)
            for h in range(HEADS):
                done = pe.transpose(bank[0][0:SL, head(h)], probs[:, head(h)], m.ident[0:SL, 0:SL])
            done.then_inc(made, 1)
            pe.wait_ge(step, 19)
            for h in range(HEADS):
                done = pe.matmul(bank[1][0:HD, head(h)], v[:, head(h)], probs_t[:, head(h)], start=True, stop=True)
            done.then_inc(made, 1)
            pe.wait_ge(step, 21)
            for c in range(CH):
                half = slice(c % 2 * D, (c % 2 + 1) * D)
                pe.matmul(bank[2 + c // 2][:, half], out_t[:, 2 * c, :], w_out[:, 2 * c, :], start=True, stop=False)
                done = pe.matmul(bank[2 + c // 2][:, half], out_t[:, 2 * c + 1, :], w_out[:, 2 * c + 1, :],
                                 start=False, stop=True)
            done.then_inc(made, 1)

        @block.scalar
        def _(act):
            act.wait_ge(step, 15)
            act.activation(expd[:, :], shifted[:, :], ACT.Exp, scale=float(HD) ** -0.5).then_inc(exp_ok, 1)

        @block.vector
        def _(dve):
            for c in range(CH):
                last = dve.tensor_scalar(safe[:, c:c + 1], m.tokens[c][:, D:D + 1], TOKEN_EPS, None, ALU.add)
            last.then_inc(step, 1)
            dve.wait_ge(step, 1)
            dve.reciprocal(inv[:, :], safe[:, :]).then_inc(step, 1)
            dve.wait_ge(step, 2)
            for c in range(CH):
                dve.tensor_scalar(mean_y[:, c, :], m.tokens[c][:, :], inv[:, c:c + 1], None, ALU.mult
                                  ).then_inc(step, 1)
            dve.wait_ge(made, 1)
            for k in range(KD):
                dve.tensor_copy(mean_t[:, k, :], bank[k][:, :]).then_inc(step, 1)
            dve.tensor_copy(share[:, :], bank[2][0:1, :]).then_inc(step, 1)
            dve.wait_ge(made, 2)
            dve.tensor_copy(token_t[:, :], bank[3][0:HD, :]).then_inc(step, 1)
            dve.wait_ge(made, 3)
            for n, to in enumerate((q_t, k_t, v)):
                dve.tensor_copy(to[:, :], bank[n][0:HD, :]).then_inc(step, 1)
            dve.wait_ge(made, 4)
            dve.tensor_reduce(top[:, :], heads(bank[3][0:SL, :]), AX.X, ALU.max).then_inc(step, 1)
            dve.wait_ge(step, 14)
            dve.tensor_tensor(heads(shifted[:, :]), heads(bank[3][0:SL, :]), per_head(top[:, :]),
                              ALU.subtract).then_inc(step, 1)
            dve.wait_ge(exp_ok, 1)
            dve.tensor_reduce(total[:, :], heads(expd[:, :]), AX.X, ALU.add).then_inc(step, 1)
            dve.wait_ge(step, 16)
            dve.reciprocal(inv_total[:, :], total[:, :]).then_inc(step, 1)
            dve.wait_ge(step, 17)
            dve.tensor_tensor(heads(probs[:, :]), heads(expd[:, :]), per_head(inv_total[:, :]),
                              ALU.mult).then_inc(step, 1)
            dve.wait_ge(made, 5)
            dve.tensor_copy(probs_t[:, :], bank[0][0:SL, :]).then_inc(step, 1)
            dve.wait_ge(made, 6)
            dve.wait_ge(zero_ok, 1)
            outs = bank[1][0:HD, :].rearrange("p (c a s) -> p c a s", a=2, s=SL)
            slots = out_t[:, :, :].rearrange("p (c a) s -> p c a s", a=2)
            for a in range(2):
                dve.tensor_copy(slots[:, :, a, a * SL:(a + 1) * SL], outs[:, :, a, :]).then_inc(step, 1)
            dve.wait_ge(made, 7)
            for n in range(2):
                dve.tensor_copy(m.mixed[:, 2 * n:2 * n + 2, :],
                                bank[2 + n][:, :].rearrange("p (c n) -> p c n", c=2)).then_inc(step, 1)
            dve.wait_ge(step, 23)


def write_output(nc, m):
    weights_dram, x1_dram, out_dram = grouped(m.slice_weights, HS), grouped(m.x1, D), grouped(m.out, D)
    with ExitStack() as ctx:
        sb = lambda n, s, d=F32: ctx.enter_context(nc.sbuf_tensor(n, s, d))
        sem = lambda n: ctx.enter_context(nc.semaphore(n))
        weights = sb("o_weights", [P, RING, SLOTS, HS])
        x1, out = (sb(n, [P, RING, SLOTS, D]) for n in ("o_x1", "o_out"))
        base = sb("o_base", [P, 2, SLOTS, D])
        hi, lo = sb("o_hi", [P, 2, CH, P], F32R), sb("o_lo", [P, 2, CH, P], F32R)
        mixed_hi, mixed_lo = sb("mixed_hi", [P, CH, D], F32R), sb("mixed_lo", [P, CH, D], F32R)
        turned = [ctx.enter_context(nc.psum_tensor(f"o_turned{i}", [P, CH, P], F32)) for i in range(2)]
        product = [ctx.enter_context(nc.psum_tensor(f"o_product{i}", [P, D], F32)) for i in range(2)]
        rows_in = [sem(f"o_rows_in{b}") for b in range(RING)]
        stored = [sem(f"o_stored{b}") for b in range(RING)]
        turned_ok, hi_ok, lo_ok, product_ok, base_ok, out_ok, split = (
            sem("o_" + n) for n in ("turned_ok", "hi_ok", "lo_ok", "product_ok", "base_ok", "out_ok", "split"))
        block = ctx.enter_context(nc.Block())

        def steps(engine, step):
            def group(it, b):
                for j in range(SLOTS):
                    step(it, b, j, (RING * it + b) * SLOTS + j)
            loop(engine, m, group)

        @block.sync
        def _(sp):
            def load(g, b):
                wait(sp, turned_ok, SLOTS * (g - RING + 1))
                wait(sp, base_ok, SLOTS * (g - RING + 1))
                sp.dma_start(weights[:, b, :, :], one_group(weights_dram, g, HS)).then_inc(rows_in[b], 16)
                sp.dma_start(x1[:, b, :, :], one_group(x1_dram, g, D)).then_inc(rows_in[b], 16)

            def group(it, b):
                g = RING * it + b
                later = shifted_group(m, it, b, RING - 1)
                if later is not None:
                    load(g + RING - 1, later[1])
                sp.wait_ge(out_ok, SLOTS * (g + 1))
                sp.dma_start(one_group(out_dram, g, D), out[:, b, :, :]).then_inc(stored[b], 16)
            for g in range(RING - 1):
                load(g, g)
            loop(sp, m, group)
            for b in range(RING):
                sp.wait_ge(stored[b], 16 * slot_uses(m, b))

        @block.tensor
        def _(pe):
            pe.wait_ge(split, 2)

            def multiply(t, par):
                pe.wait_ge(hi_ok, t + 1)
                wait(pe, out_ok, t - 1)
                for c in range(CH):
                    pe.matmul(product[par][:, :], hi[:, par, c, :], mixed_hi[:, c, :], start=c == 0, stop=False)
                    pe.matmul(product[par][:, :], hi[:, par, c, :], mixed_lo[:, c, :], start=False, stop=False)
                pe.wait_ge(lo_ok, t + 1)
                for c in range(CH):
                    done = pe.matmul(product[par][:, :], lo[:, par, c, :], mixed_hi[:, c, :],
                                     start=False, stop=c == CH - 1)
                done.then_inc(product_ok, 1)

            def step(it, b, j, t):
                if j == 0:
                    ring_wait(pe, rows_in, it, b, 32)
                wait(pe, lo_ok, t - 1)
                for c in range(CH):
                    done = pe.transpose(turned[j % 2][:, c, :], weights[:, b, j, c * P:(c + 1) * P], m.ident[:, :])
                done.then_inc(turned_ok, 1)
                if not (isinstance(t, int) and t == 0):
                    multiply(t - 1, (j - 1) % 2)
            steps(pe, step)
            multiply(m.nt - 1, 1)

        @block.scalar
        def _(act):
            def step(it, b, j, t):
                act.wait_ge(turned_ok, t + 1)
                wait(act, product_ok, t - 1)
                act.activation(hi[:, j % 2, :, :], turned[j % 2][:, :, :], ACT.Copy).then_inc(hi_ok, 1)
            steps(act, step)

        @block.gpsimd
        def _(pool):
            def step(it, b, j, t):
                if j == 0:
                    ring_wait(pool, rows_in, it, b, 32)
                    wait(pool, out_ok, t - SLOTS)
                pool.tensor_tensor(base[:, b % 2, j, :], x1[:, b, j, :], m.b_out[:, :], ALU.add).then_inc(base_ok, 1)
            steps(pool, step)

        @block.vector
        def _(dve):
            dve.tensor_copy(mixed_hi[:, :, :], m.mixed[:, :, :]).then_inc(split, 1)
            dve.wait_ge(split, 1)
            dve.tensor_tensor(mixed_lo[:, :, :], m.mixed[:, :, :], mixed_hi[:, :, :].bitcast(F32), ALU.subtract
                              ).then_inc(split, 1)

            def finish(it, b, j, t):
                if j == 0:
                    ring_wait(dve, stored, it, b, 16, uses_back=1)
                dve.wait_ge(product_ok, t + 1)
                dve.wait_ge(base_ok, t + 1)
                dve.tensor_tensor(out[:, b, j, :], product[j % 2][:, :], base[:, b % 2, j, :], ALU.add
                                  ).then_inc(out_ok, 1)

            def step(it, b, j, t):
                dve.wait_ge(hi_ok, t + 1)
                wait(dve, product_ok, t - 1)
                dve.tensor_tensor(lo[:, j % 2, :, :], turned[j % 2][:, :, :], hi[:, j % 2, :, :].bitcast(F32),
                                  ALU.subtract).then_inc(lo_ok, 1)
                if not (isinstance(t, int) and t == 0):
                    if j:
                        finish(it, b, j - 1, t - 1)
                    elif b:
                        finish(it, b - 1, SLOTS - 1, t - 1)
                    else:
                        finish(it - 1, RING - 1, SLOTS - 1, t - 1)
            steps(dve, step)
            finish(m.iters - 1, m.last - 1, SLOTS - 1, m.nt - 1)


def gnn_and_slice_attention(nc, ins, out, n):
    m = Model()
    m.x, m.src_cols, m.dst_cols, m.prev_cols, m.dst_rows = (
        ins[k] for k in ("x", "src_cols", "dst_cols", "prev_cols", "dst_rows"))
    m.w1, m.b1_dram, m.w2, m.b2_dram = (ins[k] for k in ("w1", "b1_dram", "w2", "b2_dram"))
    m.w_fx_dram, m.b_fx_dram, m.wx_t_dram, m.bx_t_dram = (
        ins[k] for k in ("w_fx_dram", "b_fx_dram", "wx_t_dram", "bx_t_dram"))
    m.w_slice_dram, m.b_slice_dram, m.temp_dram = (ins[k] for k in ("w_slice_dram", "b_slice_dram", "temp_dram"))
    m.w_q_dram, m.w_k_dram, m.w_v_dram = (ins[k] for k in ("w_q_dram", "w_k_dram", "w_v_dram"))
    m.w_out_dram, m.b_out_dram = ins["w_out_dram"], ins["b_out_dram"]
    m.out, m.n, m.np = out, n, padded(n)
    m.nt, m.ng = m.np // P, m.np // GROUP
    m.iters = (m.ng + RING - 1) // RING
    m.last = m.ng - (m.iters - 1) * RING
    assert (n - (m.ng - 1) * GROUP) % SLOTS == 0 and 0 < n - (m.ng - 1) * GROUP
    dram = lambda name, rows, width: nc.dram_tensor(name, [rows, width], F32).ap()
    m.messages = [dram(f"messages{c}", m.np, D) for c in range(2)]
    m.table = [dram(f"table{c}", m.np + GROUP, D) for c in range(2)]
    m.base = dram("base", m.np, D)
    m.x1 = dram("x1", m.np, D)
    m.slice_weights = dram("slice_weights", m.np, HS)
    with ExitStack() as ctx:
        sb = lambda name, s, d=F32: ctx.enter_context(nc.sbuf_tensor(name, s, d))
        m.ident = sb("ident", [P, P])
        m.earlier = sb("earlier", [P, GROUP])
        m.spare = sb("spare", [P, SLOTS])
        m.dst_i, m.src_i, m.dst_f = sb("dst_i", [P, m.nt], I32), sb("src_i", [P, m.nt], I32), sb("dst_f", [P, m.nt])
        m.dinv, m.prev_last, m.node_row = sb("dinv", [P, m.nt]), sb("prev_last", [P, m.nt]), sb("node_row", [P, m.nt], I32)
        m.in_order = sb("in_order", [1, 1], I32)
        m.b1, m.b2, m.b_out = sb("b1", [P, D]), sb("b2", [P, D]), sb("b_out", [P, D])
        m.w_logit = sb("w_logit", [P, KD, HS])
        m.w_hi, m.w_lo = sb("logit_hi", [P, KD, HS], F32R), sb("logit_lo", [P, KD, HS], F32R)
        m.bias_rows, m.ones3 = sb("bias_rows", [3, HS], BF16), sb("ones3", [3, P], BF16)
        m.y = sb("y", [P, 2, SLOTS, D + 2])
        m.half = sb("half", [P, 2])
        m.mixed = sb("mixed", [P, CH, D])
        m.const_ok, m.pool_passed, m.dve_passed = (
            ctx.enter_context(nc.semaphore(name)) for name in ("const_ok", "pool_passed", "dve_passed"))
        count_degrees(nc, m)
        transform(nc, m, 0)
        sum_edges(nc, m, 0)
        transform(nc, m, 1)
        sum_edges(nc, m, 1)
        prepare_attention(nc, m)
        m.tokens = [ctx.enter_context(nc.psum_tensor(f"tokens{c}", [P, D + 1], F32)) for c in range(CH)]
        attend_tokens(nc, m)
        mix_tokens(nc, m)
        write_output(nc, m)


def kernel(**inputs):
    import numpy as _np
    import concourse.bacc as _bacc
    from concourse import mybir as _mybir
    from concourse.bass_utils import run_bass_kernel_spmd as _run

    a = {k: _np.asarray(v) for k, v in inputs.items()}
    n = a["x"].shape[0]
    rows = padded(n)
    x = _np.zeros((rows, D), _np.float32)
    x[:n] = a["x"]
    pad = _np.arange(n, rows, dtype=_np.int32)
    src, dst = (_np.concatenate([a[k], pad]) for k in ("src", "dst"))
    columns = lambda e: _np.ascontiguousarray(e.reshape(-1, P).T)
    row = lambda v: _np.ascontiguousarray(v.reshape(1, -1))
    arrays = {
        "x": x,
        "src_cols": columns(src),
        "dst_cols": columns(dst),
        "prev_cols": columns(_np.concatenate([dst[:1], dst[:-1]])),
        "dst_rows": dst.reshape(-1, GROUP),
        "w1": a["L0_gnn_W1"], "b1_dram": a["L0_gnn_b1"],
        "w2": a["L0_gnn_W2"], "b2_dram": a["L0_gnn_b2"],
        "w_fx_dram": a["L0_ffn_W_fx"], "b_fx_dram": row(a["L0_ffn_b_fx"]),
        "wx_t_dram": _np.ascontiguousarray(a["L0_ffn_W_x"].T),
        "bx_t_dram": _np.ascontiguousarray(a["L0_ffn_b_x"].reshape(HEADS, HD).T),
        "w_slice_dram": a["L0_ffn_W_slice"], "b_slice_dram": row(a["L0_ffn_b_slice"]),
        "w_q_dram": a["L0_ffn_W_q"], "w_k_dram": a["L0_ffn_W_k"], "w_v_dram": a["L0_ffn_W_v"],
        "w_out_dram": a["L0_ffn_W_out"], "b_out_dram": a["L0_ffn_b_out"],
        "temp_dram": a["L0_ffn_temperature"].reshape(-1),
    }
    nc = _bacc.Bacc("TRN2", target_bir_lowering=False, num_devices=1)
    ins = {k: nc.dram_tensor(f"in_{k}", v.shape, _mybir.dt.from_np(v.dtype), kind="ExternalInput").ap()
           for k, v in arrays.items()}
    out = nc.dram_tensor("out_0", (rows, D), F32, kind="ExternalOutput").ap()
    gnn_and_slice_attention(nc, ins, out, n)
    r = _run(nc, [{f"in_{k}": v for k, v in arrays.items()}], core_ids=[0])
    return r.results[0]["out_0"][:n]
```

```python
from contextlib import ExitStack

import concourse.bass as bass
from concourse import mybir

F32 = mybir.dt.float32
F32R = mybir.dt.float32r
BF16 = mybir.dt.bfloat16
I32 = mybir.dt.int32
ACT = mybir.ActivationFunctionType
ALU = mybir.AluOpType
AX = mybir.AxisListType

P = 128
D = 256
KD = D // P
SLOTS = 4
GROUP = P * SLOTS
HEADS = 8
HD = 64
SL = 64
HS = HEADS * SL
CH = HS // P
LN_EPS = 1e-5
TOKEN_EPS = 1e-5
RING = 4
WIDE = 4


class Model:
    pass


def padded(n):
    step = GROUP * 2
    return (n + step - 1) // step * step


def wait(engine, semaphore, value):
    if isinstance(value, int) and value <= 0:
        return
    engine.wait_ge(semaphore, value)


def carry(engine, passed):
    engine.sem_inc(passed, 1)


def loop(engine, m, group):
    for b in range(RING):
        group(0, b)
    if m.iters > 3:
        with engine.Fori(1, m.iters - 2) as it:
            for b in range(RING):
                group(it, b)
    for it in range(max(1, m.iters - 2), m.iters):
        for b in range(RING if it < m.iters - 1 else m.last):
            group(it, b)


def slot_uses(m, b):
    return m.iters - (b >= m.last)


def ring_wait(engine, semaphores, it, b, increment, uses_back=0):
    wait(engine, semaphores[b], increment * (it + 1 - uses_back))


def shifted_group(m, it, b, by):
    if isinstance(it, int) and RING * it + b + by >= m.ng:
        return None
    return it + (b + by) // RING, (b + by) % RING


def edge_group(dram, g):
    view = dram[0:dram.shape[0] // GROUP * GROUP, :].rearrange("(g j p) d -> g p j d", p=P, j=SLOTS)
    return view[bass.ds(g, 1), :, :, :].rearrange("g p j d -> p (g j) d")


def grouped(dram, width):
    return dram[0:dram.shape[0] // GROUP * GROUP, :].rearrange(
        "(g p j) d -> g p (j d)", p=P, j=SLOTS)


def one_group(view, g, width):
    return view[bass.ds(g, 1), :, :].rearrange("g p (j d) -> p (g j) d", d=width)


def cleared_semaphores(nc, ctx):
    made = []

    def give_back():
        nc.clear_and_free_semaphores(made)
        nc.all_engine_barrier()
    ctx.callback(give_back)

    def semaphore(name):
        made.append(nc.alloc_semaphore(name))
        return made[-1]
    return semaphore


def count_degrees(nc, m):
    nt, ng = m.nt, m.ng
    no_row = float(m.np)
    ring_tiles = SLOTS * RING
    on_pool = (0, 2, 5, 7, 9, 12, 14)
    with ExitStack() as ctx:
        sb = lambda n, s, d=F32: ctx.enter_context(nc.sbuf_tensor(n, s, d))
        sem = lambda n: ctx.enter_context(nc.semaphore(n))
        ps = lambda n, s: ctx.enter_context(nc.psum_tensor(n, s, F32))
        lo_i, hi_a, hi_b, hi_i, prev_i = (
            sb(n, [P, nt], I32) for n in ("lo_i", "hi_a", "hi_b", "hi_i", "prev_i"))
        lo_f, hi_f = sb("lo_f", [P, nt]), sb("hi_f", [P, nt])
        lo_now = sb("lo_now", [P, 2, SLOTS])
        iota_hi, iota_lo = sb("iota_hi", [P, nt], BF16), sb("iota_lo", [P, P], BF16)
        hot_hi, hot_lo = sb("hot_hi", [P, ring_tiles, nt], BF16), sb("hot_lo", [P, ring_tiles, P], BF16)
        degree, root = sb("degree", [P, nt]), sb("root", [P, nt])
        falls, any_fall = sb("falls", [P, nt]), sb("any_fall", [P, 1])
        order = sb("order", [P, 1])
        cumulated, has_edges = sb("cumulated", [P, nt]), sb("has_edges", [P, nt])
        node_id, row_a, row_b = sb("node_id", [P, nt]), sb("row_a", [P, nt]), sb("row_b", [P, nt])
        scan = [sb(f"scan{i}", [P, ng]) for i in range(2)]
        group_base, first_row = sb("group_base", [P, ng]), sb("first_row", [P, ng])
        before, ones = sb("before", [P, P]), sb("ones", [P, P])
        zeros = sb("zeros", [P, SLOTS * D])
        counts = ps("counts", [P, nt])
        in_group, of_group, n_falls = ps("in_group", [P, ng]), ps("of_group", [P, ng]), ps("n_falls", [P, 1])
        dst_in, prev_in, rows_in, zeroed = sem("dst_in"), sem("prev_in"), sem("rows_in"), sem("zeroed")
        consts, split, digits, picked = sem("consts"), sem("split"), sem("digits"), sem("picked")
        lo_copied, hi_hot, lo_hot, lo_hot_pool, counted = (
            sem(n) for n in ("lo_copied", "hi_hot", "lo_hot", "lo_hot_pool", "counted"))
        degree_ok, rooted, linked, summed = sem("degree_ok"), sem("rooted"), sem("linked"), sem("summed")
        block = ctx.enter_context(nc.Block())
        by_slot = lambda a: a[:, :].rearrange("p (g j) -> p g j", j=SLOTS)

        @block.sync
        def _(sp):
            sp.dma_start(m.dst_i[:, :], m.dst_cols).then_inc(dst_in, 16)
            sp.dma_start(prev_i[:, :], m.prev_cols).then_inc(prev_in, 16)
            sp.dma_start(m.src_i[:, :], m.src_cols).then_inc(rows_in, 16)
            sp.dma_start(m.b1[:, :], m.b1_dram.partition_broadcast(P)).then_inc(rows_in, 16)
            sp.dma_start(m.b2[:, :], m.b2_dram.partition_broadcast(P)).then_inc(rows_in, 16)
            sp.dma_start(m.b_out[:, :], m.b_out_dram.partition_broadcast(P)).then_inc(rows_in, 16)
            sp.wait_ge(zeroed, 1)
            for table in m.table:
                sp.dma_start(table[m.np:m.np + GROUP, :].rearrange("(p j) d -> p (j d)", j=SLOTS),
                             zeros[:, :]).then_inc(rows_in, 16)
            sp.wait_ge(rows_in, 96)

        @block.gpsimd
        def _(pool):
            pool.iota(iota_hi[:, :], [[1, nt]], base=-(nt // 2), channel_multiplier=0,
                      allow_small_or_imprecise_dtypes=True).then_inc(consts, 1)
            pool.iota(iota_lo[:, :], [[1, P]], base=0, channel_multiplier=0,
                      allow_small_or_imprecise_dtypes=True).then_inc(consts, 1)
            pool.memset(zeros[:, :], 0.0).then_inc(zeroed, 1)
            pool.memset(m.ident[:, :], 0.0).then_inc(consts, 1)
            pool.memset(m.earlier[:, :], 1.0).then_inc(consts, 1)
            pool.memset(before[:, :], 1.0).then_inc(consts, 1)
            pool.memset(ones[:, :], 1.0).then_inc(consts, 1)
            pool.iota(m.spare[:, :], [[1, SLOTS]], base=m.np, channel_multiplier=SLOTS,
                      allow_small_or_imprecise_dtypes=True).then_inc(consts, 1)
            pool.iota(node_id[:, :], [[GROUP, ng], [1, SLOTS]], base=0, channel_multiplier=SLOTS,
                      allow_small_or_imprecise_dtypes=True).then_inc(consts, 1)
            pool.wait_ge(consts, 8)
            pool.affine_select(out=m.ident[:, :], in_=m.ident[:, :], compare_op=ALU.not_equal,
                               fill=1.0, base=0, pattern=[[-1, P]], channel_multiplier=1).then_inc(consts, 1)
            last = m.earlier[:, (SLOTS - 1) * P:]
            pool.affine_select(out=last, in_=last, compare_op=ALU.is_gt, fill=0.0, base=0,
                               pattern=[[-1, P]], channel_multiplier=1).then_inc(consts, 1)
            pool.affine_select(out=before[:, :], in_=before[:, :], compare_op=ALU.is_gt, fill=0.0, base=0,
                               pattern=[[1, P]], channel_multiplier=-1).then_inc(consts, 1)
            pool.wait_ge(picked, 2)
            pool.affine_select(out=m.prev_last[:, :], in_=m.prev_last[:, :], compare_op=ALU.is_ge, fill=-1.0,
                               base=-(P - 1), pattern=[[0, nt]], channel_multiplier=1).then_inc(consts, 1)
            pool.wait_ge(digits, 2)

            def group(it, b):
                g = RING * it + b
                mine = [j for j in range(SLOTS) if b * SLOTS + j in on_pool]
                per_ring = len(on_pool)
                done_before = len([k for k in on_pool if k < b * SLOTS])
                back = len([k for k in on_pool if (b - 1) * SLOTS <= k < b * SLOTS]) if b else len(
                    [k for k in on_pool if k >= (RING - 1) * SLOTS])
                wait(pool, lo_hot_pool, it * per_ring + done_before - back)
                pool.tensor_copy(lo_now[:, b % 2, :], lo_f[:, bass.ds(g * SLOTS, SLOTS)]).then_inc(lo_copied, 1)
                pool.wait_ge(lo_copied, g + 1)
                for j in mine:
                    wait(pool, counted, g * SLOTS + j - ring_tiles + 1)
                    carry(pool, m.pool_passed)
                    pool.tensor_scalar(hot_lo[:, b * SLOTS + j, :], iota_lo[:, :], lo_now[:, b % 2, j:j + 1],
                                       None, ALU.is_equal).then_inc(lo_hot_pool, 1)
            loop(pool, m, group)

        @block.vector
        def _(dve):
            dve.wait_ge(dst_in, 16)
            dve.tensor_scalar(lo_i[:, :], m.dst_i[:, :], 2, P - 1, ALU.logical_shift_right,
                              ALU.bitwise_and).then_inc(split, 1)
            dve.tensor_scalar(hi_a[:, :], m.dst_i[:, :], 9, 2, ALU.logical_shift_right,
                              ALU.logical_shift_left).then_inc(split, 1)
            dve.tensor_scalar(hi_b[:, :], m.dst_i[:, :], SLOTS - 1, None, ALU.bitwise_and).then_inc(split, 1)
            dve.tensor_copy(m.dst_f[:, :], m.dst_i[:, :]).then_inc(split, 1)
            dve.wait_ge(split, 4)
            dve.tensor_copy(lo_f[:, :], lo_i[:, :]).then_inc(digits, 1)
            dve.tensor_tensor(hi_i[:, :], hi_a[:, :], hi_b[:, :], ALU.bitwise_or).then_inc(split, 1)
            dve.tensor_copy(m.prev_last[:, 1:nt], m.dst_f[:, 0:nt - 1]).then_inc(picked, 1)
            dve.memset(m.prev_last[:, 0:1], -1.0).then_inc(picked, 1)
            dve.wait_ge(split, 5)
            dve.tensor_scalar(hi_f[:, :], hi_i[:, :], float(-(nt // 2)), None, ALU.add).then_inc(digits, 1)
            dve.wait_ge(digits, 2)
            dve.wait_ge(consts, 2)

            def group(it, b):
                g = RING * it + b
                for j in range(SLOTS):
                    t = g * SLOTS + j
                    wait(dve, counted, t - ring_tiles + 1)
                    dve.tensor_scalar(hot_hi[:, b * SLOTS + j, :], iota_hi[:, :], hi_f[:, bass.ds(t, 1)], None,
                                      ALU.is_equal).then_inc(hi_hot, 1)
                    if b * SLOTS + j not in on_pool:
                        dve.tensor_scalar(hot_lo[:, b * SLOTS + j, :], iota_lo[:, :], lo_f[:, bass.ds(t, 1)],
                                          None, ALU.is_equal).then_inc(lo_hot, 1)
            loop(dve, m, group)

            links = [0]

            def link(done):
                links[0] += 1
                done.then_inc(linked, 1)
                dve.wait_ge(linked, links[0])

            dve.wait_ge(prev_in, 16)
            link(dve.tensor_tensor(falls[:, :], prev_i[:, :], m.dst_i[:, :], ALU.is_gt))
            link(dve.tensor_reduce(any_fall[:, :], falls[:, :], AX.X, ALU.max))
            dve.sem_inc(summed, 1)
            dve.wait_ge(counted, nt)
            dve.tensor_scalar(degree[:, :], counts[:, :], 1.0, 1e-12, ALU.add, ALU.max).then_inc(degree_ok, 1)
            link(dve.tensor_copy(cumulated[:, :], counts[:, :]))
            link(dve.tensor_scalar(has_edges[:, :], cumulated[:, :], 1.0, None, ALU.min))
            for j in range(1, SLOTS):
                link(dve.tensor_tensor(by_slot(cumulated)[:, :, j], by_slot(cumulated)[:, :, j],
                                       by_slot(cumulated)[:, :, j - 1], ALU.add))
            dve.sem_inc(summed, 1)
            dve.wait_ge(summed, 3)
            link(dve.tensor_copy(scan[0][:, :], of_group[:, :]))
            at, reach = 0, 1
            while reach < ng:
                link(dve.tensor_copy(scan[1 - at][:, 0:reach], scan[at][:, 0:reach]))
                link(dve.tensor_tensor(scan[1 - at][:, reach:ng], scan[at][:, reach:ng],
                                       scan[at][:, 0:ng - reach], ALU.add))
                at, reach = 1 - at, 2 * reach
            link(dve.tensor_tensor(group_base[:, :], scan[at][:, :], of_group[:, :], ALU.subtract))
            link(dve.tensor_tensor(first_row[:, :], group_base[:, :], in_group[:, :], ALU.add))
            link(dve.tensor_tensor(by_slot(row_a), by_slot(cumulated),
                                   first_row[:, :, None].to_broadcast([P, ng, SLOTS]), ALU.add))
            link(dve.scalar_tensor_tensor(row_b[:, :], row_a[:, :], -1.0 - no_row, has_edges[:, :],
                                          ALU.add, ALU.mult))
            link(dve.tensor_scalar(order[:, :], n_falls[:, :], 0.0, None, ALU.is_equal))
            link(dve.tensor_copy(m.in_order[:, :], order[0:1, :]))
            link(dve.scalar_tensor_tensor(row_a[:, :], row_b[:, :], no_row, node_id[:, :], ALU.add, ALU.subtract))
            link(dve.scalar_tensor_tensor(m.node_row[:, :], row_a[:, :], order[:, :], node_id[:, :],
                                          ALU.mult, ALU.add))
            dve.wait_ge(rooted, 1)
            link(dve.reciprocal(m.dinv[:, :], root[:, :]))

        @block.scalar
        def _(act):
            act.wait_ge(degree_ok, 1)
            act.activation(root[:, :], degree[:, :], ACT.Sqrt).then_inc(rooted, 1)

        @block.tensor
        def _(pe):
            def group(it, b):
                g = RING * it + b
                dve_slots = [k for k in range(ring_tiles) if k not in on_pool]
                for j in range(SLOTS):
                    t, k = g * SLOTS + j, b * SLOTS + j
                    pe.wait_ge(hi_hot, t + 1)
                    slots, ready = (on_pool, lo_hot_pool) if k in on_pool else (dve_slots, lo_hot)
                    pe.wait_ge(ready, it * len(slots) + len([n for n in slots if n <= k]))
                    pe.matmul(counts[:, :], hot_lo[:, k, :], hot_hi[:, k, :],
                              start=isinstance(t, int) and t == 0,
                              stop=isinstance(t, int) and t == nt - 1).then_inc(counted, 1)
            loop(pe, m, group)
            pe.wait_ge(consts, 11)
            pe.wait_ge(summed, 2)
            edges = by_slot(cumulated)[:, :, SLOTS - 1]
            pe.matmul(n_falls[:, :], ones[:, :], any_fall[:, :], start=True, stop=True)
            pe.matmul(in_group[:, :], before[:, :], edges, start=True, stop=True)
            pe.matmul(of_group[:, :], ones[:, :], edges, start=True, stop=True).then_inc(summed, 1)


def transform(nc, m, conv):
    source = grouped(m.x if conv == 0 else m.messages[0], D)
    message_rows = grouped(m.messages[conv], D)
    weights = m.w1 if conv == 0 else m.w2
    with ExitStack() as ctx:
        sb = lambda n, s, d=F32: ctx.enter_context(nc.sbuf_tensor(f"{n}{conv}", s, d))
        new_semaphore = cleared_semaphores(nc, ctx)
        sem = lambda n: new_semaphore(f"{n}{conv}")
        ps = lambda n, s: ctx.enter_context(nc.psum_tensor(f"{n}{conv}", s, F32))
        w = sb("w", [P, KD, D])
        w_hi, w_lo = sb("w_hi", [P, KD, D], F32R), sb("w_lo", [P, KD, D], F32R)
        rows = sb("rows", [P, RING, SLOTS, D])
        cent = sb("cent", [P, 2, SLOTS, D])
        hi, lo = sb("hi", [P, 4, 2, KD, P], F32R), sb("lo", [P, 4, 2, KD, P], F32R)
        out = sb("out", [P, RING, SLOTS, D])
        stats = sb("stats", [P, 2, SLOTS, 6])
        mean_var = sb("mean_var", [P, 2, SLOTS, 2])
        var = sb("var", [P, 2, SLOTS])
        root = sb("root_r", [P, 2, SLOTS])
        safe = sb("safe", [P, 2, SLOTS])
        inverse = sb("inverse", [P, 2, SLOTS])
        factor = sb("factor", [P, RING, SLOTS])
        turned = ps("turned", [P, 4, 2, KD, P])
        product = ps("product", [P, 4, 2, D])
        if conv == 0:
            scale_ok = sem("scale_ok")
        else:
            row_now = sb("row_now", [P, RING, SLOTS], I32)
            squares = sb("squares", [P, SLOTS, D])
            found_in = [sem(f"found_in{b}_") for b in range(RING)]
            row_ok, made_safe, squared = sem("row_ok"), sem("made_safe"), sem("squared")
        w_in, w_split = sem("w_in"), sem("w_split")
        rows_in = [sem(f"rows_in{b}_") for b in range(RING)]
        stored = [sem(f"stored{b}_") for b in range(RING)]
        stats_ok, mean_ok, var_ok, cent_ok = sem("stats_ok"), sem("mean_ok"), sem("var_ok"), sem("cent_ok")
        rooted, inverted, factor_ok = sem("rooted"), sem("inverted"), sem("factor_ok")
        turned_ok, hi_ok, lo_ok, product_ok, out_ok = (
            sem(n) for n in ("turned_ok", "hi_ok", "lo_ok", "product_ok", "out_ok"))
        block = ctx.enter_context(nc.Block())
        place = lambda b, h: (2 * b + h) % 4

        def group_before(it, b):
            return (it, b - 1) if b else (it - 1, RING - 1)

        @block.sync
        def _(sp):
            sp.dma_start(w[:, :, :], weights.rearrange("(k p) n -> p k n", p=P)).then_inc(w_in, 16)

            ahead = RING + conv

            def load(g, b):
                wait(sp, cent_ok, SLOTS * (g - RING + 1))
                sp.dma_start(rows[:, b, :, :], one_group(source, g, D)).then_inc(rows_in[b], 16)

            def group(it, b):
                g = RING * it + b
                later = shifted_group(m, it, b, ahead)
                if later is not None:
                    load(g + ahead, later[1])
                sp.wait_ge(out_ok, 2 * g + 2)
                sp.dma_start(one_group(message_rows, g, D), out[:, b, :, :]).then_inc(stored[b], 16)
            for g in range(ahead):
                load(g, g % RING)
            loop(sp, m, group)
            for b in range(RING):
                sp.wait_ge(stored[b], 16 * slot_uses(m, b))

        @block.vector
        def _(dve):
            dve.wait_ge(w_in, 16)
            dve.tensor_copy(w_hi[:, :, :], w[:, :, :]).then_inc(w_split, 1)
            dve.wait_ge(w_split, 1)
            dve.tensor_tensor(w_lo[:, :, :], w[:, :, :], w_hi[:, :, :].bitcast(F32), ALU.subtract
                              ).then_inc(w_split, 1)

            def rest_of(it, b, h):
                u, k = 2 * (RING * it + b) + h, place(b, h)
                dve.wait_ge(hi_ok, u + 1)
                wait(dve, product_ok, u - 3)
                dve.tensor_tensor(lo[:, k, :, :, :], turned[:, k, :, :, :], hi[:, k, :, :, :].bitcast(F32),
                                  ALU.subtract).then_inc(lo_ok, 1)

            def row_factor(it, b):
                g, c = RING * it + b, b % 2
                wait(dve, out_ok, 2 * (g - 3))
                dve.tensor_tensor(factor[:, b, :], inverse[:, c, :], m.dinv[:, bass.ds(g * SLOTS, SLOTS)],
                                  ALU.mult).then_inc(factor_ok, 1)

            def statistics(it, b):
                g, c = RING * it + b, b % 2
                ring_wait(dve, rows_in, it, b, 16)
                for j in range(SLOTS):
                    dve.bn_stats(stats[:, c, j, :], rows[:, b, j, :]).then_inc(stats_ok, 1)

            def means(it, b):
                g, c = RING * it + b, b % 2
                wait(dve, cent_ok, SLOTS * (g - 1))
                dve.wait_ge(stats_ok, SLOTS * (g + 1))
                carry(dve, m.dve_passed)
                for j in range(SLOTS):
                    dve.bn_aggr(mean_var[:, c, j, :], stats[:, c, j, :]).then_inc(mean_ok, 1)

            def variances(it, b):
                g, c = RING * it + b, b % 2
                dve.wait_ge(mean_ok, SLOTS * (g + 1))
                dve.tensor_scalar(var[:, c, :], mean_var[:, c, :, 1], LN_EPS, None, ALU.add).then_inc(var_ok, 1)

            def invert(it, b):
                g, c = RING * it + b, b % 2
                dve.wait_ge(rooted, g + 1)
                dve.reciprocal(inverse[:, c, :], root[:, c, :]).then_inc(inverted, 1)

            def keep_scale(it, b):
                g, c = RING * it + b, b % 2
                cols = bass.ds(g * SLOTS, SLOTS)
                dve.wait_ge(inverted, g + 1)
                dve.tensor_scalar(m.scale[:, cols], inverse[:, c, :], 1.0, None, ALU.add).then_inc(scale_ok, 1)
                dve.scalar_tensor_tensor(m.shift[:, cols], mean_var[:, c, :, 0], -1.0, inverse[:, c, :],
                                         ALU.mult, ALU.mult).then_inc(scale_ok, 1)
                row_factor(it, b)

            def rows_of(it, b):
                ring_wait(dve, found_in, it, b, 64, uses_back=1)
                dve.tensor_copy(row_now[:, b, :], m.node_row[:, bass.ds((RING * it + b) * SLOTS, SLOTS)]
                                ).then_inc(row_ok, 1)

            def first_result(it, b):
                g, c = RING * it + b, b % 2
                ring_wait(dve, found_in, it, b, 64)
                wait(dve, turned_ok, 2 * (g - 1))
                wait(dve, rooted, g - 1)
                for j in range(SLOTS):
                    dve.scalar_tensor_tensor(cent[:, c, j, :], rows[:, b, j, :],
                                             m.dinv[:, bass.ds(g * SLOTS + j, 1)], m.b1[:, :],
                                             ALU.mult, ALU.add).then_inc(cent_ok, 1)

            def lengths(it, b):
                g, c = RING * it + b, b % 2
                dve.wait_ge(rooted, g + 1)
                dve.tensor_scalar(safe[:, c, :], root[:, c, :], 1e-12, None, ALU.max).then_inc(made_safe, 1)
                dve.wait_ge(made_safe, g + 1)
                dve.reciprocal(inverse[:, c, :], safe[:, c, :]).then_inc(inverted, 1)
                dve.wait_ge(inverted, g + 1)
                row_factor(it, b)


            def group_of_conv0(it, b):
                later, far = shifted_group(m, it, b, 1), shifted_group(m, it, b, 2)
                rest_of(it, b, 1)
                if later is not None:
                    invert(*later)
                if far is not None:
                    statistics(*far)
                if later is not None:
                    rest_of(*later, 0)
                if far is not None:
                    means(*far)
                if later is not None:
                    keep_scale(*later)
                if far is not None:
                    variances(*far)

            def group_of_conv1(it, b):
                later, far = shifted_group(m, it, b, 1), shifted_group(m, it, b, 2)
                rest_of(it, b, 1)
                if shifted_group(m, it, b, RING) is not None:
                    rows_of(*shifted_group(m, it, b, RING))
                lengths(it, b)
                if later is not None:
                    rest_of(*later, 0)
                if far is not None:
                    first_result(*far)

            if conv == 0:
                for b in range(2):
                    for stage in (statistics, means, variances):
                        stage(0, b)
                invert(0, 0)
                keep_scale(0, 0)
            else:
                for b in range(RING):
                    rows_of(0, b)
                for b in range(2):
                    first_result(0, b)
            rest_of(0, 0, 0)
            loop(dve, m, group_of_conv0 if conv == 0 else group_of_conv1)

        @block.gpsimd
        def _(pool):
            if conv == 0:
                def group(it, b):
                    g, c = RING * it + b, b % 2
                    wait(pool, turned_ok, 2 * (g - 1))
                    for j in range(SLOTS):
                        pool.wait_ge(mean_ok, g * SLOTS + j + 1)
                        pool.tensor_tensor(cent[:, c, j, :], rows[:, b, j, :],
                                           mean_var[:, c, j, 0:1].to_broadcast([P, D]), ALU.subtract
                                           ).then_inc(cent_ok, 1)
                loop(pool, m, group)
                return

            def group(it, b):
                g = RING * it + b
                pool.wait_ge(row_ok, g + 1)
                ring_wait(pool, rows_in, it, b, 16)
                carry(pool, m.pool_passed)
                for j in range(SLOTS):
                    pool.indirect_dma_start(
                        out=rows[:, b, j, :], out_offset=None, in_=m.table[0],
                        in_offset=bass.IndirectOffsetOnAxis(ap=row_now[:, b, j:j + 1], axis=0), compute_op=ALU.add
                    ).then_inc(found_in[b], 16)
            loop(pool, m, group)

        @block.scalar
        def _(act):
            def deviations(it, b):
                act.wait_ge(var_ok, RING * it + b + 1)
                act.activation(root[:, b % 2, :], var[:, b % 2, :], ACT.Sqrt).then_inc(rooted, 1)

            def sum_squares(it, b, h):
                g, c = RING * it + b, b % 2
                for j in (2 * h, 2 * h + 1):
                    act.wait_ge(cent_ok, SLOTS * g + j + 1)
                    wait(act, squared, SLOTS * (g - 1) + j + 1)
                    act.activation(squares[:, j, :], cent[:, c, j, :], ACT.Square,
                                   accum_out=var[:, c, j:j + 1]).then_inc(squared, 1)
                if h == 1:
                    act.wait_ge(squared, SLOTS * (g + 1))
                    act.activation(root[:, c, :], var[:, c, :], ACT.Sqrt).then_inc(rooted, 1)

            def copy_turned(it, b, h):
                u, k = 2 * (RING * it + b) + h, place(b, h)
                act.wait_ge(turned_ok, u + 1)
                wait(act, product_ok, u - 3)
                act.activation(hi[:, k, :, :, :], turned[:, k, :, :, :], ACT.Copy).then_inc(hi_ok, 1)

            def scale_product(it, b, h):
                g = RING * it + b
                act.wait_ge(product_ok, 2 * g + h + 1)
                if h == 0:
                    act.wait_ge(factor_ok, g + 1)
                    ring_wait(act, stored, it, b, 16, uses_back=1)
                for j in (2 * h, 2 * h + 1):
                    done = act.activation(out[:, b, j, :], product[:, place(b, h), j % 2, :], ACT.Copy,
                                          scale=factor[:, b, j:j + 1])
                done.then_inc(out_ok, 1)

            def group(it, b):
                later = shifted_group(m, it, b, 1)
                if later is not None:
                    if conv == 0:
                        deviations(*later)
                    copy_turned(*later, 0)
                if not (isinstance(it, int) and it == 0 and b == 0):
                    scale_product(*group_before(it, b), 1)
                if conv == 1 and later is not None:
                    sum_squares(*later, 0)
                if later is not None:
                    copy_turned(*later, 1)
                scale_product(it, b, 0)
                if conv == 1 and later is not None:
                    sum_squares(*later, 1)

            if conv == 0:
                deviations(0, 0)
            else:
                for h in range(2):
                    sum_squares(0, 0, h)
            for h in range(2):
                copy_turned(0, 0, h)
            loop(act, m, group)
            scale_product(m.iters - 1, m.last - 1, 1)

        @block.tensor
        def _(pe):
            pe.wait_ge(w_split, 2)

            def turn(it, b, h):
                u = 2 * (RING * it + b) + h
                pe.wait_ge(cent_ok, 2 * u + 2)
                wait(pe, lo_ok, u - 3)
                for i in range(2):
                    for c in range(KD):
                        done = pe.transpose(turned[:, place(b, h), i, c, :],
                                            cent[:, b % 2, 2 * h + i, c * P:(c + 1) * P], m.ident[:, :])
                done.then_inc(turned_ok, 1)

            def multiply(it, b, h):
                u, k = 2 * (RING * it + b) + h, place(b, h)
                pe.wait_ge(hi_ok, u + 1)
                wait(pe, out_ok, u - 3)
                for i in range(2):
                    for c in range(KD):
                        pe.matmul(product[:, k, i, :], hi[:, k, i, c, :], w_hi[:, c, :], start=c == 0, stop=False)
                        pe.matmul(product[:, k, i, :], hi[:, k, i, c, :], w_lo[:, c, :], start=False, stop=False)
                    if i == 0:
                        pe.wait_ge(lo_ok, u + 1)
                    for c in range(KD):
                        done = pe.matmul(product[:, k, i, :], lo[:, k, i, c, :], w_hi[:, c, :],
                                         start=False, stop=c == KD - 1)
                done.then_inc(product_ok, 1)

            def group(it, b):
                later = shifted_group(m, it, b, 1)
                for h in range(2):
                    if later is not None:
                        turn(*later, h)
                    multiply(it, b, h)
            for h in range(2):
                turn(0, 0, h)
            loop(pe, m, group)


def sum_edges(nc, m, conv):
    in_order = nc.values_load(m.in_order[0:1, 0:1], min_val=0, max_val=1)
    with nc.If(in_order == 1):
        sum_sorted_edges(nc, m, conv)
    with nc.Else():
        sum_any_edges(nc, m, conv)


def sum_sorted_edges(nc, m, conv):
    messages, table = m.messages[conv], m.table[conv]
    with ExitStack() as ctx:
        sb = lambda n, s, d=F32: ctx.enter_context(nc.sbuf_tensor(f"s_{n}{conv}", s, d))
        new_semaphore = cleared_semaphores(nc, ctx)
        sem = lambda n: new_semaphore(f"s_{n}{conv}")
        dst_row = sb("dst_row", [P, RING, GROUP], I32)
        same = sb("same", [P, 2, SLOTS, P])
        same_as_last = sb("same_as_last", [P, 2, SLOTS, P])
        src_now = sb("src_now", [P, RING, SLOTS], I32)
        got = sb("got", [P, RING, SLOTS, D])
        merged = sb("merged", [P, RING, SLOTS, D])
        half_d = D // 2
        half = lambda h: slice(h * half_d, (h + 1) * half_d)
        total = [[ctx.enter_context(nc.psum_tensor(f"s_total{i}_{h}_{conv}", [P, 512], F32)) for h in range(2)]
                 for i in range(SLOTS)]
        row_in = [sem(f"row_in{b}_") for b in range(RING)]
        gathered = [sem(f"gathered{b}_") for b in range(RING)]
        stored = [sem(f"stored{b}_") for b in range(RING)]
        src_ok, same_ok = sem("src_ok"), sem("same_ok")
        total_ok = [sem(f"total_ok{h}_") for h in range(2)]
        merged_ok = [sem(f"merged_ok{h}_") for h in range(2)]
        block = ctx.enter_context(nc.Block())

        @block.sync
        def _(sp):
            def load(g, b):
                wait(sp, same_ok, 2 * SLOTS * (g - RING + 1))
                sp.dma_start(dst_row[:, b, :], m.dst_rows[bass.ds(g, 1), :].to_broadcast([P, GROUP])
                             ).then_inc(row_in[b], 16)

            def group(it, b):
                g = RING * it + b
                later = shifted_group(m, it, b, RING - 1)
                if later is not None:
                    load(g + RING - 1, later[1])
                for h in range(2):
                    sp.wait_ge(merged_ok[h], SLOTS * (g + 1))
                sp.dma_start(edge_group(table, g), merged[:, b, :, :]).then_inc(stored[b], 16)
            for g in range(RING - 1):
                load(g, g)
            loop(sp, m, group)
            for b in range(RING):
                sp.wait_ge(stored[b], 16 * slot_uses(m, b))

        @block.vector
        def _(dve):
            def sources(it, b):
                ring_wait(dve, gathered, it, b, 64, uses_back=1)
                dve.tensor_copy(src_now[:, b, :], m.src_i[:, bass.ds((RING * it + b) * SLOTS, SLOTS)]
                                ).then_inc(src_ok, 1)

            def group(it, b):
                g, c = RING * it + b, b % 2
                ahead = shifted_group(m, it, b, 3)
                if ahead is not None:
                    sources(*ahead)
                ring_wait(dve, row_in, it, b, 16)
                wait(dve, total_ok[1], SLOTS * (g - 1))
                for j in range(SLOTS):
                    col = bass.ds(g * SLOTS + j, 1)
                    for to, of in ((same, m.dst_f), (same_as_last, m.prev_last)):
                        dve.tensor_scalar(to[:, c, j, :], dst_row[:, b, j * P:(j + 1) * P], of[:, col], None,
                                          ALU.is_equal).then_inc(same_ok, 1)
            for i in range(3):
                sources(0, i)
            loop(dve, m, group)

        @block.gpsimd
        def _(pool):
            def group(it, b):
                g = RING * it + b
                pool.wait_ge(src_ok, g + 1)
                wait(pool, total_ok[1], SLOTS * (g - RING + 1))
                carry(pool, m.pool_passed)
                for j in range(SLOTS):
                    pool.indirect_dma_start(
                        out=got[:, b, j, :], out_offset=None, in_=messages,
                        in_offset=bass.IndirectOffsetOnAxis(ap=src_now[:, b, j:j + 1], axis=0)
                    ).then_inc(gathered[b], 16)
            loop(pool, m, group)

        @block.tensor
        def _(pe):
            def own(it, b, j):
                g = RING * it + b
                t = g * SLOTS + j
                if j == 0:
                    ring_wait(pe, gathered, it, b, 64)
                pe.wait_ge(same_ok, 2 * t + 2)
                first = isinstance(t, int) and t == 0
                for h in range(2):
                    wait(pe, merged_ok[h], t - SLOTS + 1)
                    done = pe.matmul(total[j][h][:, 0:half_d], same[:, b % 2, j, :], got[:, b, j, half(h)],
                                     start=True, stop=first)
                    if first:
                        done.then_inc(total_ok[h], 1)

            def carried(it, b, j):
                t = (RING * it + b) * SLOTS + j
                if isinstance(t, int) and t == 0:
                    return
                before = merged[:, b, j - 1, :] if j else merged[:, (b - 1) % RING, SLOTS - 1, :]
                for h in range(2):
                    pe.wait_ge(merged_ok[h], t)
                    pe.matmul(total[j][h][:, 0:half_d], same_as_last[:, b % 2, j, :], before[:, half(h)],
                              start=False, stop=True).then_inc(total_ok[h], 1)

            def group(it, b):
                for j in range(SLOTS):
                    if j + 1 < SLOTS:
                        own(it, b, j + 1)
                    else:
                        later = shifted_group(m, it, b, 1)
                        if later is not None:
                            own(*later, 0)
                    carried(it, b, j)
            own(0, 0, 0)
            loop(pe, m, group)

        @block.scalar
        def _(act):
            def group(it, b):
                ring_wait(act, stored, it, b, 16, uses_back=1)
                for j in range(SLOTS):
                    t = (RING * it + b) * SLOTS + j
                    for h in range(2):
                        act.wait_ge(total_ok[h], t + 1)
                        act.activation(merged[:, b, j, half(h)], total[j][h][:, 0:half_d], ACT.Copy
                                       ).then_inc(merged_ok[h], 1)
            loop(act, m, group)


def sum_any_edges(nc, m, conv):
    first_block = [0, 1, 3, 6]
    messages, table = m.messages[conv], m.table[conv]
    table_rows = grouped(table, D)
    with ExitStack() as ctx:
        sb = lambda n, s, d=F32: ctx.enter_context(nc.sbuf_tensor(f"{n}{conv}", s, d))
        new_semaphore = cleared_semaphores(nc, ctx)
        sem = lambda n: new_semaphore(f"{n}{conv}")
        zeros = sb("any_zeros", [P, SLOTS, D])
        dst_row = sb("dst_row", [P, 2, GROUP], I32)
        same = sb("same", [P, 2, 10, P])
        seen = sb("seen", [P, SLOTS, GROUP])
        n_before = sb("n_before", [P, 2, SLOTS])
        not_owner = sb("not_owner", [P, 2, SLOTS])
        to_spare = sb("to_spare", [P, 2, SLOTS])
        moved = sb("moved", [P, 2, SLOTS])
        target = sb("target", [P, 2, SLOTS], I32)
        src_now = sb("src_now", [P, 2, SLOTS], I32)
        got = sb("got", [P, 2, SLOTS, D])
        merged = sb("merged", [P, 2, SLOTS, D])
        total = ctx.enter_context(nc.psum_tensor(f"total{conv}", [P, 2, SLOTS, D], F32))
        row_in = [sem(f"row_in{b}_") for b in range(2)]
        gathered = [sem(f"gathered{b}_") for b in range(2)]
        added = [sem(f"added{b}_") for b in range(2)]
        src_ok, same_ok, before_ok, spare_ok, moved_ok, target_ok = (
            sem(n) for n in ("src_ok", "same_ok", "before_ok", "spare_ok", "moved_ok", "target_ok"))
        total_ok, merged_ok, zeroed, cleared = sem("total_ok"), sem("merged_ok"), sem("any_zeroed"), sem("cleared")
        block = ctx.enter_context(nc.Block())

        def pairs(engine, pair):
            for b in range(2):
                pair(0, b)
            if m.ng > 4:
                with engine.Fori(1, m.ng // 2 - 1) as i:
                    for b in range(2):
                        pair(i, b)
            for b in range(2):
                pair(m.ng // 2 - 1, b)

        @block.sync
        def _(sp):
            sp.wait_ge(zeroed, 1)
            with sp.Fori(0, m.ng) as g:
                sp.dma_start(one_group(table_rows, g, D), zeros[:, :, :]).then_inc(cleared, 16)

            def pair(i, b):
                g = i * 2 + b
                wait(sp, before_ok, SLOTS * (g - 1))
                sp.dma_start(dst_row[:, b, :], m.dst_rows[bass.ds(g, 1), :].to_broadcast([P, GROUP])
                             ).then_inc(row_in[b], 16)
            pairs(sp, pair)

        @block.vector
        def _(dve):
            def pair(i, b):
                g = i * 2 + b
                cols = bass.ds(g * SLOTS, SLOTS)
                wait(dve, gathered[b], 64 * i)
                dve.tensor_copy(src_now[:, b, :], m.src_i[:, cols]).then_inc(src_ok, 1)
                dve.wait_ge(row_in[b], 16 * (i + 1))
                wait(dve, total_ok, 2 * (g - 1))
                for q in range(SLOTS):
                    f = first_block[q]
                    dve.tensor_scalar(same[:, b, f:f + q + 1, :], dst_row[:, b, 0:(q + 1) * P],
                                      m.dst_f[:, bass.ds(g * SLOTS + q, 1)], None, ALU.is_equal
                                      ).then_inc(same_ok, 1)
                wait(dve, moved_ok, g - 1)
                for q in range(SLOTS):
                    dve.scalar_tensor_tensor(
                        seen[:, q, 0:(q + 1) * P], dst_row[:, b, 0:(q + 1) * P],
                        m.dst_f[:, bass.ds(g * SLOTS + q, 1)],
                        m.earlier[:, (SLOTS - 1 - q) * P:], ALU.is_equal, ALU.mult,
                        accum_out=n_before[:, b, q:q + 1]).then_inc(before_ok, 1)
                dve.tensor_tensor(to_spare[:, b, :], m.spare[:, :], m.dst_f[:, cols], ALU.subtract
                                  ).then_inc(spare_ok, 1)
                dve.wait_ge(before_ok, SLOTS * (g + 1))
                dve.tensor_scalar(not_owner[:, b, :], n_before[:, b, :], 1.0, None, ALU.min
                                  ).then_inc(spare_ok, 1)
                dve.wait_ge(spare_ok, 2 * (g + 1))
                dve.tensor_tensor(moved[:, b, :], not_owner[:, b, :], to_spare[:, b, :], ALU.mult
                                  ).then_inc(moved_ok, 1)
                dve.wait_ge(moved_ok, g + 1)
                wait(dve, added[b], 64 * i)
                dve.tensor_tensor(target[:, b, :], moved[:, b, :], m.dst_f[:, cols], ALU.add
                                  ).then_inc(target_ok, 1)
            pairs(dve, pair)

        @block.gpsimd
        def _(pool):
            pool.memset(zeros[:, :, :], 0.0).then_inc(zeroed, 1)

            def gather(g, b):
                pool.wait_ge(src_ok, g + 1)
                wait(pool, total_ok, 2 * (g - 1))
                carry(pool, m.pool_passed)
                for q in range(SLOTS):
                    pool.indirect_dma_start(
                        out=got[:, b, q, :], out_offset=None, in_=messages,
                        in_offset=bass.IndirectOffsetOnAxis(ap=src_now[:, b, q:q + 1], axis=0)
                    ).then_inc(gathered[b], 16)

            def scatter(i, b):
                g = i * 2 + b
                pool.wait_ge(target_ok, g + 1)
                pool.wait_ge(merged_ok, 2 * g + 2)
                wait(pool, added[1 - b], 64 * (i + b))
                carry(pool, m.pool_passed)
                for q in range(SLOTS):
                    pool.indirect_dma_start(
                        out=table, out_offset=bass.IndirectOffsetOnAxis(ap=target[:, b, q:q + 1], axis=0),
                        in_=merged[:, b, q, :], in_offset=None, compute_op=ALU.add
                    ).then_inc(added[b], 16)

            def pair(i, b):
                g = i * 2 + b
                if not (isinstance(g, int) and g + 1 >= m.ng):
                    gather(g + 1, 1 - b)
                scatter(i, b)
            gather(0, 0)
            pool.wait_ge(cleared, 16 * m.ng)
            pairs(pool, pair)
            for b in range(2):
                pool.wait_ge(added[b], 32 * m.ng)

        @block.tensor
        def _(pe):
            def pair(i, b):
                g = i * 2 + b
                pe.wait_ge(gathered[b], 64 * (i + 1))
                pe.wait_ge(same_ok, SLOTS * (g + 1))
                for h in range(2):
                    wait(pe, merged_ok, 2 * (g - 2) + h + 1)
                    for owner in (2 * h, 2 * h + 1):
                        for q in range(owner, SLOTS):
                            done = pe.matmul(total[:, b, owner, :],
                                             same[:, b, first_block[q] + owner, :], got[:, b, q, :],
                                             start=q == owner, stop=q == SLOTS - 1)
                    done.then_inc(total_ok, 1)
            pairs(pe, pair)

        @block.scalar
        def _(act):
            def pair(i, b):
                g = i * 2 + b
                wait(act, added[b], 64 * i)
                for h in range(2):
                    act.wait_ge(total_ok, 2 * g + h + 1)
                    act.activation(merged[:, b, 2 * h:2 * h + 2, :], total[:, b, 2 * h:2 * h + 2, :],
                                   ACT.Copy).then_inc(merged_ok, 1)
            pairs(act, pair)


def prepare_attention(nc, m):
    with ExitStack() as ctx:
        sb = lambda n, s, d=F32: ctx.enter_context(nc.sbuf_tensor(n, s, d))
        sem = lambda n: ctx.enter_context(nc.semaphore(n))
        wx_t = sb("wx_t", [HD, HEADS, D])
        w_slice = sb("w_slice", [HD, SL])
        bx_t = sb("bx_t", [HD, HEADS])
        b_slice = sb("b_slice", [1, SL])
        temp, clipped, inv_temp = sb("temp", [P, HEADS]), sb("clipped", [P, HEADS]), sb("inv_temp", [P, HEADS])
        bias0, bias = sb("bias0", [1, HS]), sb("bias", [1, HS])
        rest1, rest2 = sb("rest1", [1, HS]), sb("rest2", [1, HS])
        parts = sb("parts", [1, 3, HS], BF16)
        folded = ctx.enter_context(nc.psum_tensor("folded", [P, KD, HS], F32))
        bias_ps = ctx.enter_context(nc.psum_tensor("bias_ps", [1, HS], F32))
        inputs_in, parts_in, step, projected = sem("inputs_in"), sem("parts_in"), sem("step"), sem("projected")
        block = ctx.enter_context(nc.Block())

        @block.sync
        def _(sp):
            sp.dma_start(wx_t[:, :, :], m.wx_t_dram.rearrange("(h c) f -> c h f", c=HD)).then_inc(inputs_in, 16)
            sp.dma_start(w_slice[:, :], m.w_slice_dram).then_inc(inputs_in, 16)
            sp.dma_start(bx_t[:, :], m.bx_t_dram).then_inc(inputs_in, 16)
            sp.dma_start(b_slice[:, :], m.b_slice_dram).then_inc(inputs_in, 16)
            sp.dma_start(temp[:, :], m.temp_dram.partition_broadcast(P)).then_inc(inputs_in, 16)
            sp.wait_ge(step, 9)
            for r in range(3):
                sp.dma_start(m.bias_rows[r:r + 1, :], parts[0:1, r, :]).then_inc(parts_in, 16)
            sp.wait_ge(parts_in, 48)

        @block.gpsimd
        def _(pool):
            pool.memset(m.ones3[:, :], 1.0).then_inc(m.const_ok, 1)
            pool.memset(m.y[:, :, :, D:D + 2], 1.0).then_inc(m.const_ok, 1)
            pool.memset(m.half[:, :], -0.5).then_inc(m.const_ok, 1)
            pool.wait_ge(m.const_ok, 3)

        @block.tensor
        def _(pe):
            pe.wait_ge(inputs_in, 80)
            for c in range(KD):
                for h in range(HEADS):
                    pe.matmul(folded[:, c, h * SL:(h + 1) * SL], wx_t[:, h, c * P:(c + 1) * P],
                              w_slice[:, :], start=True, stop=True)
            for h in range(HEADS):
                done = pe.matmul(bias_ps[:, h * SL:(h + 1) * SL], bx_t[:, h:h + 1], w_slice[:, :],
                                 start=True, stop=True)
            done.then_inc(projected, 1)

        @block.vector
        def _(dve):
            dve.wait_ge(inputs_in, 80)
            dve.tensor_scalar(clipped[:, :], temp[:, :], 0.1, 5.0, ALU.max, ALU.min).then_inc(step, 1)
            dve.wait_ge(step, 1)
            dve.reciprocal(inv_temp[:, :], clipped[:, :]).then_inc(step, 1)
            dve.wait_ge(step, 2)
            dve.wait_ge(projected, 1)
            for c in range(KD):
                dve.tensor_tensor(m.w_logit[:, c, :].rearrange("p (h s) -> p h s", h=HEADS),
                                  folded[:, c, :].rearrange("p (h s) -> p h s", h=HEADS),
                                  inv_temp[:, :, None].to_broadcast([P, HEADS, SL]), ALU.mult
                                  ).then_inc(projected, 1)
            heads = lambda a: a[:, :].rearrange("p (h s) -> p h s", h=HEADS)
            dve.tensor_tensor(heads(bias0), heads(bias_ps),
                              b_slice[:, None, :].to_broadcast([1, HEADS, SL]), ALU.add).then_inc(step, 1)
            dve.wait_ge(step, 3)
            dve.tensor_tensor(heads(bias), heads(bias0),
                              inv_temp[0:1, :, None].to_broadcast([1, HEADS, SL]), ALU.mult).then_inc(step, 1)
            dve.wait_ge(step, 4)
            dve.tensor_copy(parts[:, 0, :], bias[:, :]).then_inc(step, 1)
            dve.wait_ge(step, 5)
            dve.tensor_tensor(rest1[:, :], bias[:, :], parts[:, 0, :], ALU.subtract).then_inc(step, 1)
            dve.wait_ge(step, 6)
            dve.tensor_copy(parts[:, 1, :], rest1[:, :]).then_inc(step, 1)
            dve.wait_ge(step, 7)
            dve.tensor_tensor(rest2[:, :], rest1[:, :], parts[:, 1, :], ALU.subtract).then_inc(step, 1)
            dve.wait_ge(step, 8)
            dve.tensor_copy(parts[:, 2, :], rest2[:, :]).then_inc(step, 1)
            dve.wait_ge(projected, 3)
            dve.tensor_copy(m.w_hi[:, :, :], m.w_logit[:, :, :]).then_inc(projected, 1)
            dve.wait_ge(projected, 4)
            dve.tensor_tensor(m.w_lo[:, :, :], m.w_logit[:, :, :], m.w_hi[:, :, :].bitcast(F32), ALU.subtract
                              ).then_inc(projected, 1)
            dve.wait_ge(projected, 5)


def attend_tokens(nc, m):
    last_rows = (m.n - (m.ng - 1) * GROUP) // SLOTS
    message_rows, x_rows = grouped(m.messages[1], D), grouped(m.x, D)
    x1_dram, weights_dram = grouped(m.x1, D), grouped(m.slice_weights, HS)
    with ExitStack() as ctx:
        sb = lambda n, s, d=F32: ctx.enter_context(nc.sbuf_tensor(n, s, d))
        sem = lambda n: ctx.enter_context(nc.semaphore(n))
        ps = lambda n, s: ctx.enter_context(nc.psum_tensor(n, s, F32))
        message = sb("message", [P, RING, SLOTS, D])
        base = sb("a_base", [P, RING, SLOTS, D])
        row_now = sb("a_row_now", [P, RING, SLOTS], I32)
        x1 = sb("x1_now", [P, 2, SLOTS, D])
        stats = sb("a_stats", [P, 2, SLOTS, 6])
        mean_var = sb("a_mean_var", [P, 2, SLOTS, 2])
        var, rstd = sb("a_var", [P, 2, SLOTS]), sb("a_rstd", [P, 2, SLOTS])
        y_hi, y_lo = sb("y_hi", [P, 2, KD, P], F32R), sb("y_lo", [P, 2, KD, P], F32R)
        mean_shift = sb("a_mean_shift", [P, 2, SLOTS])
        shifted = sb("shifted", [P, 2, WIDE * SL])
        expd = sb("expd", [P, 2, HS])
        neg_top, total, inv_total = sb("neg_top", [P, 2, HEADS]), sb("total", [P, 2, HEADS]), sb("inv_total", [P, 2, HEADS])
        weights = sb("weights", [P, RING, SLOTS, HS])
        turned = [ps(f"y_turned{i}", [P, KD, P]) for i in range(2)]
        logits = [ps(f"logits{i}", [P, HS]) for i in range(2)]
        rows_in = [sem(f"a_rows_in{b}") for b in range(RING)]
        found_in = [sem(f"a_found_in{b}") for b in range(RING)]
        x1_stored = [sem(f"x1_stored{b}") for b in range(2)]
        w_stored = [sem(f"w_stored{b}") for b in range(RING)]
        row_ok, scaled_ok, base_ok, x1_ok, stats_ok, mean_ok, var_ok, rstd_ok, mean_shift_ok, y_ok = (
            sem("a_" + n) for n in ("row_ok", "scaled_ok", "base_ok", "x1_ok", "stats_ok", "mean_ok",
                                    "var_ok", "rstd_ok", "mean_shift_ok", "y_ok"))
        turned_ok, hi_ok, lo_ok, logits_ok, top_ok, shifted_ok, exp_ok, total_ok, inv_ok, weights_ok, tokens_ok = (
            sem("a_" + n) for n in ("turned_ok", "hi_ok", "lo_ok", "logits_ok", "top_ok", "shifted_ok", "exp_ok",
                                    "total_ok", "inv_ok", "weights_ok", "tokens_ok"))
        block = ctx.enter_context(nc.Block())
        heads = lambda a: a.rearrange("p (h s) -> p h s", s=SL)
        per_head = lambda a: a[:, :, None].to_broadcast([P, a.shape[1], SL])

        def steps(engine, step):
            def group(it, b):
                for j in range(SLOTS):
                    step(it, b, j)
            loop(engine, m, group)

        def tile_before(it, b, j, by):
            k = b * SLOTS + j - by
            return (it, k // SLOTS, k % SLOTS) if k >= 0 else (it - 1, RING - 1, SLOTS + k)

        def tile_after(it, b, j, by):
            later = shifted_group(m, it, b, (j + by) // SLOTS)
            return None if later is None else (*later, (j + by) % SLOTS)

        number = lambda it, b, j: (RING * it + b) * SLOTS + j

        @block.sync
        def _(sp):
            def load(g, b):
                wait(sp, x1_ok, SLOTS * (g - RING + 1))
                sp.dma_start(message[:, b, :, :], one_group(message_rows, g, D)).then_inc(rows_in[b], 16)
                sp.dma_start(base[:, b, :, :], one_group(x_rows, g, D)).then_inc(rows_in[b], 16)

            def group(it, b):
                g = RING * it + b
                sp.wait_ge(x1_ok, SLOTS * (g + 1))
                sp.dma_start(one_group(x1_dram, g, D), x1[:, b % 2, :, :]).then_inc(x1_stored[b % 2], 16)
                if shifted_group(m, it, b, RING) is not None:
                    load(g + RING, b)
                sp.wait_ge(weights_ok, SLOTS * (g + 1))
                sp.dma_start(one_group(weights_dram, g, HS), weights[:, b, :, :]).then_inc(w_stored[b], 16)
            for g in range(RING):
                load(g, g)
            loop(sp, m, group)
            for b in range(2):
                sp.wait_ge(x1_stored[b], 8 * m.ng)
            for b in range(RING):
                sp.wait_ge(w_stored[b], 16 * slot_uses(m, b))

        @block.scalar
        def _(act):
            def copy_turned(t, par):
                act.wait_ge(turned_ok, t + 1)
                wait(act, logits_ok, t - 1)
                act.activation(y_hi[:, par, :, :], turned[par][:, :, :], ACT.Copy).then_inc(hi_ok, 1)

            def scale_x(it, b, j):
                t = number(it, b, j)
                if j == 0:
                    ring_wait(act, rows_in, it, b, 32)
                act.activation(base[:, b, j, :], base[:, b, j, :], ACT.Identity, bias=m.shift[:, bass.ds(t, 1)],
                               scale=m.scale[:, bass.ds(t, 1)]).then_inc(scaled_ok, 1)

            def make_y(it, b, j):
                t, c = number(it, b, j), b % 2
                act.wait_ge(mean_shift_ok, t + 1)
                wait(act, tokens_ok, t - 2 * SLOTS + 1)
                act.activation(m.y[:, c, j, 0:D], x1[:, c, j, :], ACT.Identity,
                               bias=mean_shift[:, c, j:j + 1], scale=rstd[:, c, j:j + 1]).then_inc(y_ok, 1)

            def step(it, b, j):
                t = number(it, b, j)
                later = tile_after(it, b, j, 3)
                if later is not None:
                    make_y(*later)
                if not (isinstance(t, int) and t >= m.nt - 2):
                    copy_turned(t + 2, j % 2)
                act.wait_ge(shifted_ok, t + 1)
                wait(act, inv_ok, t - 1)
                wait(act, weights_ok, t - 1)
                act.activation(expd[:, j % 2, 0:WIDE * SL], shifted[:, j % 2, :], ACT.Exp)
                for h in range(WIDE, HEADS):
                    done = act.activation(expd[:, j % 2, h * SL:(h + 1) * SL], logits[j % 2][:, h * SL:(h + 1) * SL],
                                          ACT.Exp, bias=neg_top[:, j % 2, h:h + 1],
                                          accum_out=total[:, j % 2, h:h + 1])
                done.then_inc(exp_ok, 1)
                far = tile_after(it, b, j, 6)
                if far is not None:
                    scale_x(*far)

            for k in range(6):
                scale_x(0, k // SLOTS, k % SLOTS)
            for j in range(3):
                make_y(0, 0, j)
            copy_turned(0, 0)
            copy_turned(1, 1)
            steps(act, step)

        @block.gpsimd
        def _(pool):
            def find(it, b, j):
                g = RING * it + b
                if j == 0:
                    pool.wait_ge(row_ok, g + 1)
                    ring_wait(pool, rows_in, it, b, 32)
                    carry(pool, m.pool_passed)
                pool.indirect_dma_start(
                    out=message[:, b, j, :], out_offset=None, in_=m.table[1],
                    in_offset=bass.IndirectOffsetOnAxis(ap=row_now[:, b, j:j + 1], axis=0), compute_op=ALU.add
                ).then_inc(found_in[b], 16)

            def make_rstd(it, b, j):
                pool.wait_ge(var_ok, number(it, b, j) + 1)
                pool.tensor_tensor(rstd[:, b % 2, j:j + 1], var[:, b % 2, j:j + 1], m.half[:, :], ALU.pow
                                   ).then_inc(rstd_ok, 1)

            def add_b2(it, b, j):
                pool.wait_ge(scaled_ok, number(it, b, j) + 1)
                pool.tensor_tensor(base[:, b, j, :], base[:, b, j, :], m.b2[:, :], ALU.add).then_inc(base_ok, 1)

            def normalise(it, b, j):
                t = number(it, b, j)
                pool.wait_ge(inv_ok, t + 1)
                wait(pool, tokens_ok, t - SLOTS * RING + 1)
                if j == 0:
                    ring_wait(pool, w_stored, it, b, 16, uses_back=1)
                pool.tensor_tensor(heads(weights[:, b, j, :]), heads(expd[:, j % 2, :]),
                                   per_head(inv_total[:, j % 2, :]), ALU.mult).then_inc(weights_ok, 1)

            def step(it, b, j):
                t = number(it, b, j)
                nxt, far = shifted_group(m, it, b, 1), shifted_group(m, it, b, 3)
                if far is not None:
                    find(*far, j)
                coming = tile_after(it, b, j, 5)
                if coming is not None:
                    add_b2(*coming)
                if nxt is not None:
                    make_rstd(*nxt, j)
                if not (isinstance(t, int) and t == 0):
                    normalise(*tile_before(it, b, j, 1))

            for b in range(3):
                for j in range(SLOTS):
                    find(0, b, j)
            for k in range(5):
                add_b2(0, k // SLOTS, k % SLOTS)
            for j in range(SLOTS):
                make_rstd(0, 0, j)
            steps(pool, step)
            normalise(m.iters - 1, m.last - 1, SLOTS - 1)

        @block.vector
        def _(dve):
            def rows_of(it, b):
                ring_wait(dve, found_in, it, b, 64, uses_back=1)
                dve.tensor_copy(row_now[:, b, :], m.node_row[:, bass.ds((RING * it + b) * SLOTS, SLOTS)]
                                ).then_inc(row_ok, 1)

            def make_x1(it, b, j):
                t, c = number(it, b, j), b % 2
                if j == 0:
                    wait(dve, x1_stored[c], 16 * (RING // 2 * it + b // 2))
                    ring_wait(dve, found_in, it, b, 64)
                dve.wait_ge(base_ok, t + 1)
                wait(dve, y_ok, t - 2 * SLOTS + 1)
                dve.scalar_tensor_tensor(x1[:, c, j, :], message[:, b, j, :], m.dinv[:, bass.ds(t, 1)],
                                         base[:, b, j, :], ALU.mult, ALU.add).then_inc(x1_ok, 1)

            def make_stats(it, b, j):
                dve.wait_ge(x1_ok, number(it, b, j) + 1)
                dve.bn_stats(stats[:, b % 2, j, :], x1[:, b % 2, j, :]).then_inc(stats_ok, 1)

            def make_mean(it, b, j):
                dve.wait_ge(stats_ok, number(it, b, j) + 1)
                carry(dve, m.dve_passed)
                dve.bn_aggr(mean_var[:, b % 2, j, :], stats[:, b % 2, j, :]).then_inc(mean_ok, 1)

            def make_var(it, b, j):
                dve.wait_ge(mean_ok, number(it, b, j) + 1)
                dve.tensor_scalar(var[:, b % 2, j:j + 1], mean_var[:, b % 2, j, 1:2], LN_EPS, None, ALU.add
                                  ).then_inc(var_ok, 1)

            def make_mean_shift(it, b, j):
                c = b % 2
                dve.wait_ge(rstd_ok, number(it, b, j) + 1)
                dve.scalar_tensor_tensor(mean_shift[:, c, j:j + 1], mean_var[:, c, j, 0:1], -1.0,
                                         rstd[:, c, j:j + 1], ALU.mult, ALU.mult).then_inc(mean_shift_ok, 1)

            def rest_of(t, par):
                dve.wait_ge(hi_ok, t + 1)
                wait(dve, logits_ok, t - 1)
                dve.tensor_tensor(y_lo[:, par, :, :], turned[par][:, :, :], y_hi[:, par, :, :].bitcast(F32),
                                  ALU.subtract).then_inc(lo_ok, 1)

            def make_total(t, par):
                dve.wait_ge(exp_ok, t + 1)
                dve.tensor_reduce(total[:, par, 0:WIDE], heads(expd[:, par, 0:WIDE * SL]), AX.X, ALU.add
                                  ).then_inc(total_ok, 1)

            def make_inverse(t, par):
                dve.wait_ge(total_ok, t + 1)
                wait(dve, weights_ok, t - 1)
                dve.reciprocal(inv_total[:, par, :], total[:, par, :]).then_inc(inv_ok, 1)

            def make_top(t, par):
                dve.wait_ge(logits_ok, t + 1)
                wait(dve, exp_ok, t - 1)
                dve.tensor_reduce(neg_top[:, par, :], heads(logits[par][:, :]), AX.X, ALU.max, negate=True
                                  ).then_inc(top_ok, 1)

            def shift_logits(t, par):
                dve.wait_ge(top_ok, t + 1)
                dve.tensor_tensor(heads(shifted[:, par, :]), heads(logits[par][:, 0:WIDE * SL]),
                                  per_head(neg_top[:, par, 0:WIDE]), ALU.add).then_inc(shifted_ok, 1)

            def step(it, b, j):
                t, par = number(it, b, j), j % 2
                first, last = isinstance(t, int) and t == 0, isinstance(t, int) and t == m.nt - 1
                later, far = tile_after(it, b, j, 3), tile_after(it, b, j, SLOTS)
                if j == 0:
                    farther = shifted_group(m, it, b, RING)
                    if farther is not None:
                        rows_of(*farther)
                if far is not None:
                    make_x1(*far)
                if not last:
                    rest_of(t + 1, 1 - par)
                if far is not None:
                    make_stats(*far)
                if later is not None:
                    make_mean_shift(*later)
                if far is not None:
                    make_mean(*far)
                make_top(t, par)
                if far is not None:
                    make_var(*far)
                if not first:
                    make_total(t - 1, 1 - par)
                shift_logits(t, par)
                if not first:
                    make_inverse(t - 1, 1 - par)

            for b in range(RING):
                rows_of(0, b)
            for stage in (make_x1, make_stats, make_mean, make_var):
                for j in range(SLOTS):
                    stage(0, 0, j)
            for j in range(3):
                make_mean_shift(0, 0, j)
            rest_of(0, 0)
            steps(dve, step)
            make_total(m.nt - 1, 1)
            make_inverse(m.nt - 1, 1)

        @block.tensor
        def _(pe):
            def turn(it, b, j):
                t = number(it, b, j)
                pe.wait_ge(y_ok, t + 1)
                wait(pe, lo_ok, t - 1)
                for c in range(KD):
                    done = pe.transpose(turned[j % 2][:, c, :], m.y[:, b % 2, j, c * P:(c + 1) * P], m.ident[:, :])
                done.then_inc(turned_ok, 1)

            def project(t, par):
                wait(pe, exp_ok, t - 1)
                pe.matmul(logits[par][:, :], m.ones3[:, :], m.bias_rows[:, :], start=True, stop=False)
                pe.wait_ge(hi_ok, t + 1)
                for c in range(KD):
                    pe.matmul(logits[par][:, :], y_hi[:, par, c, :], m.w_hi[:, c, :], start=False, stop=False)
                    pe.matmul(logits[par][:, :], y_hi[:, par, c, :], m.w_lo[:, c, :], start=False, stop=False)
                pe.wait_ge(lo_ok, t + 1)
                for c in range(KD):
                    done = pe.matmul(logits[par][:, :], y_lo[:, par, c, :], m.w_hi[:, c, :],
                                     start=False, stop=c == KD - 1)
                done.then_inc(logits_ok, 1)

            def add_tokens(it, b, j):
                t = number(it, b, j)
                pe.wait_ge(weights_ok, t + 1)
                at = t if isinstance(t, int) else None
                rows = last_rows if at is not None and at >= m.nt - SLOTS else P
                for c in range(CH):
                    done = pe.matmul(m.tokens[c][:, :], weights[0:rows, b, j, c * P:(c + 1) * P],
                                     m.y[0:rows, b % 2, j, 0:D + 1], start=at == 0, stop=at == m.nt - 1)
                done.then_inc(tokens_ok, 1)

            def step(it, b, j):
                t = number(it, b, j)
                at = t if isinstance(t, int) else None
                project(t, j % 2)
                if at is None or at < m.nt - 2:
                    turn(*((it, b, j + 2) if j + 2 < SLOTS else (*shifted_group(m, it, b, 1), j + 2 - SLOTS)))
                if at is None or at >= 3:
                    add_tokens(*tile_before(it, b, j, 3))

            turn(0, 0, 0)
            turn(0, 0, 1)
            steps(pe, step)
            for j in range(1, SLOTS):
                add_tokens(m.iters - 1, m.last - 1, j)


def mix_tokens(nc, m):
    with ExitStack() as ctx:
        sb = lambda n, s, d=F32: ctx.enter_context(nc.sbuf_tensor(n, s, d))
        sem = lambda n: ctx.enter_context(nc.semaphore(n))
        ps = lambda n, s: ctx.enter_context(nc.psum_tensor(n, s, F32))
        w_fx, b_fx = sb("w_fx", [P, KD, HEADS * HD]), sb("b_fx", [1, HEADS * HD])
        w_q, w_k, w_v = sb("w_q", [HD, HD]), sb("w_k", [HD, HD]), sb("w_v", [HD, HD])
        w_out = sb("w_out", [HD, HEADS, D])
        safe, inv = sb("m_safe", [P, CH]), sb("m_inv", [P, CH])
        mean_y = sb("mean_y", [P, CH, D + 1])
        mean_t, share = sb("mean_t", [P, KD, HS]), sb("share", [1, HS])
        token_t = sb("token_t", [HD, HS])
        q_t, k_t, v = sb("q_t", [HD, HS]), sb("k_t", [HD, HS]), sb("v", [SL, HS])
        top, total, inv_total = sb("m_top", [SL, HEADS]), sb("m_total", [SL, HEADS]), sb("m_inv_total", [SL, HEADS])
        shifted, expd, probs, probs_t = (sb(n, [SL, HS]) for n in ("m_shifted", "m_expd", "probs", "probs_t"))
        out_t = sb("out_t", [HD, HEADS, P])
        bank = [ps(f"mix{i}", [P, HS]) for i in range(4)]
        inputs_in, zero_ok, step, made = sem("m_inputs_in"), sem("m_zero_ok"), sem("m_step"), sem("m_made")
        exp_ok = sem("m_exp_ok")
        block = ctx.enter_context(nc.Block())
        heads = lambda a: a.rearrange("p (h s) -> p h s", h=HEADS)
        per_head = lambda a: a[:, :, None].to_broadcast([SL, HEADS, SL])
        head = lambda h: slice(h * SL, (h + 1) * SL)

        @block.sync
        def _(sp):
            sp.dma_start(w_fx[:, :, :], m.w_fx_dram.rearrange("(k p) n -> p k n", p=P)).then_inc(inputs_in, 16)
            sp.dma_start(b_fx[:, :], m.b_fx_dram).then_inc(inputs_in, 16)
            for to, of in ((w_q, m.w_q_dram), (w_k, m.w_k_dram), (w_v, m.w_v_dram)):
                sp.dma_start(to[:, :], of).then_inc(inputs_in, 16)
            sp.dma_start(w_out[:, :, :], m.w_out_dram.rearrange("(h c) n -> c h n", c=HD)).then_inc(inputs_in, 16)

        @block.gpsimd
        def _(pool):
            pool.memset(out_t[:, :, :], 0.0).then_inc(zero_ok, 1)

        @block.tensor
        def _(pe):
            pe.wait_ge(inputs_in, 96)
            pe.wait_ge(step, 6)
            for c in range(CH):
                for k in range(KD):
                    pe.transpose(bank[k][:, c * P:(c + 1) * P], mean_y[:, c, k * P:(k + 1) * P], m.ident[:, :])
                done = pe.transpose(bank[2][0:1, c * P:(c + 1) * P], mean_y[:, c, D:D + 1], m.ident[:, :])
            done.then_inc(made, 1)
            pe.wait_ge(step, 9)
            for h in range(HEADS):
                for k in range(KD):
                    pe.matmul(bank[3][0:HD, head(h)], w_fx[:, k, head(h)], mean_t[:, k, head(h)],
                              start=k == 0, stop=False)
                done = pe.matmul(bank[3][0:HD, head(h)], b_fx[:, head(h)], share[:, head(h)],
                                 start=False, stop=True)
            done.then_inc(made, 1)
            pe.wait_ge(step, 10)
            pe.matmul(bank[0][0:HD, :], w_q[:, :], token_t[:, :], start=True, stop=True)
            pe.matmul(bank[1][0:HD, :], w_k[:, :], token_t[:, :], start=True, stop=True)
            for h in range(HEADS):
                done = pe.matmul(bank[2][0:SL, head(h)], token_t[:, head(h)], w_v[:, :], start=True, stop=True)
            done.then_inc(made, 1)
            pe.wait_ge(step, 13)
            for h in range(HEADS):
                done = pe.matmul(bank[3][0:SL, head(h)], q_t[:, head(h)], k_t[:, head(h)], start=True, stop=True)
            done.then_inc(made, 1)
            pe.wait_ge(step, 18)
            for h in range(HEADS):
                done = pe.transpose(bank[0][0:SL, head(h)], probs[:, head(h)], m.ident[0:SL, 0:SL])
            done.then_inc(made, 1)
            pe.wait_ge(step, 19)
            for h in range(HEADS):
                done = pe.matmul(bank[1][0:HD, head(h)], v[:, head(h)], probs_t[:, head(h)], start=True, stop=True)
            done.then_inc(made, 1)
            pe.wait_ge(step, 21)
            for c in range(CH):
                half = slice(c % 2 * D, (c % 2 + 1) * D)
                pe.matmul(bank[2 + c // 2][:, half], out_t[:, 2 * c, :], w_out[:, 2 * c, :], start=True, stop=False)
                done = pe.matmul(bank[2 + c // 2][:, half], out_t[:, 2 * c + 1, :], w_out[:, 2 * c + 1, :],
                                 start=False, stop=True)
            done.then_inc(made, 1)

        @block.scalar
        def _(act):
            act.wait_ge(step, 15)
            act.activation(expd[:, :], shifted[:, :], ACT.Exp, scale=float(HD) ** -0.5).then_inc(exp_ok, 1)

        @block.vector
        def _(dve):
            for c in range(CH):
                last = dve.tensor_scalar(safe[:, c:c + 1], m.tokens[c][:, D:D + 1], TOKEN_EPS, None, ALU.add)
            last.then_inc(step, 1)
            dve.wait_ge(step, 1)
            dve.reciprocal(inv[:, :], safe[:, :]).then_inc(step, 1)
            dve.wait_ge(step, 2)
            for c in range(CH):
                dve.tensor_scalar(mean_y[:, c, :], m.tokens[c][:, :], inv[:, c:c + 1], None, ALU.mult
                                  ).then_inc(step, 1)
            dve.wait_ge(made, 1)
            for k in range(KD):
                dve.tensor_copy(mean_t[:, k, :], bank[k][:, :]).then_inc(step, 1)
            dve.tensor_copy(share[:, :], bank[2][0:1, :]).then_inc(step, 1)
            dve.wait_ge(made, 2)
            dve.tensor_copy(token_t[:, :], bank[3][0:HD, :]).then_inc(step, 1)
            dve.wait_ge(made, 3)
            for n, to in enumerate((q_t, k_t, v)):
                dve.tensor_copy(to[:, :], bank[n][0:HD, :]).then_inc(step, 1)
            dve.wait_ge(made, 4)
            dve.tensor_reduce(top[:, :], heads(bank[3][0:SL, :]), AX.X, ALU.max).then_inc(step, 1)
            dve.wait_ge(step, 14)
            dve.tensor_tensor(heads(shifted[:, :]), heads(bank[3][0:SL, :]), per_head(top[:, :]),
                              ALU.subtract).then_inc(step, 1)
            dve.wait_ge(exp_ok, 1)
            dve.tensor_reduce(total[:, :], heads(expd[:, :]), AX.X, ALU.add).then_inc(step, 1)
            dve.wait_ge(step, 16)
            dve.reciprocal(inv_total[:, :], total[:, :]).then_inc(step, 1)
            dve.wait_ge(step, 17)
            dve.tensor_tensor(heads(probs[:, :]), heads(expd[:, :]), per_head(inv_total[:, :]),
                              ALU.mult).then_inc(step, 1)
            dve.wait_ge(made, 5)
            dve.tensor_copy(probs_t[:, :], bank[0][0:SL, :]).then_inc(step, 1)
            dve.wait_ge(made, 6)
            dve.wait_ge(zero_ok, 1)
            outs = bank[1][0:HD, :].rearrange("p (c a s) -> p c a s", a=2, s=SL)
            slots = out_t[:, :, :].rearrange("p (c a) s -> p c a s", a=2)
            for a in range(2):
                dve.tensor_copy(slots[:, :, a, a * SL:(a + 1) * SL], outs[:, :, a, :]).then_inc(step, 1)
            dve.wait_ge(made, 7)
            for n in range(2):
                dve.tensor_copy(m.mixed[:, 2 * n:2 * n + 2, :],
                                bank[2 + n][:, :].rearrange("p (c n) -> p c n", c=2)).then_inc(step, 1)
            dve.wait_ge(step, 23)


def write_output(nc, m):
    weights_dram, x1_dram, out_dram = grouped(m.slice_weights, HS), grouped(m.x1, D), grouped(m.out, D)
    with ExitStack() as ctx:
        sb = lambda n, s, d=F32: ctx.enter_context(nc.sbuf_tensor(n, s, d))
        sem = lambda n: ctx.enter_context(nc.semaphore(n))
        weights = sb("o_weights", [P, RING, SLOTS, HS])
        x1, out = (sb(n, [P, RING, SLOTS, D]) for n in ("o_x1", "o_out"))
        base = sb("o_base", [P, 2, SLOTS, D])
        hi, lo = sb("o_hi", [P, 2, CH, P], F32R), sb("o_lo", [P, 2, CH, P], F32R)
        mixed_hi, mixed_lo = sb("mixed_hi", [P, CH, D], F32R), sb("mixed_lo", [P, CH, D], F32R)
        turned = [ctx.enter_context(nc.psum_tensor(f"o_turned{i}", [P, CH, P], F32)) for i in range(2)]
        product = [ctx.enter_context(nc.psum_tensor(f"o_product{i}", [P, D], F32)) for i in range(2)]
        rows_in = [sem(f"o_rows_in{b}") for b in range(RING)]
        stored = [sem(f"o_stored{b}") for b in range(RING)]
        turned_ok, hi_ok, lo_ok, product_ok, base_ok, out_ok, split = (
            sem("o_" + n) for n in ("turned_ok", "hi_ok", "lo_ok", "product_ok", "base_ok", "out_ok", "split"))
        block = ctx.enter_context(nc.Block())

        def steps(engine, step):
            def group(it, b):
                for j in range(SLOTS):
                    step(it, b, j, (RING * it + b) * SLOTS + j)
            loop(engine, m, group)

        @block.sync
        def _(sp):
            def load(g, b):
                wait(sp, turned_ok, SLOTS * (g - RING + 1))
                wait(sp, base_ok, SLOTS * (g - RING + 1))
                sp.dma_start(weights[:, b, :, :], one_group(weights_dram, g, HS)).then_inc(rows_in[b], 16)
                sp.dma_start(x1[:, b, :, :], one_group(x1_dram, g, D)).then_inc(rows_in[b], 16)

            def group(it, b):
                g = RING * it + b
                later = shifted_group(m, it, b, RING - 1)
                if later is not None:
                    load(g + RING - 1, later[1])
                sp.wait_ge(out_ok, SLOTS * (g + 1))
                sp.dma_start(one_group(out_dram, g, D), out[:, b, :, :]).then_inc(stored[b], 16)
            for g in range(RING - 1):
                load(g, g)
            loop(sp, m, group)
            for b in range(RING):
                sp.wait_ge(stored[b], 16 * slot_uses(m, b))

        @block.tensor
        def _(pe):
            pe.wait_ge(split, 2)

            def multiply(t, par):
                pe.wait_ge(hi_ok, t + 1)
                wait(pe, out_ok, t - 1)
                for c in range(CH):
                    pe.matmul(product[par][:, :], hi[:, par, c, :], mixed_hi[:, c, :], start=c == 0, stop=False)
                    pe.matmul(product[par][:, :], hi[:, par, c, :], mixed_lo[:, c, :], start=False, stop=False)
                pe.wait_ge(lo_ok, t + 1)
                for c in range(CH):
                    done = pe.matmul(product[par][:, :], lo[:, par, c, :], mixed_hi[:, c, :],
                                     start=False, stop=c == CH - 1)
                done.then_inc(product_ok, 1)

            def step(it, b, j, t):
                if j == 0:
                    ring_wait(pe, rows_in, it, b, 32)
                wait(pe, lo_ok, t - 1)
                for c in range(CH):
                    done = pe.transpose(turned[j % 2][:, c, :], weights[:, b, j, c * P:(c + 1) * P], m.ident[:, :])
                done.then_inc(turned_ok, 1)
                if not (isinstance(t, int) and t == 0):
                    multiply(t - 1, (j - 1) % 2)
            steps(pe, step)
            multiply(m.nt - 1, 1)

        @block.scalar
        def _(act):
            def step(it, b, j, t):
                act.wait_ge(turned_ok, t + 1)
                wait(act, product_ok, t - 1)
                act.activation(hi[:, j % 2, :, :], turned[j % 2][:, :, :], ACT.Copy).then_inc(hi_ok, 1)
            steps(act, step)

        @block.gpsimd
        def _(pool):
            def step(it, b, j, t):
                if j == 0:
                    ring_wait(pool, rows_in, it, b, 32)
                    wait(pool, out_ok, t - SLOTS)
                pool.tensor_tensor(base[:, b % 2, j, :], x1[:, b, j, :], m.b_out[:, :], ALU.add).then_inc(base_ok, 1)
            steps(pool, step)

        @block.vector
        def _(dve):
            dve.tensor_copy(mixed_hi[:, :, :], m.mixed[:, :, :]).then_inc(split, 1)
            dve.wait_ge(split, 1)
            dve.tensor_tensor(mixed_lo[:, :, :], m.mixed[:, :, :], mixed_hi[:, :, :].bitcast(F32), ALU.subtract
                              ).then_inc(split, 1)

            def finish(it, b, j, t):
                if j == 0:
                    ring_wait(dve, stored, it, b, 16, uses_back=1)
                dve.wait_ge(product_ok, t + 1)
                dve.wait_ge(base_ok, t + 1)
                dve.tensor_tensor(out[:, b, j, :], product[j % 2][:, :], base[:, b % 2, j, :], ALU.add
                                  ).then_inc(out_ok, 1)

            def step(it, b, j, t):
                dve.wait_ge(hi_ok, t + 1)
                wait(dve, product_ok, t - 1)
                dve.tensor_tensor(lo[:, j % 2, :, :], turned[j % 2][:, :, :], hi[:, j % 2, :, :].bitcast(F32),
                                  ALU.subtract).then_inc(lo_ok, 1)
                if not (isinstance(t, int) and t == 0):
                    if j:
                        finish(it, b, j - 1, t - 1)
                    elif b:
                        finish(it, b - 1, SLOTS - 1, t - 1)
                    else:
                        finish(it - 1, RING - 1, SLOTS - 1, t - 1)
            steps(dve, step)
            finish(m.iters - 1, m.last - 1, SLOTS - 1, m.nt - 1)


def gnn_and_slice_attention(nc, ins, out, n):
    m = Model()
    m.x, m.src_cols, m.dst_cols, m.prev_cols, m.dst_rows = (
        ins[k] for k in ("x", "src_cols", "dst_cols", "prev_cols", "dst_rows"))
    m.w1, m.b1_dram, m.w2, m.b2_dram = (ins[k] for k in ("w1", "b1_dram", "w2", "b2_dram"))
    m.w_fx_dram, m.b_fx_dram, m.wx_t_dram, m.bx_t_dram = (
        ins[k] for k in ("w_fx_dram", "b_fx_dram", "wx_t_dram", "bx_t_dram"))
    m.w_slice_dram, m.b_slice_dram, m.temp_dram = (ins[k] for k in ("w_slice_dram", "b_slice_dram", "temp_dram"))
    m.w_q_dram, m.w_k_dram, m.w_v_dram = (ins[k] for k in ("w_q_dram", "w_k_dram", "w_v_dram"))
    m.w_out_dram, m.b_out_dram = ins["w_out_dram"], ins["b_out_dram"]
    m.out, m.n, m.np = out, n, padded(n)
    m.nt, m.ng = m.np // P, m.np // GROUP
    m.iters = (m.ng + RING - 1) // RING
    m.last = m.ng - (m.iters - 1) * RING
    assert (n - (m.ng - 1) * GROUP) % SLOTS == 0 and 0 < n - (m.ng - 1) * GROUP
    dram = lambda name, rows, width: nc.dram_tensor(name, [rows, width], F32).ap()
    m.messages = [dram(f"messages{c}", m.np, D) for c in range(2)]
    m.table = [dram(f"table{c}", m.np + GROUP, D) for c in range(2)]
    m.x1 = dram("x1", m.np, D)
    m.slice_weights = dram("slice_weights", m.np, HS)
    with ExitStack() as ctx:
        sb = lambda name, s, d=F32: ctx.enter_context(nc.sbuf_tensor(name, s, d))
        m.ident = sb("ident", [P, P])
        m.earlier = sb("earlier", [P, GROUP])
        m.spare = sb("spare", [P, SLOTS])
        m.dst_i, m.src_i, m.dst_f = sb("dst_i", [P, m.nt], I32), sb("src_i", [P, m.nt], I32), sb("dst_f", [P, m.nt])
        m.dinv, m.prev_last, m.node_row = sb("dinv", [P, m.nt]), sb("prev_last", [P, m.nt]), sb("node_row", [P, m.nt], I32)
        m.scale, m.shift = sb("scale", [P, m.nt]), sb("shift", [P, m.nt])
        m.in_order = sb("in_order", [1, 1], I32)
        m.b1, m.b2, m.b_out = sb("b1", [P, D]), sb("b2", [P, D]), sb("b_out", [P, D])
        m.w_logit = sb("w_logit", [P, KD, HS])
        m.w_hi, m.w_lo = sb("logit_hi", [P, KD, HS], F32R), sb("logit_lo", [P, KD, HS], F32R)
        m.bias_rows, m.ones3 = sb("bias_rows", [3, HS], BF16), sb("ones3", [3, P], BF16)
        m.y = sb("y", [P, 2, SLOTS, D + 2])
        m.half = sb("half", [P, 1])
        m.mixed = sb("mixed", [P, CH, D])
        m.const_ok, m.pool_passed, m.dve_passed = (
            ctx.enter_context(nc.semaphore(name)) for name in ("const_ok", "pool_passed", "dve_passed"))
        count_degrees(nc, m)
        transform(nc, m, 0)
        sum_edges(nc, m, 0)
        transform(nc, m, 1)
        sum_edges(nc, m, 1)
        prepare_attention(nc, m)
        m.tokens = [ctx.enter_context(nc.psum_tensor(f"tokens{c}", [P, D + 1], F32)) for c in range(CH)]
        attend_tokens(nc, m)
        mix_tokens(nc, m)
        write_output(nc, m)


def kernel(**inputs):
    import numpy as _np
    import concourse.bacc as _bacc
    from concourse import mybir as _mybir
    from concourse.bass_utils import run_bass_kernel_spmd as _run

    a = {k: _np.asarray(v) for k, v in inputs.items()}
    n = a["x"].shape[0]
    rows = padded(n)
    x = _np.zeros((rows, D), _np.float32)
    x[:n] = a["x"]
    pad = _np.arange(n, rows, dtype=_np.int32)
    src, dst = (_np.concatenate([a[k], pad]) for k in ("src", "dst"))
    columns = lambda e: _np.ascontiguousarray(e.reshape(-1, P).T)
    row = lambda v: _np.ascontiguousarray(v.reshape(1, -1))
    arrays = {
        "x": x,
        "src_cols": columns(src),
        "dst_cols": columns(dst),
        "prev_cols": columns(_np.concatenate([dst[:1], dst[:-1]])),
        "dst_rows": dst.reshape(-1, GROUP),
        "w1": a["L0_gnn_W1"], "b1_dram": a["L0_gnn_b1"],
        "w2": a["L0_gnn_W2"], "b2_dram": a["L0_gnn_b2"],
        "w_fx_dram": a["L0_ffn_W_fx"], "b_fx_dram": row(a["L0_ffn_b_fx"]),
        "wx_t_dram": _np.ascontiguousarray(a["L0_ffn_W_x"].T),
        "bx_t_dram": _np.ascontiguousarray(a["L0_ffn_b_x"].reshape(HEADS, HD).T),
        "w_slice_dram": a["L0_ffn_W_slice"], "b_slice_dram": row(a["L0_ffn_b_slice"]),
        "w_q_dram": a["L0_ffn_W_q"], "w_k_dram": a["L0_ffn_W_k"], "w_v_dram": a["L0_ffn_W_v"],
        "w_out_dram": a["L0_ffn_W_out"], "b_out_dram": a["L0_ffn_b_out"],
        "temp_dram": a["L0_ffn_temperature"].reshape(-1),
    }
    nc = _bacc.Bacc("TRN2", target_bir_lowering=False, num_devices=1)
    ins = {k: nc.dram_tensor(f"in_{k}", v.shape, _mybir.dt.from_np(v.dtype), kind="ExternalInput").ap()
           for k, v in arrays.items()}
    out = nc.dram_tensor("out_0", (rows, D), F32, kind="ExternalOutput").ap()
    gnn_and_slice_attention(nc, ins, out, n)
    r = _run(nc, [{f"in_{k}": v for k, v in arrays.items()}], core_ids=[0])
    return r.results[0]["out_0"][:n]
```
